# Optimizing a Trainium2 kernel written in Bass

```python
import numpy as np
import jax
import jax.numpy as jnp

def _softmax(x, axis=-1):
    return jax.nn.softmax(x, axis=axis)

def _gelu(x):
    return jax.nn.gelu(x, approximate=True)

def _silu(x):
    return jax.nn.silu(x)

def _sigmoid(x):
    return jax.nn.sigmoid(x)

def _layernorm(x, axis=-1, eps=1e-05):
    m = jnp.mean(x, axis=axis, keepdims=True)
    v = jnp.var(x, axis=axis, keepdims=True)
    return (x - m) / jnp.sqrt(v + eps)

def _scatter_add(tgt, idx, src, axis=0):
    return tgt.at[idx].add(src)

def _segment_sum(src, seg, n):
    return jax.ops.segment_sum(src, seg, n)
kernel_name = 'mk_seq_preln_d2_jaxref_r8_7f50ee'

def setup_inputs(seed: int=0):
    np.random.seed(seed)
    _w = jnp.asarray

    def _L0_attn_setup():
        import jax, jax.numpy as jnp
        import numpy as np
        H = 256
        NH = 16
        HD = H // NH
        key = jax.random.key(seed)
        ks = jax.random.split(key, 9)
        s = 1.0 / np.sqrt(H)
        return {'x': jax.random.normal(ks[0], (2, 256, H), dtype=jnp.float32), 'Wq': jax.random.uniform(ks[1], (H, H), jnp.float32, -s, s), 'bq': jax.random.uniform(ks[2], (H,), jnp.float32, -s, s), 'Wk': jax.random.uniform(ks[3], (H, H), jnp.float32, -s, s), 'bk': jax.random.uniform(ks[4], (H,), jnp.float32, -s, s), 'Wv': jax.random.uniform(ks[5], (H, H), jnp.float32, -s, s), 'bv': jax.random.uniform(ks[6], (H,), jnp.float32, -s, s), 'Wo': jax.random.uniform(ks[7], (H, H), jnp.float32, -s, s), 'bo': jax.random.uniform(ks[8], (H,), jnp.float32, -s, s)}
    _L0_attn_in = _L0_attn_setup()

    def _L0_ffn_setup():
        import jax, jax.numpy as jnp
        import numpy as np
        B, S, H = (2, 128, 256)
        E, K = (8, 2)
        I = 176
        IS = 704
        WSCALE = 0.02
        key = jax.random.key(seed)
        ks = jax.random.split(key, 9)
        f32 = jnp.float32
        return {'hidden_states': jax.random.normal(ks[0], (B, S, H), dtype=f32), 'gate_w': jax.random.normal(ks[1], (E, H), dtype=f32) * WSCALE, 'w_gate': jax.random.normal(ks[2], (E, H, I), dtype=f32) * WSCALE, 'w_up': jax.random.normal(ks[3], (E, H, I), dtype=f32) * WSCALE, 'w_down': jax.random.normal(ks[4], (E, I, H), dtype=f32) * WSCALE, 'sw_gate': jax.random.normal(ks[5], (H, IS), dtype=f32) * WSCALE, 'sw_up': jax.random.normal(ks[6], (H, IS), dtype=f32) * WSCALE, 'sw_down': jax.random.normal(ks[7], (IS, H), dtype=f32) * WSCALE, 'shared_gate_w': jax.random.normal(ks[8], (H, 1), dtype=f32) * WSCALE}
    _L0_ffn_in = _L0_ffn_setup()

    def _L1_attn_setup():
        import math
        import jax, jax.numpy as jnp
        import numpy as np
        BLOCK = 64

        def build_slope_tensor(n_heads):

            def p2(n):
                start = 2.0 ** (-2.0 ** (-(math.log2(n) - 3)))
                return [start * start ** i for i in range(n)]
            if math.log2(n_heads).is_integer():
                s = p2(n_heads)
            else:
                closest = 2 ** math.floor(math.log2(n_heads))
                s = p2(closest) + p2(2 * closest)[0::2][:n_heads - closest]
            return jnp.asarray(np.array(s, dtype=np.float32))

        def lightning_attn(q, k, v, slopes, block=BLOCK):
            B, H, N, d = q.shape
            nc = N // block
            i = jnp.arange(block, dtype=q.dtype)
            diff = i[:, None] - i[None, :]
            intra_decay = jnp.where(diff >= 0, jnp.exp(-slopes[:, None, None] * diff), 0.0)
            q_decay = jnp.exp(-slopes[:, None] * i[None, :])
            k_decay = jnp.exp(-slopes[:, None] * (block - i[None, :]))
            blk_decay = jnp.exp(-slopes * block)

            def to_chunks(t):
                return t.reshape(B, H, nc, block, d).transpose(2, 0, 1, 3, 4)
            qc, kc, vc = (to_chunks(q), to_chunks(k), to_chunks(v))

            def body(S, xs):
                qb, kb, vb = xs
                scores = jnp.einsum('bhid,bhjd->bhij', qb, kb) * intra_decay[None]
                o_intra = jnp.einsum('bhij,bhjd->bhid', scores, vb)
                o_inter = jnp.einsum('bhid,bhde->bhie', qb * q_decay[None, :, :, None], S)
                S_new = blk_decay[None, :, None, None] * S + jnp.einsum('bhjd,bhje->bhde', kb * k_decay[None, :, :, None], vb)
                return (S_new, o_intra + o_inter)
            S0 = jnp.zeros((B, H, d, d), dtype=q.dtype)
            _, o = jax.lax.scan(body, S0, (qc, kc, vc))
            return o.transpose(1, 2, 0, 3, 4).reshape(B, H, N, d)
        key = jax.random.key(seed)
        k1, k2, k3 = jax.random.split(key, 3)
        dim, num_heads = (256, 16)
        B, N = (2, 512)
        x = jax.random.normal(k1, (B, N, dim), dtype=jnp.float32)
        Wqkv = jax.random.normal(k2, (dim, 3 * dim), dtype=jnp.float32) / math.sqrt(dim)
        bqkv = jnp.zeros((3 * dim,), dtype=jnp.float32)
        Wout = jax.random.normal(k3, (dim, dim), dtype=jnp.float32) / math.sqrt(dim)
        bout = jnp.zeros((dim,), dtype=jnp.float32)
        slopes = build_slope_tensor(num_heads)
        return {'x': x, 'Wqkv': Wqkv, 'bqkv': bqkv, 'Wout': Wout, 'bout': bout, 'slopes': slopes}
    _L1_attn_in = _L1_attn_setup()

    def _L1_ffn_setup():
        import jax, jax.numpy as jnp
        import numpy as np
        H, I, E = (256, 512, 8)
        B, S = (2, 256)
        key = jax.random.key(seed)
        ks = jax.random.split(key, 5)
        scale = 0.02
        return {'hidden_states': jax.random.normal(ks[0], (B, S, H), dtype=jnp.float32), 'router_w': jax.random.normal(ks[1], (H, E), dtype=jnp.float32) * scale, 'gate_w': jax.random.normal(ks[2], (E, H, I), dtype=jnp.float32) * scale, 'up_w': jax.random.normal(ks[3], (E, H, I), dtype=jnp.float32) * scale, 'down_w': jax.random.normal(ks[4], (E, I, H), dtype=jnp.float32) * scale}
    _L1_ffn_in = _L1_ffn_setup()
    _d = {'L0_attn_x': _L0_attn_in['x'], 'L0_attn_Wq': _L0_attn_in['Wq'], 'L0_attn_bq': _L0_attn_in['bq'], 'L0_attn_Wk': _L0_attn_in['Wk'], 'L0_attn_bk': _L0_attn_in['bk'], 'L0_attn_Wv': _L0_attn_in['Wv'], 'L0_attn_bv': _L0_attn_in['bv'], 'L0_attn_Wo': _L0_attn_in['Wo'], 'L0_attn_bo': _L0_attn_in['bo'], 'L0_ffn_gate_w': _L0_ffn_in['gate_w'], 'L0_ffn_w_gate': _L0_ffn_in['w_gate'], 'L0_ffn_w_up': _L0_ffn_in['w_up'], 'L0_ffn_w_down': _L0_ffn_in['w_down'], 'L0_ffn_sw_gate': _L0_ffn_in['sw_gate'], 'L0_ffn_sw_up': _L0_ffn_in['sw_up'], 'L0_ffn_sw_down': _L0_ffn_in['sw_down'], 'L0_ffn_shared_gate_w': _L0_ffn_in['shared_gate_w'], 'L1_attn_Wqkv': _L1_attn_in['Wqkv'], 'L1_attn_bqkv': _L1_attn_in['bqkv'], 'L1_attn_Wout': _L1_attn_in['Wout'], 'L1_attn_bout': _L1_attn_in['bout'], 'L1_attn_slopes': _L1_attn_in['slopes'], 'L1_ffn_router_w': _L1_ffn_in['router_w'], 'L1_ffn_gate_w': _L1_ffn_in['gate_w'], 'L1_ffn_up_w': _L1_ffn_in['up_w'], 'L1_ffn_down_w': _L1_ffn_in['down_w']}
    _x0 = _d['L0_attn_x']
    _d['L0_attn_x'] = jax.random.normal(jax.random.fold_in(jax.random.key(seed), 1), (2, 512, 256), dtype=_x0.dtype)
    del _x0
    return _d

def reference(L0_attn_x, L0_attn_Wq, L0_attn_bq, L0_attn_Wk, L0_attn_bk, L0_attn_Wv, L0_attn_bv, L0_attn_Wo, L0_attn_bo, L0_ffn_gate_w, L0_ffn_w_gate, L0_ffn_w_up, L0_ffn_w_down, L0_ffn_sw_gate, L0_ffn_sw_up, L0_ffn_sw_down, L0_ffn_shared_gate_w, L1_attn_Wqkv, L1_attn_bqkv, L1_attn_Wout, L1_attn_bout, L1_attn_slopes, L1_ffn_router_w, L1_ffn_gate_w, L1_ffn_up_w, L1_ffn_down_w):

    def _L0_attn_ref(x, Wq, bq, Wk, bk, Wv, bv, Wo, bo):
        import jax, jax.numpy as jnp
        import numpy as np
        H = 256
        NH = 16
        HD = H // NH
        B, S, _ = x.shape
        q = (x @ Wq.T + bq).reshape(B, S, NH, HD).transpose(0, 2, 1, 3)
        k = (x @ Wk.T + bk).reshape(B, S, NH, HD).transpose(0, 2, 1, 3)
        v = (x @ Wv.T + bv).reshape(B, S, NH, HD).transpose(0, 2, 1, 3)
        scores = jnp.einsum('bhqd,bhkd->bhqk', q, k) / np.sqrt(HD).astype(jnp.float32)
        probs = jax.nn.softmax(scores, axis=-1)
        ctx = jnp.einsum('bhqk,bhkd->bhqd', probs, v)
        ctx = ctx.transpose(0, 2, 1, 3).reshape(B, S, NH * HD)
        return ctx @ Wo.T + bo

    def _L0_ffn_ref(hidden_states, gate_w, w_gate, w_up, w_down, sw_gate, sw_up, sw_down, shared_gate_w):
        import jax, jax.numpy as jnp
        import numpy as np
        B, S, H = (2, 128, 256)
        E, K = (8, 2)
        I = 176
        IS = 704
        WSCALE = 0.02
        x = hidden_states
        logits = jnp.einsum('bsh,eh->bse', x, gate_w)
        probs = jax.nn.softmax(logits, axis=-1)
        top_w, top_i = jax.lax.top_k(probs, K)
        top_w = top_w / jnp.sum(top_w, axis=-1, keepdims=True)
        onehot = jax.nn.one_hot(top_i, E, dtype=x.dtype)
        combine = jnp.einsum('bsk,bske->bse', top_w, onehot)
        g = jnp.einsum('bsh,ehi->besi', x, w_gate)
        u = jnp.einsum('bsh,ehi->besi', x, w_up)
        h = jax.nn.silu(g) * u
        expert_out = jnp.einsum('besi,eih->besh', h, w_down)
        moe_out = jnp.einsum('besh,bse->bsh', expert_out, combine)
        sh = jax.nn.silu(x @ sw_gate) * (x @ sw_up)
        shared_out = sh @ sw_down
        shared_gate = jax.nn.sigmoid(x @ shared_gate_w)
        return moe_out + shared_out * shared_gate

    def _L1_attn_ref(x, Wqkv, bqkv, Wout, bout, slopes):
        import math
        import jax, jax.numpy as jnp
        import numpy as np
        BLOCK = 64

        def build_slope_tensor(n_heads):

            def p2(n):
                start = 2.0 ** (-2.0 ** (-(math.log2(n) - 3)))
                return [start * start ** i for i in range(n)]
            if math.log2(n_heads).is_integer():
                s = p2(n_heads)
            else:
                closest = 2 ** math.floor(math.log2(n_heads))
                s = p2(closest) + p2(2 * closest)[0::2][:n_heads - closest]
            return jnp.asarray(np.array(s, dtype=np.float32))

        def lightning_attn(q, k, v, slopes, block=BLOCK):
            B, H, N, d = q.shape
            nc = N // block
            i = jnp.arange(block, dtype=q.dtype)
            diff = i[:, None] - i[None, :]
            intra_decay = jnp.where(diff >= 0, jnp.exp(-slopes[:, None, None] * diff), 0.0)
            q_decay = jnp.exp(-slopes[:, None] * i[None, :])
            k_decay = jnp.exp(-slopes[:, None] * (block - i[None, :]))
            blk_decay = jnp.exp(-slopes * block)

            def to_chunks(t):
                return t.reshape(B, H, nc, block, d).transpose(2, 0, 1, 3, 4)
            qc, kc, vc = (to_chunks(q), to_chunks(k), to_chunks(v))

            def body(S, xs):
                qb, kb, vb = xs
                scores = jnp.einsum('bhid,bhjd->bhij', qb, kb) * intra_decay[None]
                o_intra = jnp.einsum('bhij,bhjd->bhid', scores, vb)
                o_inter = jnp.einsum('bhid,bhde->bhie', qb * q_decay[None, :, :, None], S)
                S_new = blk_decay[None, :, None, None] * S + jnp.einsum('bhjd,bhje->bhde', kb * k_decay[None, :, :, None], vb)
                return (S_new, o_intra + o_inter)
            S0 = jnp.zeros((B, H, d, d), dtype=q.dtype)
            _, o = jax.lax.scan(body, S0, (qc, kc, vc))
            return o.transpose(1, 2, 0, 3, 4).reshape(B, H, N, d)
        B, N, C = x.shape
        H = slopes.shape[0]
        hd = C // H
        qkv = (x @ Wqkv + bqkv).reshape(B, N, 3, H, hd)
        qkv = qkv.transpose(2, 0, 3, 1, 4)
        q, k, v = (qkv[0], qkv[1], qkv[2])
        attn = lightning_attn(q, k, v, slopes)
        out = attn.transpose(0, 2, 1, 3).reshape(B, N, C)
        return out @ Wout + bout

    def _L1_ffn_ref(hidden_states, router_w, gate_w, up_w, down_w):
        import jax, jax.numpy as jnp
        import numpy as np
        H, I, E = (256, 512, 8)
        B, S = (2, 256)
        hidden_shape = hidden_states.shape
        x = hidden_states.reshape(-1, hidden_shape[-1])
        route = jax.nn.sigmoid(x @ router_w)
        max_ind = jnp.argmax(route, axis=1)
        max_prob = jnp.take_along_axis(route, max_ind[:, None], axis=1)
        out = jnp.zeros_like(x)
        num_experts = gate_w.shape[0]
        for e in range(num_experts):
            mask = (max_ind == e)[:, None]
            h = jax.nn.silu(x @ gate_w[e]) * (x @ up_w[e])
            out = out + jnp.where(mask, h @ down_w[e], 0.0)
        out = out * max_prob
        return out.reshape(hidden_shape)
    x = L0_attn_x
    x = x + _L0_attn_ref(_layernorm(x, axis=-1), L0_attn_Wq, L0_attn_bq, L0_attn_Wk, L0_attn_bk, L0_attn_Wv, L0_attn_bv, L0_attn_Wo, L0_attn_bo)
    x = x + _L0_ffn_ref(_layernorm(x, axis=-1), L0_ffn_gate_w, L0_ffn_w_gate, L0_ffn_w_up, L0_ffn_w_down, L0_ffn_sw_gate, L0_ffn_sw_up, L0_ffn_sw_down, L0_ffn_shared_gate_w)
    x = x + _L1_attn_ref(_layernorm(x, axis=-1), L1_attn_Wqkv, L1_attn_bqkv, L1_attn_Wout, L1_attn_bout, L1_attn_slopes)
    x = x + _L1_ffn_ref(_layernorm(x, axis=-1), L1_ffn_router_w, L1_ffn_gate_w, L1_ffn_up_w, L1_ffn_down_w)
    return x

_drawn_inputs = setup_inputs


def setup_inputs(seed=0):
    import zlib

    import numpy as np

    out = dict(_drawn_inputs(seed))
    spreads = {'L1_attn_bqkv': (0.0, 0.1), 'L1_attn_bout': (0.0, 0.8)}
    factors = {'L0_attn_Wq': 3.496,
     'L0_attn_bq': 8.0,
     'L0_attn_Wk': 3.233,
     'L0_attn_bk': 8.0,
     'L0_ffn_gate_w': 4.488,
     'L0_ffn_w_gate': 3.899,
     'L0_ffn_w_up': 3.863,
     'L0_ffn_w_down': 3.846,
     'L0_ffn_shared_gate_w': 8.0,
     'L1_ffn_router_w': 8.0,
     'L1_ffn_gate_w': 8.0,
     'L1_ffn_up_w': 8.0,
     'L1_ffn_down_w': 8.0}
    for name, (base, spread) in spreads.items():
        noise = np.random.default_rng([zlib.crc32(name.encode()), seed]).standard_normal(out[name].shape)
        drawn = base * np.exp(spread * noise) if base else spread * noise
        out[name] = jnp.asarray(drawn.astype(out[name].dtype))
    for name, factor in factors.items():
        out[name] = (out[name] * factor).astype(out[name].dtype)
    return out
```

```python
from contextlib import ExitStack

import concourse.bass as bass
from concourse import mybir

F32 = mybir.dt.float32
BF16 = mybir.dt.bfloat16
I32 = mybir.dt.int32
ALU = mybir.AluOpType
ACT = mybir.ActivationFunctionType
AX = mybir.AxisListType

P = 128
B, S, H = 2, 512, 256
TB = S // P
T = B * TB
KT = H // P
NH, HD = 16, 16
HP = P // HD
E = 8
I0, IS0, I1 = 176, 704, 512
GU0 = 2 * I0
MS = 6
NT0 = 2 * B * S // P + E - 1
NT1 = B * S // P + E - 1
FFN0_PIECES = 20
NZ = (NT0 + 1) // 2 + (NT1 + 1) // 2
TERMS_Q = (0, 0, 0, 1, 1, 2)
TERMS_K = (0, 1, 2, 0, 1, 0)
KR = 6 * HD
UN = 8
LAG = 8
NPT = 8


class Uses:

    def __init__(self):
        self.at, self.count, self.turn = {}, [0] * 8, 0

    def add(self, key, bank=None):
        if bank is None:
            bank = self.turn
            self.turn = (self.turn + 1) % 8
        self.at[key] = (bank, self.count[bank])
        self.count[bank] += 1


def quarter_of(q):
    out = {}
    if q < 4 * UN:
        out["max"] = divmod(q, 4)
    if q % 4 == 0 and 0 < q <= 4 * UN:
        out["negmax"] = q // 4 - 1
    if 0 <= q - LAG < 4 * UN:
        out["score"] = divmod(q - LAG, 4)
    if 0 <= q - LAG - 1 < 4 * UN:
        out["pv"] = divmod(q - LAG - 1, 4)
    if 0 <= q - LAG - 2 < 4 * UN and (q - LAG - 2) % 4 == 3:
        out["norm"] = (q - LAG - 2) // 4
    if 0 <= q - LAG - 3 < 4 * UN and (q - LAG - 3) % 16 == 15:
        out["ctxT"] = (q - LAG - 3) // 16
    if 0 <= q - LAG - 4 < 4 * UN and (q - LAG - 4) % 16 == 15:
        out["wo"] = (q - LAG - 4) // 16
    if 2 <= q < 6:
        out["proj"] = q + 2
    if 3 <= q < 7:
        out["split"] = q + 1
    if 6 <= q < 8:
        out["v"] = q - 6
    return out


NQ = 4 * UN + LAG + 4


def proj_key(i):
    return i % 2, i // 4, i // 2 % 2


def plan():
    u = Uses()
    for b in range(B):
        for kt in range(KT):
            u.add(("xt", 0, b, kt))
    for i in range(4):
        u.add(("qk", i))
    for pr in range(2):
        u.add(("v", 0, pr))
    u.before_attention = list(u.count)
    for q in range(NQ):
        w = quarter_of(q)
        if "max" in w:
            for hp in range(2):
                u.add(("mx", *w["max"], hp), 2 * hp)
        if "proj" in w:
            u.add(("qk", w["proj"]), 7)
        if "v" in w:
            u.add(("v", 1, w["v"]), 7)
        if "negmax" in w:
            u.add(("nm", w["negmax"]), 7)
        if "score" in w:
            for h in range(4):
                u.add(("s", *w["score"], h), 4 + h % 2)
        if "pv" in w and w["pv"][1] == 0:
            u.add(("pv", w["pv"][0]), 6)
        if "norm" in w:
            u.add(("ct", w["norm"]), 7)
        if "ctxT" in w:
            for kt in range(KT):
                u.add(("cx", w["ctxT"], kt), 7)
        if "wo" in w:
            for pr in range(2):
                u.add(("o", w["wo"], pr), 7)
    u.attention_ends = u.count[0], u.count[2]
    u.turn = 4
    for b in range(B):
        for kt in range(KT):
            u.add(("xt", 1, b, kt), 4 + (2 * b + kt) % 4)
    u.turn = 0
    u.add(("r", 0))
    u.add(("rank", 0))
    def shared(c):
        for m in range(MS):
            u.add(("sg", c, m))
            u.add(("su", c, m))
        for pr in range(2):
            u.add(("sd", c, pr))

    shared(0)
    for i in range(NT0 + 3):
        if i < NT0:
            u.add(("ex", 0, i))
        if 0 <= i - 1 < NT0:
            u.add(("eg", 0, i - 1))
        if 0 <= i - 2 < NT0:
            u.add(("eh", 0, i - 2))
        if 0 <= i - 3 < NT0:
            u.add(("ed", 0, i - 3))
    shared(1)
    for b in range(B):
        for kt in range(KT):
            u.add(("xt", 2, b, kt))
    for b in range(B):
        for m in range(KT):
            u.add(("q1", b, m))
            u.add(("k1", b, m))
        for t in range(TB):
            u.add(("kv", TB * b + t))
    for n in range(len(CHUNKS)):
        for hf in range(2):
            u.add(("sc", n, hf))
        if n > 0:
            u.add(("oc", n - 1))
            if CHUNKS[n - 1][0] < TB - 1:
                u.add(("st", n - 1))
    u.add(("oc", len(CHUNKS) - 1))
    for b in range(B):
        for pr in range(2):
            u.add(("op", b, pr))
    for b in range(B):
        for kt in range(KT):
            u.add(("xt", 3, b, kt))
    u.add(("r", 1))
    u.add(("rank", 1))
    for i in range(NT1 + 3):
        if i < NT1:
            u.add(("ex", 1, i))
        if 0 <= i - 1 < NT1:
            u.add(("eg", 1, i - 1))
            u.add(("eu", 1, i - 1))
        if 0 <= i - 2 < NT1:
            u.add(("eh", 1, i - 2))
        if 0 <= i - 3 < NT1:
            u.add(("ed", 1, i - 3))
    return u


CHUNKS = [(c, b, m) for c in range(TB) for b in range(B) for m in range(KT)]


def two_layers(nc, d):
    uses = plan()
    ctx = ExitStack()
    with ctx:
        def sb(name, shape, dt=F32):
            return ctx.enter_context(nc.sbuf_tensor(name, shape, dt))

        def sem(name):
            return ctx.enter_context(nc.semaphore(name))

        def sems(name, n):
            return [sem(f"{name}{i}") for i in range(n)]

        R1 = sb("R1", [P, 16384])
        R2 = sb("R2", [P, 8192])
        R3 = sb("R3", [P, 4096])
        R4 = sb("R4", [P, 14080])
        W = sb("W", [P, 2048])
        X = sb("X", [P, T, H])
        XN = sb("XN", [P, T, H])
        XT = sb("XT", [P, KT, B * S])

        def part(region, at, *shape, dt=F32):
            n = 1
            for s in shape:
                n *= s
            words = n // 2 if dt == BF16 else n
            v = region[:, at:at + words]
            if dt != F32:
                v = v.bitcast(dt)
            if len(shape) == 2:
                v = v.rearrange("p (a b) -> p a b", a=shape[0])
            elif len(shape) == 3:
                v = v.rearrange("p (a b c) -> p a b c", a=shape[0], b=shape[1])
            return v

        QP = [part(R1, 8192 * b, NH, S, dt=BF16) for b in range(B)]
        KP = [part(R1, 8192 * b + 4096, NH, S, dt=BF16) for b in range(B)]
        up1 = part(R1, 0, KT, E, I1)
        down1 = part(R1, 8192, I1 // P, E, H)
        gate1 = part(R2, 0, KT, E, I1)
        VS = NH * (HD + 1) + HD
        VA = part(R2, 0, T, VS)
        PT = part(R2, 2304, NPT, S)
        CT = part(R2, 6400, 2, S)
        bv_row = part(R2, 7424, H)
        bo_row = part(R2, 7680, H)
        PC = part(R3, 0, 4, 3 * S, dt=BF16)
        RES = part(R3, 3072, 2, S)
        HS = part(R3, 0, MS, S)
        SSG = part(R3, 3072, 2, S)
        DT = part(R3, 0, NH, P)
        PD = part(R3, 2048, 2, HP * P)
        gu0 = part(R4, 0, KT, E, GU0)
        da0 = part(R4, 5632, E, H)
        db0 = part(R4, 7680, E, H)
        sg0 = part(R4, 9728, KT, IS0)
        su0 = part(R4, 11136, KT, IS0)
        sd0 = part(R4, 12544, MS, H)
        QT1 = part(R4, 0, KT, B * S)
        KT1 = part(R4, 2048, KT, B * S)
        KD1 = part(R4, 4096, T, H)
        VP = part(R4, 6144, T, 8 * 48)
        QB = part(R4, 9216, 2, HP * P)
        QDEC = part(R4, 11264, 2, P)
        QD = part(R4, 11520, KT, P)
        ST = part(R4, 11776, 4, P)
        bkv_row = part(R4, 12288, 2 * H)
        bout_row = part(R4, 12800, H)
        TMP = part(R4, 13056, 2, P)

        def tile_buffers(region, n, hw):
            at, out = 0, []
            for shape in ((4, H), (2, H), (2, hw), (2, hw), (2, max(hw, H)), (2, H), (8, H)):
                out.append(part(region, at, *shape))
                at += shape[0] * shape[1]
            return out + [at]

        *bufs0, small0 = tile_buffers(R2, 0, I0)
        *bufs1, small1 = tile_buffers(R4, 1, I1)

        logits = [part(R2, small0, T, E + 1), part(R4, small1, T, E + 1)]
        OT = XN[:].rearrange("p t h -> p (t h)").rearrange("p (k n) -> p k n", k=KT)
        chosen_of = {}

        identity = sb("identity", [P, P])
        identity_bf = sb("identity_bf", [P, P], BF16)
        ones_bf = sb("ones_bf", [P, P], BF16)
        before_bf = sb("before_bf", [P, P], BF16)
        diff = sb("diff", [P, P])
        iota_i = sb("iota_i", [P, P])
        block_diag = sb("block_diag", [P, HP, HD])
        iota_e = sb("iota_e", [P, E])
        steps = sb("steps", [P, E])
        upto = sb("upto", [P, E, E])
        iota_j = sb("iota_j", [P, NT0])
        back = sb("back", [P, 1])
        zeros = sb("zeros", [P, H])
        slopes_row = sb("slopes_row", [P, NH])
        nslopes_row = sb("nslopes_row", [P, NH])
        slopes_col = sb("slopes_col", [P, KT])
        nslopes_col = sb("nslopes_col", [P, KT])
        KDEC = sb("KDEC", [P, NH])
        chunk_decay = sb("chunk_decay", [P, KT])
        bias_col = sb("bias_col", [P, 4, KT])
        r0w = sb("r0w", [P, KT, E + 1])
        r1w = sb("r1w", [P, KT, E])
        stats = sb("stats", [P, T, 6])
        mv = sb("mv", [P, T, 2])
        sd = sb("sd", [P, T])
        rstd = sb("rstd", [P, T])
        eps = sb("eps", [P, 1])
        MX = sb("MX", [P, UN, 4, TB])
        nres = sb("nres", [P, 16])
        NM = sb("NM", [P, 2, 48], BF16)
        NMT = sb("NMT", [48, 2, P], BF16)
        RD = sb("RD", [P, 16])
        gate = sb("gate", [P, T])
        weight = [sb(f"weight{k}", [P, T]) for k in range(2)]
        slot = sb("slot", [P, 2, T], I32)
        owner = [sb(f"owner{n}", [1, nt], I32) for n, nt in enumerate((NT0, NT1))]
        ps = ctx.enter_context(nc.psum_tensor("ps", [P, 8, 512], F32))

        qkp = [nc.dram_tensor(f"qkp{i}", [P, 3, S], BF16, kind="Internal").ap() for i in range(8)]
        nmr = [nc.dram_tensor(f"nmr{i}", [48, P], BF16, kind="Internal").ap() for i in range(UN)]
        sorted_x = [nc.dram_tensor(f"sorted_x{n}", [(nt + 1) // 2 * 2 * P, H], F32, kind="Internal").ap()
                    for n, nt in enumerate((NT0, NT1))]
        sorted_y = [nc.dram_tensor(f"sorted_y{n}", [nt * P, H], F32, kind="Internal").ap()
                    for n, nt in enumerate((NT0, NT1))]

        filled, drained = sems("filled", 8), sems("drained", 8)
        in_x = sems("in_x", B)
        in_w = sems("in_proj", 4)
        in_small = sem("in_small")
        in_bias = sem("in_bias")
        in_rows0 = sem("in_rows0")
        in_ffn0 = sem("in_ffn0")
        in_w1 = sem("in_w1")
        in_rows1 = sem("in_rows1")
        in_ffn1 = sem("in_ffn1")
        in_gate1 = sem("in_gate1")
        zeroed = sem("zeroed")
        consts = sem("consts")
        iotas = sem("iotas")
        vector_step = sem("vector_step")
        scalar_step = sem("scalar_step")
        pool_step = sem("pool_step")
        moments = sem("moments")
        sqrt_done = sem("sqrt_done")
        xn_done = sem("xn_done")
        part1_done = sem("part1_done")
        part2_done = sem("part2_done")
        part3_done = sem("part3_done")
        parts_stored = sems("parts_stored", 8)
        packed = sems("packed", 4)
        bias_added = sem("bias_added")
        negmax_done = sem("negmax_done")
        negmax_stored = sems("negmax_stored", UN)
        negmax_loaded = sems("negmax_loaded", UN)
        pv_done = sem("pv_done")
        silu_done = sem("silu_done")
        route_exp_done = sem("route_exp_done")
        counted = sem("counted")
        slots_done = sem("slots_done")
        scattered = sems("scattered", 2)
        sorted_loaded = [sems(f"sorted_loaded{n}", 4) for n in range(2)]
        y_stored = [sems(f"y_stored{n}", 2) for n in range(2)]
        gathered = [sems(f"gathered{n}", 8) for n in range(2)]
        added = sems("added", 2)
        decays = sem("decays")
        masks_made = sem("masks_made")
        spread = sem("spread")
        qdec_done = sem("qdec_done")
        kdec_done = sem("kdec_done")
        state_done = sem("state_done")
        out_sent = sem("out_sent")

        def wait_free(pe, key):
            bank, n = uses.at[key]
            if n:
                pe.wait_ge(drained[bank], n)
            return bank

        def wait_filled(eng, key):
            bank, n = uses.at[key]
            eng.wait_ge(filled[bank], n + 1)
            return bank

        def wait_drained(eng, key):
            bank, n = uses.at[key]
            eng.wait_ge(drained[bank], n + 1)

        def tok(t, n=1):
            return slice(P * t, P * (t + n))

        block = ctx.enter_context(nc.Block())

        @block.sync
        def _(sp):
            for b in range(B):
                sp.dma_start(X[:, TB * b:TB * b + TB, :], d["x"][b].rearrange("(t p) h -> p t h", p=P))\
                    .then_inc(in_x[b], 16)
                if b == 0:
                    for n in range(2):
                        sp.dma_start(part(W, 512 * n, 512), d["w0"][n]).then_inc(in_w[n], 16)
                    sp.dma_start(bias_col[:], d["bias_col"]).then_inc(in_bias, 16)
            sp.dma_start(part(W, 1024, 512), d["w0"][2]).then_inc(in_w[2], 16)
            sp.dma_start(bv_row, d["bv0"].partition_broadcast(P)).then_inc(in_rows0, 16)
            sp.dma_start(bo_row, d["bo0"].partition_broadcast(P)).then_inc(in_rows0, 16)
            sp.dma_start(part(W, 1536, 512), d["w0"][3]).then_inc(in_w[3], 16)
            sp.dma_start(slopes_row[:], d["slopes"].partition_broadcast(P)).then_inc(in_small, 16)
            sp.dma_start(slopes_col[:], d["slopes_col"]).then_inc(in_small, 16)
            sp.dma_start(r0w[:], d["r0w"]).then_inc(in_small, 16)
            sp.dma_start(r1w[:], d["r1w"]).then_inc(in_small, 16)

            def pack(i):
                qk, b, m = proj_key(i)
                sp.wait_ge(part3_done, i + 1)
                sp.dma_start(qkp[i], PC[:, i % 4, :].rearrange("p (a t) -> p a t", a=3))\
                    .then_inc(parts_stored[i], 16)
                sp.wait_ge(parts_stored[i], 16)
                for row, p in enumerate((TERMS_Q, TERMS_K)[qk]):
                    sp.dma_start((QP, KP)[qk][b][HD * row:HD * row + HD, HP * m:HP * m + HP, :],
                                 qkp[i][:, p, :].rearrange("(j e) t -> e j t", e=HD))\
                        .then_inc(packed[2 * b + m], 16)

            for i in range(4):
                pack(i)
            sp.wait_ge(consts, 3)

            def ffn0_weights(c):
                cols = slice(704 * c, 704 * c + 704)
                sp.dma_start(R4[:, cols], d["ffn0"][:, cols]).then_inc(in_ffn0, 16)

            def zero_rows(n, j):
                sp.dma_start(sorted_x[n][P * j:P * j + 2 * P, :].rearrange("(j p) h -> p j h", p=P),
                             zeros[:].unsqueeze(1).to_broadcast([P, 2, H])).then_inc(zeroed, 16)

            pieces = [(ffn0_weights, (c,)) for c in range(FFN0_PIECES)]
            pieces += [(zero_rows, (n, j)) for n, nt in enumerate((NT0, NT1)) for j in range(0, nt, 2)]
            per_quarter = -(-len(pieces) // (4 * UN - 1))
            for q in range(NQ):
                w = quarter_of(q)
                if "max" in w and q:
                    wait_filled(sp, ("mx", *w["max"], 1))
                    for piece, args in pieces[per_quarter * (q - 1):per_quarter * q]:
                        piece(*args)
                if "split" in w:
                    pack(w["split"])
                if "negmax" in w:
                    u = w["negmax"]
                    wait_drained(sp, ("nm", u))
                    sp.dma_start(nmr[u], NMT[:, u % 2, :]).then_inc(negmax_stored[u], 16)
                    sp.wait_ge(negmax_stored[u], 16)
                    b, g = divmod(u, 4)
                    sp.dma_start(QP[b][KR:KR + 3, 4 * g:4 * g + 4, :],
                                 nmr[u].rearrange("(a h q) t -> a h (q t)", a=3, h=4))\
                        .then_inc(negmax_loaded[u], 16)
            for b in range(B):
                for pr in range(2):
                    wait_filled(sp, ("o", b, pr))
            sp.dma_start(part(W, 0, 1536), d["wqkv1"]).then_inc(in_w1, 16)
            sp.dma_start(part(W, 1536, 512), d["wout1"]).then_inc(in_w1, 16)
            def ffn1_weights(c):
                cols = slice(1024 * c, 1024 * c + 1024)
                sp.dma_start(R1[:, cols], d["ffn1"][:, cols]).then_inc(in_ffn1, 16)

            def expert_tiles(n, nt, k, bufs):
                rows, out = bufs[0], bufs[5]

                def load(j):
                    if j >= 4:
                        wait_filled(sp, ("ex", n, j - 4))
                    sp.dma_start(rows[:, j % 4, :], sorted_x[n][P * j:P * j + P, :])\
                        .then_inc(sorted_loaded[n][j % 4], 16)

                sp.wait_ge(scattered[n], 16 * T * k)
                for j in range(4):
                    load(j)
                for i in range(nt + 3):
                    if i + 4 < nt:
                        load(i + 4)
                    if n == 0 and i < 16:
                        ffn1_weights(i)
                    j = i - 3
                    if j >= 0:
                        wait_drained(sp, ("ed", n, j))
                        sp.dma_start(sorted_y[n][P * j:P * j + P, :], out[:, j % 2, :])\
                            .then_inc(y_stored[n][j % 2], 16)

            expert_tiles(0, NT0, 2, bufs0)
            sp.wait_ge(added[0], 2 * T)
            sp.dma_start(bkv_row, d["bkv1"].partition_broadcast(P)).then_inc(in_rows1, 16)
            sp.dma_start(bout_row, d["bout1"].partition_broadcast(P)).then_inc(in_rows1, 16)
            sp.dma_start(gate1, d["gate1"]).then_inc(in_gate1, 16)
            expert_tiles(1, NT1, 1, bufs1)
            for t in range(T):
                sp.wait_ge(added[1], t + 1)
                sp.dma_start(d["out"][t // TB, P * (t % TB):P * (t % TB) + P, :], X[:, t, :]).then_inc(out_sent, 16)
            sp.wait_ge(out_sent, 16 * T)

        @block.gpsimd
        def _(pool):
            g = nc.gpsimd
            own = [0]

            def link(ins):
                own[0] += 1
                ins.then_inc(pool_step, 1)
                pool.wait_ge(pool_step, own[0])

            link(g.memset(identity[:], 0.0))
            g.affine_select(out=identity[:], in_=identity[:], compare_op=ALU.not_equal, fill=1.0, base=0,
                            pattern=[[-1, P]], channel_multiplier=1).then_inc(consts, 1)
            pool.wait_ge(consts, 1)
            g.tensor_copy(identity_bf[:], identity[:]).then_inc(consts, 1)
            g.memset(zeros[:], 0.0).then_inc(consts, 1)
            g.memset(eps[:], 1e-5).then_inc(consts, 1)
            g.memset(part(R2, 0, T * VS), 1.0).then_inc(consts, 1)

            def third_part(i):
                pool.wait_ge(part2_done, i + 1)
                if i >= 4:
                    pool.wait_ge(parts_stored[i - 4], 16)
                g.tensor_tensor(PC[:, i % 4, 2 * S:3 * S], RES[:, i % 2, :], PC[:, i % 4, S:2 * S],
                                ALU.subtract).then_inc(part3_done, 1)

            for i in range(4):
                third_part(i)
            pool.wait_ge(part3_done, 4)
            for b in range(B):
                g.memset(KP[b][KR:KR + 3, :, :].rearrange("p h t -> p (h t)"), 1.0).then_inc(consts, 1)
                pool.wait_ge(consts, 6 + b)
            link(g.memset(ones_bf[:], 1.0))
            g.affine_select(out=before_bf[:], in_=ones_bf[:], compare_op=ALU.is_gt, fill=0.0, base=0,
                            pattern=[[1, P]], channel_multiplier=-1).then_inc(iotas, 1)
            g.iota(iota_e[:], pattern=[[1, E]], base=0, channel_multiplier=0,
                   allow_small_or_imprecise_dtypes=True).then_inc(iotas, 1)
            g.iota(steps[:], pattern=[[P, E]], base=0, channel_multiplier=0,
                   allow_small_or_imprecise_dtypes=True).then_inc(iotas, 1)
            g.iota(iota_j[:], pattern=[[1, NT0]], base=0, channel_multiplier=0,
                   allow_small_or_imprecise_dtypes=True).then_inc(iotas, 1)
            link(g.memset(upto[:], 1.0))
            g.affine_select(out=upto[:], in_=upto[:], compare_op=ALU.is_ge, fill=0.0, base=0,
                            pattern=[[1, E], [-1, E]], channel_multiplier=0).then_inc(iotas, 1)
            g.iota(iota_i[:], pattern=[[1, P]], base=0, channel_multiplier=0,
                   allow_small_or_imprecise_dtypes=True).then_inc(iotas, 1)
            g.iota(back[:], pattern=[[0, 1]], base=-P, channel_multiplier=1,
                   allow_small_or_imprecise_dtypes=True).then_inc(iotas, 1)
            link(g.iota(diff[:], pattern=[[1, P]], base=0, channel_multiplier=-1,
                        allow_small_or_imprecise_dtypes=True))
            g.tensor_scalar(diff[:], diff[:], 0.0, None, ALU.max).then_inc(iotas, 1)
            link(g.memset(block_diag[:], 1.0))
            link(g.affine_select(out=block_diag[:], in_=block_diag[:], compare_op=ALU.is_ge, fill=0.0, base=0,
                                 pattern=[[-HD, HP], [0, HD]], channel_multiplier=1))
            g.affine_select(out=block_diag[:], in_=block_diag[:], compare_op=ALU.is_ge, fill=0.0, base=HD - 1,
                            pattern=[[HD, HP], [0, HD]], channel_multiplier=-1).then_inc(iotas, 1)
            pool.wait_ge(in_small, 16 * 4)
            g.tensor_scalar(nslopes_row[:], slopes_row[:], -1.0, None, ALU.mult).then_inc(iotas, 1)
            g.tensor_scalar(nslopes_col[:], slopes_col[:], -1.0, None, ALU.mult).then_inc(iotas, 1)
            pool.wait_ge(in_rows0, 32)
            for b in range(B):
                pool.wait_ge(xn_done, TB * (b + 1))
                xs = X[:, TB * b:TB * b + TB, :]
                g.tensor_tensor(xs, xs, bo_row.unsqueeze(1).to_broadcast([P, TB, H]), ALU.add)\
                    .then_inc(bias_added, 1)
            for q in range(NQ):
                w = quarter_of(q)
                if "split" in w:
                    third_part(w["split"])

            def sort_rows(n, topk):
                pool.wait_ge(slots_done, n + 1)
                pool.wait_ge(zeroed, 16 * NZ)
                for t in range(T):
                    for k in range(topk):
                        g.indirect_dma_start(sorted_x[n], bass.IndirectOffsetOnAxis(ap=slot[:, k, t:t + 1], axis=0),
                                             XN[:, t, :], None).then_inc(scattered[n], 16)

            def gather_rows(n, topk, nt, bufs):
                for s in range(2):
                    pool.wait_ge(y_stored[n][s], 16 * ((nt + 1 - s) // 2))
                for i in range(T * topk):
                    t, k = divmod(i, topk)
                    if i >= 8:
                        pool.wait_ge(added[n], i - 7)
                    g.indirect_dma_start(bufs[6][:, i % 8, :], None, sorted_y[n],
                                         bass.IndirectOffsetOnAxis(ap=slot[:, k, t:t + 1], axis=0))\
                        .then_inc(gathered[n][i % 8], 16)

            sort_rows(0, 2)
            gather_rows(0, 2, NT0, bufs0)
            pool.wait_ge(decays, 1)
            g.affine_select(out=DT, in_=DT, compare_op=ALU.is_ge, fill=0.0, base=0,
                            pattern=[[0, NH], [1, P]], channel_multiplier=-1).then_inc(masks_made, 1)
            pool.wait_ge(added[0], 2 * T)
            g.memset(part(R4, 6144, T * 8 * 48), 0.0).then_inc(masks_made, 1)
            g.memset(part(R4, 11776, 4 * P), 0.0).then_inc(masks_made, 1)
            pool.wait_ge(in_rows1, 32)
            for b in range(B):
                pool.wait_ge(xn_done, 2 * T + TB * (b + 1))
                xs = X[:, TB * b:TB * b + TB, :]
                g.tensor_tensor(xs, xs, bout_row.unsqueeze(1).to_broadcast([P, TB, H]), ALU.add)\
                    .then_inc(bias_added, 1)
            for n, (c, b, m) in enumerate(CHUNKS):
                if c == 0:
                    wait_drained(pool, ("q1", b, m))
                if n >= 2:
                    wait_filled(pool, ("sc", n - 2, 1))
                q = QT1[:, m, tok(TB * b + c)]
                g.tensor_tensor(QB[:, n % 2, :].rearrange("p (j i) -> p j i", j=HP),
                                q.unsqueeze(1).to_broadcast([P, HP, P]),
                                block_diag[:, :, 0:1].to_broadcast([P, HP, P]), ALU.mult).then_inc(spread, 1)
            sort_rows(1, 1)
            gather_rows(1, 1, NT1, bufs1)

        @block.scalar
        def _(act):
            s = nc.scalar
            own = [0]

            def link(ins):
                own[0] += 1
                ins.then_inc(scalar_step, 1)
                act.wait_ge(scalar_step, own[0])

            def norm_sqrt(n):
                for b in range(B):
                    act.wait_ge(moments, B * n + b + 1)
                    if n == 0 and b == 0:
                        act.wait_ge(consts, 4)
                    s.activation(sd[:, TB * b:TB * b + TB], mv[:, TB * b:TB * b + TB, 1], ACT.Sqrt, bias=eps[:])\
                        .then_inc(sqrt_done, 1)

            def take_xt(n):
                for b in range(B):
                    for kt in range(KT):
                        bank = wait_filled(act, ("xt", n, b, kt))
                        s.activation(XT[:, kt, S * b:S * b + S], ps[:, bank, :], ACT.Copy).then_inc(drained[bank], 1)

            def first_part(i):
                qk, b, m = proj_key(i)
                if i == 0:
                    act.wait_ge(in_bias, 16)
                bank = wait_filled(act, ("qk", i))
                if i >= 4:
                    act.wait_ge(parts_stored[i - 4], 16)
                s.activation(PC[:, i % 4, 0:S], ps[:, bank, :], ACT.Identity, bias=bias_col[:, qk, m:m + 1])\
                    .then_inc(part1_done, 1)

            def second_part(i):
                wait_drained(act, ("qk", i))
                s.activation(PC[:, i % 4, S:2 * S], RES[:, i % 2, :], ACT.Copy).then_inc(part2_done, 1)

            norm_sqrt(0)
            take_xt(0)
            for i in range(4):
                first_part(i)
                if i:
                    second_part(i - 1)
            second_part(3)
            for q in range(NQ):
                w = quarter_of(q)
                if "proj" in w:
                    first_part(w["proj"])
                if "split" in w:
                    second_part(w["split"])
                if "negmax" in w:
                    u = w["negmax"]
                    bank = wait_filled(act, ("nm", u))
                    if u >= 2:
                        act.wait_ge(negmax_stored[u - 2], 16)
                    s.activation(NMT[:, u % 2, :], ps[0:48, bank, 0:P // 2].bitcast(BF16), ACT.Copy)\
                        .then_inc(drained[bank], 1)
                if "score" in w:
                    u, kt = w["score"]
                    for h in range(4):
                        i = 16 * u + 4 * kt + h
                        bank = wait_filled(act, ("s", u, kt, h))
                        if i >= NPT:
                            pu, pk = divmod((i - NPT) // 4, 4)
                            if pk == 3:
                                wait_filled(act, ("pv", pu))
                            else:
                                act.wait_ge(pv_done, 3 * pu + pk + 1)
                        s.activation(PT[:, i % NPT, :], ps[:, bank, :], ACT.Exp, scale=1.0 / HD ** 0.5)\
                            .then_inc(drained[bank], 1)
                if "pv" in w and w["pv"][1] == 3:
                    u = w["pv"][0]
                    wait_filled(act, ("pv", u))
                    if u >= 2:
                        wait_filled(act, ("ct", u - 2))
                    s.activation(CT[:, u % 2, :], ps[:, 6, :], ACT.Copy).then_inc(drained[6], 1)
                if "ctxT" in w:
                    b = w["ctxT"]
                    for kt in range(KT):
                        bank = wait_filled(act, ("cx", b, kt))
                        s.activation(XT[:, kt, S * b:S * b + S], ps[:, bank, :], ACT.Copy).then_inc(drained[bank], 1)

            norm_sqrt(1)
            take_xt(1)

            def route_exp(n):
                wait_drained(act, ("r", n))
                lg = logits[n]
                if n == 0:
                    link(s.activation(lg[:, :, 0:E], lg[:, :, 0:E], ACT.Exp))
                    s.activation(lg[:, :, E:E + 1], lg[:, :, E:E + 1], ACT.Exp, scale=-1.0).then_inc(route_exp_done, 1)
                else:
                    s.activation(lg[:, :, 0:E], lg[:, :, 0:E], ACT.Exp, scale=-1.0).then_inc(route_exp_done, 1)

            route_exp(0)
            def shared_silus(c):
                for m in range(MS):
                    rows = min(P, IS0 - P * m)
                    i = MS * c + m
                    bank = wait_filled(act, ("sg", c, m))
                    if i >= 2:
                        wait_drained(act, ("su", (i - 2) // MS, (i - 2) % MS))
                    s.activation(SSG[0:rows, i % 2, :], ps[0:rows, bank, :], ACT.Silu).then_inc(drained[bank], 1)

            def expert_tiles(n, nt, hw, bufs):
                xst, sg, ht, out = bufs[1], bufs[2], bufs[4], bufs[5]
                for i in range(nt + 3):
                    if i < nt:
                        bank = wait_filled(act, ("ex", n, i))
                        s.activation(xst[:, i % 2, :], ps[:, bank, 0:H], ACT.Copy).then_inc(drained[bank], 1)
                    j = i - 1
                    if 0 <= j < nt:
                        bank = wait_filled(act, ("eg", n, j))
                        if j >= 2:
                            wait_drained(act, ("eg" if n == 0 else "eu", n, j - 2))
                        ins = s.activation(sg[:, j % 2, :], ps[:, bank, 0:hw], ACT.Silu)
                        ins.then_inc(silu_done if n == 0 else drained[bank], 1)
                    j = i - 3
                    if 0 <= j < nt:
                        bank = wait_filled(act, ("ed", n, j))
                        if j >= 2:
                            act.wait_ge(y_stored[n][j % 2], 16 * (j // 2))
                        s.activation(out[:, j % 2, :], ps[:, bank, 0:H], ACT.Copy).then_inc(drained[bank], 1)

            shared_silus(0)
            expert_tiles(0, NT0, I0, bufs0)
            shared_silus(1)
            act.wait_ge(iotas, 11)
            for pr in range(2):
                wait_filled(act, ("sd", 1, pr))
            for h in range(NH):
                ins = s.activation(DT[:, h, :], diff[:], ACT.Exp, scale=nslopes_row[:, h:h + 1])
            link(ins)
            link(s.activation(KDEC[:], slopes_row[:], ACT.Exp, scale=back[:]))
            s.activation(chunk_decay[:], nslopes_col[:], ACT.Exp, scale=float(P)).then_inc(decays, 1)

            norm_sqrt(2)
            take_xt(2)
            for m in range(KT):
                s.activation(QD[:, m, :], iota_i[:], ACT.Exp, scale=nslopes_col[:, m:m + 1]).then_inc(decays, 1)
            for b in range(B):
                for m in range(KT):
                    for key, dst, n in (("q1", QT1, 2), ("k1", KT1, 3)):
                        bank = wait_filled(act, (key, b, m))
                        s.activation(dst[:, m, S * b:S * b + S], ps[:, bank, :], ACT.Identity,
                                     bias=bias_col[:, n, m:m + 1]).then_inc(drained[bank], 1)
            for n, (c, b, m) in enumerate(CHUNKS):
                bank = wait_filled(act, ("oc", n))
                s.activation(OT[:, m, tok(TB * b + c)], ps[:, bank, 0:P], ACT.Copy).then_inc(drained[bank], 1)
            norm_sqrt(3)
            take_xt(3)
            route_exp(1)
            expert_tiles(1, NT1, I1, bufs1)

        @block.vector
        def _(dve):
            v = nc.vector
            own = [0]

            def step(ins):
                own[0] += 1
                ins.then_inc(vector_step, 1)
                return own[0]

            def link(ins):
                dve.wait_ge(vector_step, step(ins))

            def normalise(n, written):
                for b in range(B):
                    written(b)
                    for t in range(TB * b, TB * b + TB):
                        k = step(v.bn_stats(stats[:, t, :], X[:, t, :]))
                    dve.wait_ge(vector_step, k)
                    for t in range(TB * b, TB * b + TB):
                        k = v.bn_aggr(mv[:, t, :], stats[:, t, :])
                        if t < TB * b + TB - 1:
                            step(k)
                    k.then_inc(moments, 1)
                    dve.wait_ge(sqrt_done, B * n + b + 1)
                    link(v.reciprocal(rstd[:, TB * b:TB * b + TB], sd[:, TB * b:TB * b + TB]))
                    for t in range(TB * b, TB * b + TB):
                        v.tensor_scalar(XN[:, t, :], X[:, t, :], mv[:, t, 0:1], rstd[:, t:t + 1],
                                        ALU.subtract, ALU.mult).then_inc(xn_done, 1)

            def remainder(i):
                qk, b, m = proj_key(i)
                dve.wait_ge(part1_done, i + 1)
                if i >= 2:
                    dve.wait_ge(part3_done, i - 1)
                bank, _ = uses.at["qk", i]
                v.scalar_tensor_tensor(RES[:, i % 2, :], ps[:, bank, :], bias_col[:, qk, m:m + 1],
                                       PC[:, i % 4, 0:S], ALU.add, ALU.subtract).then_inc(drained[bank], 1)

            def take_v(b, pr):
                bank = wait_filled(dve, ("v", b, pr))
                if (b, pr) == (0, 0):
                    dve.wait_ge(in_rows0, 32)
                    dve.wait_ge(consts, 5)
                t = TB * b + 2 * pr
                v.tensor_tensor(VA[:, t:t + 2, 0:NH * (HD + 1)].rearrange("p t (h e) -> p t h e", h=NH)[:, :, :, 0:HD],
                                ps[:, bank, :].rearrange("p (t h e) -> p t h e", t=2, h=NH),
                                bv_row.rearrange("p (h e) -> p h e", h=NH).unsqueeze(1).to_broadcast([P, 2, NH, HD]),
                                ALU.add).then_inc(drained[bank], 1)

            normalise(0, lambda b: dve.wait_ge(in_x[b], 16))
            dve.wait_ge(in_bias, 16)
            for i in range(4):
                remainder(i)
            for pr in range(2):
                take_v(0, pr)
            for q in range(NQ):
                w = quarter_of(q)
                if "max" in w:
                    u, qt = w["max"]
                    for hp in range(2):
                        bank = wait_filled(dve, ("mx", u, qt, hp))
                        v.tensor_reduce(MX[:, u, 2 * hp:2 * hp + 2, qt], ps[:, bank:bank + 2, :], AX.X, ALU.max)\
                            .then_inc(drained[bank], 1)
                if "proj" in w:
                    remainder(w["proj"])
                if "v" in w:
                    take_v(1, w["v"])
                if "max" in w and qt == 3:
                    mx = MX[:, u, :, :].rearrange("p h q -> p (h q)")
                    nm = NM[:, u % 2, :]
                    wait_drained(dve, ("mx", u, 3, 0))
                    wait_drained(dve, ("mx", u, 3, 1))
                    if u >= 2:
                        wait_filled(dve, ("nm", u - 2))
                    link(v.tensor_scalar(nm[:, 0:16], mx, -1.0, None, ALU.mult))
                    link(v.scalar_tensor_tensor(nres[:], mx, -1.0, nm[:, 0:16], ALU.mult, ALU.subtract))
                    link(v.tensor_copy(nm[:, 16:32], nres[:]))
                    v.tensor_tensor(nm[:, 32:48], nres[:], nm[:, 16:32], ALU.subtract).then_inc(negmax_done, 1)
                if "norm" in w:
                    u = w["norm"]
                    b, g = divmod(u, 4)
                    bank = wait_filled(dve, ("ct", u))
                    if u:
                        wait_drained(dve, ("ct", u - 1))
                    sums = ps[:, bank, :].rearrange("p (t h e) -> p t h e", t=TB, h=4)
                    rd = RD[:].rearrange("p (t h) -> p t h", t=TB).unsqueeze(3)
                    link(v.reciprocal(rd, sums[:, :, :, HD:HD + 1]))
                    v.tensor_tensor(XN[:, TB * b:TB * b + TB, 64 * g:64 * g + 64].rearrange("p t (h e) -> p t h e", h=4),
                                    sums[:, :, :, 0:HD], rd.to_broadcast([P, TB, 4, HD]), ALU.mult)\
                        .then_inc(drained[bank], 1)
                if "wo" in w:
                    b = w["wo"]
                    if b == 0:
                        dve.wait_ge(bias_added, 2)
                    for pr in range(2):
                        bank = wait_filled(dve, ("o", b, pr))
                        xs = X[:, TB * b + 2 * pr:TB * b + 2 * pr + 2, :].rearrange("p t h -> p (t h)")
                        v.tensor_tensor(xs, ps[:, bank, :], xs, ALU.add).then_inc(drained[bank], 1)

            def route(n, topk):
                nt = (NT0, NT1)[n]
                region, at = ((R2, small0), (R4, small1))[n]
                at += T * (E + 1)

                def small(*shape, dt=F32):
                    nonlocal at
                    w = 1
                    for x in shape:
                        w *= x
                    out = part(region, at, *shape, dt=dt)
                    at += w
                    return out

                lg = logits[n]
                bc = lambda a: a.unsqueeze(2).to_broadcast([P, T, E])
                row = lambda a: a[:].unsqueeze(1).to_broadcast([P, T, E])
                prob, eq, rest = small(T, E), small(T, E), small(T, E)
                one = [small(T, E) for _ in range(topk)]
                top = [small(T) for _ in range(2)]
                low, tmp = small(T), small(T)
                chosen = small(T + 1, E, dt=BF16)
                pos, cnt, tiles, ends, base = small(T, E), small(E, E), small(E), small(E), small(E)
                own_of = small(nt, E)
                own_f = small(nt)
                slot_f = small(T)

                bank = wait_filled(dve, ("r", n))
                nl = E + 1 if n == 0 else E
                raw = ps[:, bank, 0:16 * T].rearrange("p (t e) -> p t e", t=T)
                if n == 0:
                    v.tensor_copy(lg[:, :, E:E + 1], raw[:, :, E:E + 1])
                    link(v.reduce_max(tmp, raw[:, :, 0:E], AX.X))
                    v.tensor_tensor(lg[:, :, 0:E], raw[:, :, 0:E], bc(tmp), ALU.subtract).then_inc(drained[bank], 1)
                else:
                    v.tensor_copy(lg[:, :, 0:E], raw[:, :, 0:E]).then_inc(drained[bank], 1)
                dve.wait_ge(route_exp_done, n + 1)
                if n == 0:
                    link(v.reduce_sum(tmp, lg[:, :, 0:E], AX.X))
                    link(v.reciprocal(low, tmp))
                    link(v.tensor_tensor(prob, lg[:, :, 0:E], bc(low), ALU.mult))
                    link(v.tensor_scalar(gate[:].unsqueeze(2), lg[:, :, E:E + 1], 1.0, None, ALU.add))
                    link(v.reciprocal(gate[:], gate[:]))
                else:
                    link(v.tensor_scalar(prob, lg[:, :, 0:E], 1.0, None, ALU.add))
                    link(v.reciprocal(prob, prob))
                dve.wait_ge(iotas, 11)
                at_hand = prob
                for k in range(topk):
                    link(v.reduce_max(top[k], at_hand, AX.X))
                    link(v.tensor_tensor(eq, at_hand, bc(top[k]), ALU.is_equal))
                    link(v.scalar_tensor_tensor(eq, eq, -64.0, row(iota_e), ALU.mult, ALU.add))
                    link(v.tensor_reduce(low, eq, AX.X, ALU.min))
                    link(v.tensor_tensor(one[k], eq, bc(low), ALU.is_equal))
                    if k + 1 < topk:
                        link(v.scalar_tensor_tensor(rest, one[k], -2.0, prob, ALU.mult, ALU.add))
                        at_hand = rest
                link(v.memset(chosen[:, T:T + 1, :], 0.0))
                if topk == 2:
                    v.tensor_tensor(chosen[:, 0:T, :], one[0], one[1], ALU.add).then_inc(counted, 1)
                    link(v.tensor_tensor(tmp, top[0], top[1], ALU.add))
                    link(v.reciprocal(low, tmp))
                    for k in range(2):
                        link(v.tensor_tensor(weight[k][:], top[k], low, ALU.mult))
                else:
                    v.tensor_copy(chosen[:, 0:T, :], one[0]).then_inc(counted, 1)
                    link(v.tensor_copy(weight[0][:], top[0]))
                chosen_of[n] = chosen
                bank = wait_filled(dve, ("rank", n))
                rank = ps[:, bank, 0:T * E].rearrange("p (t e) -> p t e", t=T)
                total = ps[:, bank, T * E:T * E + E]
                link(v.tensor_tensor(cnt, total.unsqueeze(2).to_broadcast([P, E, E]),
                                     steps[:].unsqueeze(1).to_broadcast([P, E, E]), ALU.is_gt))
                link(v.reduce_sum(tiles, cnt, AX.X))
                link(v.tensor_tensor(cnt, upto[:], tiles.unsqueeze(1).to_broadcast([P, E, E]), ALU.mult))
                link(v.reduce_sum(ends, cnt, AX.X))
                link(v.tensor_tensor(base, ends, tiles, ALU.subtract))
                link(v.tensor_scalar(base, base, float(P), None, ALU.mult))
                v.tensor_tensor(pos, rank, base.unsqueeze(1).to_broadcast([P, T, E]), ALU.add)\
                    .then_inc(drained[bank], 1)
                wait_drained(dve, ("rank", n))
                for k in range(topk):
                    link(v.tensor_tensor(eq, one[k], pos, ALU.mult))
                    link(v.reduce_sum(slot_f, eq, AX.X))
                    link(v.tensor_copy(slot[:, k, :], slot_f))
                link(v.tensor_tensor(own_of[0:1], iota_j[0:1, 0:nt].unsqueeze(2).to_broadcast([1, nt, E]),
                                     ends[0:1].unsqueeze(1).to_broadcast([1, nt, E]), ALU.is_ge))
                link(v.reduce_sum(own_f[0:1], own_of[0:1], AX.X))
                link(v.tensor_scalar(own_f[0:1], own_f[0:1], float(E - 1), None, ALU.min))
                v.tensor_copy(owner[n][:], own_f[0:1]).then_inc(slots_done, 1)

            def expert_tiles(n, nt, hw, bufs):
                sg, hh, ht = bufs[2], bufs[3], bufs[4]
                for i in range(nt + 3):
                    j = i - 1
                    if 0 <= j < nt:
                        if n == 0:
                            bank = wait_filled(dve, ("eg", n, j))
                            dve.wait_ge(silu_done, j + 1)
                            up = ps[:, bank, hw:2 * hw]
                        else:
                            bank = wait_filled(dve, ("eu", n, j))
                            wait_drained(dve, ("eg", n, j))
                            up = ps[:, bank, 0:hw]
                        v.tensor_tensor(hh[:, j % 2, 0:hw], up, sg[:, j % 2, 0:hw], ALU.mult).then_inc(drained[bank], 1)
                    j = i - 2
                    if 0 <= j < nt:
                        bank = wait_filled(dve, ("eh", n, j))
                        w = max(hw, H)
                        v.tensor_copy(ht[:, j % 2, 0:w], ps[:, bank, 0:w]).then_inc(drained[bank], 1)

            def combine(n, topk, bufs, b):
                for i in range(TB * topk * b, TB * topk * (b + 1)):
                    t, k = divmod(i, topk)
                    dve.wait_ge(gathered[n][i % 8], 16 * (i // 8 + 1))
                    if k:
                        dve.wait_ge(added[n], i)
                    ins = v.scalar_tensor_tensor(X[:, t, :], bufs[6][:, i % 8, :], weight[k][:, t:t + 1], X[:, t, :],
                                                 ALU.mult, ALU.add)
                    ins.then_inc(added[n], 1)
                dve.wait_ge(added[n], TB * topk * (b + 1))

            normalise(1, lambda b: [wait_drained(dve, ("o", b, pr)) for pr in range(2)])
            route(0, 2)
            def shared_expert(c):
                for m in range(MS):
                    rows = min(P, IS0 - P * m)
                    bank = wait_filled(dve, ("su", c, m))
                    wait_drained(dve, ("sg", c, m))
                    v.tensor_tensor(HS[0:rows, m, :], ps[0:rows, bank, :], SSG[0:rows, (MS * c + m) % 2, :],
                                    ALU.mult).then_inc(drained[bank], 1)
                for pr in range(2):
                    bank = wait_filled(dve, ("sd", c, pr))
                    for e in range(2):
                        t = TB * c + 2 * pr + e
                        ins = v.scalar_tensor_tensor(X[:, t, :], ps[:, bank, H * e:H * e + H], gate[:, t:t + 1],
                                                     X[:, t, :], ALU.mult, ALU.add)
                    ins.then_inc(drained[bank], 1)
            shared_expert(0)
            expert_tiles(0, NT0, I0, bufs0)
            shared_expert(1)
            wait_drained(dve, ("sd", 1, 1))

            normalise(2, lambda b: combine(0, 2, bufs0, b))
            dve.wait_ge(in_rows1, 32)
            dve.wait_ge(masks_made, 3)
            dve.wait_ge(decays, 3)
            for t in range(T):
                bank = wait_filled(dve, ("kv", t))
                kd = KD1[:, t, :]
                link(v.tensor_tensor(kd, ps[:, bank, 0:H], bkv_row[:, 0:H], ALU.add))
                k3 = kd.rearrange("p (h e) -> p h e", h=NH)
                v.tensor_tensor(k3, k3, KDEC[:].unsqueeze(2).to_broadcast([P, NH, HD]), ALU.mult)\
                    .then_inc(kdec_done, 1)
                vp = VP[:, t, :].rearrange("p (a e) -> p a e", a=8)
                for e in range(2):
                    ins = v.tensor_tensor(vp[:, :, 32 * e:32 * e + HD],
                                          ps[:, bank, H:2 * H].rearrange("p (a e f) -> p a e f", a=8, e=2)[:, :, e, :],
                                          bkv_row[:, H:2 * H].rearrange("p (a e f) -> p a e f", a=8, e=2)[:, :, e, :],
                                          ALU.add)
                ins.then_inc(drained[bank], 1)
            for n in range(len(CHUNKS) + 1):
                if n < len(CHUNKS):
                    c, b, m = CHUNKS[n]
                    wait_drained(dve, ("q1", b, m))
                    if n >= 2:
                        wait_filled(dve, ("oc", n - 2))
                    v.tensor_tensor(QDEC[:, n % 2, :], QT1[:, m, tok(TB * b + c)], QD[:, m, :], ALU.mult)\
                        .then_inc(qdec_done, 1)
                    for hf in range(2):
                        bank = wait_filled(dve, ("sc", n, hf))
                        v.tensor_tensor(PD[:, n % 2, 512 * hf:512 * hf + 512].rearrange("p (h i) -> p h i", h=4),
                                        ps[:, bank, :].rearrange("p (h i) -> p h i", h=4),
                                        DT[:, 8 * m + 4 * hf:8 * m + 4 * hf + 4, :], ALU.mult).then_inc(drained[bank], 1)
                if n and CHUNKS[n - 1][0] < TB - 1:
                    c, b, m = CHUNKS[n - 1]
                    bank = wait_filled(dve, ("st", n - 1))
                    state = ST[:, 2 * b + m, :]
                    v.tensor_tensor(TMP[:, n % 2, :], ps[:, bank, 0:P],
                                    block_diag[:].rearrange("p j e -> p (j e)"), ALU.mult).then_inc(drained[bank], 1)
                    wait_drained(dve, ("st", n - 1))
                    v.scalar_tensor_tensor(state, state, chunk_decay[:, m:m + 1], TMP[:, n % 2, :],
                                           ALU.mult, ALU.add).then_inc(state_done, 1)
            for b in range(B):
                dve.wait_ge(bias_added, 3 + b)
                for pr in range(2):
                    bank = wait_filled(dve, ("op", b, pr))
                    xs = X[:, TB * b + 2 * pr:TB * b + 2 * pr + 2, :].rearrange("p t h -> p (t h)")
                    v.tensor_tensor(xs, ps[:, bank, :], xs, ALU.add).then_inc(drained[bank], 1)

            normalise(3, lambda b: [wait_drained(dve, ("op", b, pr)) for pr in range(2)])
            route(1, 1)
            expert_tiles(1, NT1, I1, bufs1)
            for b in range(B):
                combine(1, 1, bufs1, b)

        @block.tensor
        def _(pe):
            t_ = nc.tensor

            def transposes(n):
                for b in range(B):
                    pe.wait_ge(xn_done, T * n + TB * (b + 1))
                    for kt in range(KT):
                        bank = wait_free(pe, ("xt", n, b, kt))
                        for t in range(TB):
                            ins = t_.transpose(ps[:, bank, tok(t)], XN[:, TB * b + t, P * kt:P * kt + P], identity[:])
                        ins.then_inc(filled[bank], 1)

            def product(out, pairs, **kw):
                for n, (lhsT, rhs) in enumerate(pairs):
                    ins = t_.matmul(out, lhsT, rhs, start=n == 0, stop=n == len(pairs) - 1, **kw)
                return ins

            def w0(n, cols):
                w = part(W, 512 * n, KT, H)
                return [w[:, kt, cols] for kt in range(KT)]

            def project(i):
                qk, b, m = proj_key(i)
                pe.wait_ge(in_w[qk], 16)
                bank = wait_free(pe, ("qk", i))
                product(ps[:, bank, :], [(w, XT[:, kt, S * b:S * b + S]) for kt, w in
                                         enumerate(w0(qk, slice(P * m, P * m + P)))]).then_inc(filled[bank], 1)

            def token_products(key, b, pr, src, w):
                bank = wait_free(pe, key)
                for e in range(2):
                    t = TB * b + 2 * pr + e
                    ins = product(ps[:, bank, H * e:H * e + H], [(src[:, kt, tok(t)], w[kt]) for kt in range(KT)])
                ins.then_inc(filled[bank], 1)

            pe.wait_ge(consts, 2)
            transposes(0)
            for kt in range(KT):
                wait_drained(pe, ("xt", 0, 0, kt))
            for i in range(4):
                project(i)
            pe.wait_ge(in_w[2], 16)
            for pr in range(2):
                token_products(("v", 0, pr), 0, pr, XT, w0(2, slice(0, H)))
            for b in (1, 3, 5, 7):
                pe.wait_ge(drained[b], uses.before_attention[b])
            def maxima(u, qt, hp):
                b, g = divmod(u, 4)
                bank = wait_free(pe, ("mx", u, qt, hp))
                for e in range(2):
                    h = 4 * g + 2 * hp + e
                    ins = t_.matmul(ps[:, bank + e, :], QP[b][0:KR, h, tok(qt)], KP[b][0:KR, h, :],
                                    start=True, stop=True)
                ins.then_inc(filled[bank], 1)

            for q in range(NQ):
                w = quarter_of(q)
                if "max" in w:
                    u, qt = w["max"]
                    b, g = divmod(u, 4)
                    if qt == 0 and g % 2 == 0:
                        pe.wait_ge(packed[2 * b + g // 2], 16 * 12)
                    maxima(u, qt, 0)
                    if "score" not in w:
                        maxima(u, qt, 1)
                if "proj" in w:
                    if w["proj"] == 4:
                        for kt in range(KT):
                            wait_drained(pe, ("xt", 0, 1, kt))
                    project(w["proj"])
                if "v" in w:
                    token_products(("v", 1, w["v"]), 1, w["v"], XT, w0(2, slice(0, H)))
                if "negmax" in w:
                    u = w["negmax"]
                    bank = wait_free(pe, ("nm", u))
                    pe.wait_ge(negmax_done, u + 1)
                    t_.transpose(ps[0:48, bank, 0:P // 2].bitcast(BF16), NM[:, u % 2, :], identity_bf[:])\
                        .then_inc(filled[bank], 1)
                if "score" in w:
                    u, kt = w["score"]
                    b, g = divmod(u, 4)
                    if u == 0 and kt == 0:
                        pe.wait_ge(consts, 7)
                    if kt == 0:
                        pe.wait_ge(negmax_loaded[u], 16)
                    for h in range(4):
                        if h == 2 and "max" in w:
                            maxima(*w["max"], 1)
                        bank = wait_free(pe, ("s", u, kt, h))
                        t_.matmul(ps[:, bank, :], KP[b][0:KR + 3, 4 * g + h, tok(kt)], QP[b][0:KR + 3, 4 * g + h, :],
                                  start=True, stop=True).then_inc(filled[bank], 1)
                if "pv" in w:
                    u, kt = w["pv"]
                    b, g = divmod(u, 4)
                    if kt == 0:
                        wait_free(pe, ("pv", u))
                        for pr in range(2):
                            wait_drained(pe, ("v", b, pr))
                    for h in (2, 3):
                        wait_drained(pe, ("s", u, kt, h))
                    for h in range(4):
                        col = (HD + 1) * (4 * g + h)
                        ins = t_.matmul(ps[32 * h:32 * h + 32, 6, :], VA[:, TB * b + kt, col:col + 32],
                                        PT[:, (16 * u + 4 * kt + h) % NPT, :], start=kt == 0, stop=kt == 3)
                    ins.then_inc(filled[6] if kt == 3 else pv_done, 1)
                if "norm" in w:
                    u = w["norm"]
                    bank = wait_free(pe, ("ct", u))
                    wait_drained(pe, ("pv", u))
                    for t in range(TB):
                        ins = t_.transpose(ps[:, bank, tok(t)], CT[:, u % 2, tok(t)], identity[:])
                    ins.then_inc(filled[bank], 1)
                if "ctxT" in w:
                    b = w["ctxT"]
                    wait_drained(pe, ("ct", 4 * b + 3))
                    for kt in range(KT):
                        bank = wait_free(pe, ("cx", b, kt))
                        for t in range(TB):
                            ins = t_.transpose(ps[:, bank, tok(t)], XN[:, TB * b + t, P * kt:P * kt + P], identity[:])
                        ins.then_inc(filled[bank], 1)
                if "wo" in w:
                    b = w["wo"]
                    pe.wait_ge(in_w[3], 16)
                    for kt in range(KT):
                        wait_drained(pe, ("cx", b, kt))
                    for pr in range(2):
                        token_products(("o", b, pr), b, pr, XT, w0(3, slice(0, H)))

            def router(n, rw, nl):
                bank = wait_free(pe, ("r", n))
                for b in range(B):
                    for kt in range(KT):
                        wait_drained(pe, ("xt", 2 * n + 1, b, kt))
                for t in range(T):
                    ins = product(ps[:, bank, 16 * t:16 * t + nl],
                                  [(XT[:, kt, tok(t)], rw[:, kt, :]) for kt in range(KT)])
                ins.then_inc(filled[bank], 1)

            def ranks(n):
                pe.wait_ge(counted, n + 1)
                bank = wait_free(pe, ("rank", n))
                chosen = chosen_of[n]
                out = ps[:, bank, 0:(T + 1) * E]
                t_.matmul(out, before_bf[:], chosen, start=True, stop=True)
                for t in range(T):
                    ins = t_.matmul(ps[:, bank, E * (t + 1):(T + 1) * E].rearrange("p (t e) -> p t e", e=E), ones_bf[:],
                                    chosen[:, t:t + 1, :].to_broadcast([P, T - t, E]),
                                    start=False, stop=True, skip_group_check=True)
                ins.then_inc(filled[bank], 1)

            def expert_tiles(n, nt, hw, bufs, ups, downs):
                rows, xst, hh, ht = bufs[0], bufs[1], bufs[3], bufs[4]
                pe.wait_ge(slots_done, n + 1)
                expert = {}
                for i in range(nt + 3):
                    if i < nt:
                        pe.wait_ge(sorted_loaded[n][i % 4], 16 * (i // 4 + 1))
                        bank = wait_free(pe, ("ex", n, i))
                        for kt in range(KT):
                            ins = t_.transpose(ps[:, bank, tok(kt)], rows[:, i % 4, tok(kt)], identity[:])
                        ins.then_inc(filled[bank], 1)
                    j = i - 1
                    if 0 <= j < nt:
                        expert[j] = t_.value_load(owner[n][0:1, j:j + 1], min_val=0, max_val=E - 1)
                        wait_drained(pe, ("ex", n, j))
                        for key, w in ups:
                            bank = wait_free(pe, (key, n, j))
                            product(ps[:, bank, 0:w.shape[3]],
                                    [(xst[:, j % 2, tok(kt)], w[:, kt, bass.ds(expert[j], 1), :]) for kt in range(KT)])\
                                .then_inc(filled[bank], 1)
                    j = i - 2
                    if 0 <= j < nt:
                        wait_drained(pe, (ups[-1][0], n, j))
                        bank = wait_free(pe, ("eh", n, j))
                        if n == 0:
                            starts = (0, hw - P)
                        else:
                            starts = range(0, hw, P)
                        for k, c in enumerate(starts):
                            ins = t_.transpose(ps[:, bank, tok(k)], hh[:, j % 2, c:c + P], identity[:])
                        ins.then_inc(filled[bank], 1)
                    j = i - 3
                    if 0 <= j < nt:
                        wait_drained(pe, ("eh", n, j))
                        bank = wait_free(pe, ("ed", n, j))
                        product(ps[:, bank, 0:H], [(ht[:, j % 2, tok(k)], w[:, bass.ds(expert[j], 1), :])
                                                   for k, w in enumerate(downs)]).then_inc(filled[bank], 1)

            for b in (0, 2):
                pe.wait_ge(drained[b], uses.attention_ends[b // 2])
            transposes(1)
            pe.wait_ge(in_small, 16 * 4)
            router(0, r0w, E + 1)
            pe.wait_ge(in_ffn0, 16 * FFN0_PIECES)
            def shared_expert(c):
                for m in range(MS):
                    rows = min(P, IS0 - P * m)
                    for key, w in (("sg", sg0), ("su", su0)):
                        bank = wait_free(pe, (key, c, m))
                        product(ps[0:rows, bank, :], [(w[:, kt, P * m:P * m + rows], XT[:, kt, S * c:S * c + S])
                                                      for kt in range(KT)]).then_inc(filled[bank], 1)
                    if c == 0 and m == 2:
                        ranks(0)
                for m in range(MS):
                    wait_drained(pe, ("su", c, m))
                for pr in range(2):
                    bank = wait_free(pe, ("sd", c, pr))
                    for e in range(2):
                        t = 2 * pr + e
                        ins = product(ps[:, bank, H * e:H * e + H],
                                      [(HS[0:min(P, IS0 - P * m), m, tok(t)], sd0[0:min(P, IS0 - P * m), m, :])
                                       for m in range(MS)])
                    ins.then_inc(filled[bank], 1)
            shared_expert(0)
            expert_tiles(0, NT0, I0, bufs0, [("eg", gu0)], [da0, db0])
            shared_expert(1)

            transposes(2)
            pe.wait_ge(in_w1, 32)
            wqkv = part(W, 0, KT, 3 * H)
            for b in range(B):
                for kt in range(KT):
                    wait_drained(pe, ("xt", 2, b, kt))
                for m in range(KT):
                    for n, key in enumerate(("q1", "k1")):
                        bank = wait_free(pe, (key, b, m))
                        product(ps[:, bank, :], [(wqkv[:, kt, H * n + P * m:H * n + P * m + P], XT[:, kt, S * b:S * b + S])
                                                 for kt in range(KT)]).then_inc(filled[bank], 1)
                for t in range(TB * b, TB * b + TB):
                    bank = wait_free(pe, ("kv", t))
                    product(ps[:, bank, :], [(XT[:, kt, tok(t)], wqkv[:, kt, H:3 * H]) for kt in range(KT)])\
                        .then_inc(filled[bank], 1)
            states = {}

            def chunk_out(n):
                c, b, m = CHUNKS[n]
                t = TB * b + c
                pe.wait_ge(qdec_done, n + 1)
                if c:
                    pe.wait_ge(state_done, states[c - 1, b, m])
                for hf in range(2):
                    wait_drained(pe, ("sc", n, hf))
                bank = wait_free(pe, ("oc", n))
                t_.matmul(ps[:, bank, 0:P], ST[:, 2 * b + m, :], QDEC[:, n % 2, :], start=True, stop=True)
                for k in range(HP):
                    pair, e = divmod(k, 2)
                    col = 48 * (4 * m + pair) + 16 * e
                    ins = t_.matmul(ps[32 * pair:32 * pair + 32, bank, 0:P], VP[:, t, col:col + 32],
                                    PD[:, n % 2, P * k:P * k + P], start=False, stop=True, skip_group_check=True)
                ins.then_inc(filled[bank], 1)
                if c < TB - 1:
                    bank = wait_free(pe, ("st", n))
                    states[c, b, m] = len(states) + 1
                    pe.wait_ge(kdec_done, t + 1)
                    vv = VP[:, t, 192 * m:192 * m + 192].rearrange("p (a s) -> p a s", a=4)
                    vv = vv[:, :, 0:48].rearrange("p a (e f) -> p a e f", e=3)[:, :, 0:3:2, :]
                    t_.matmul(ps[:, bank, 0:P], KD1[:, t, P * m:P * m + P], vv, start=True, stop=True)\
                        .then_inc(filled[bank], 1)

            pe.wait_ge(masks_made, 3)
            for n, (c, b, m) in enumerate(CHUNKS):
                if c == 0:
                    wait_drained(pe, ("k1", b, m))
                    for t in range(TB * b, TB * b + TB):
                        wait_drained(pe, ("kv", t))
                pe.wait_ge(spread, n + 1)
                for hf in range(2):
                    bank = wait_free(pe, ("sc", n, hf))
                    t_.matmul(ps[:, bank, :], KT1[:, m, tok(TB * b + c)], QB[:, n % 2, 512 * hf:512 * hf + 512],
                              start=True, stop=True).then_inc(filled[bank], 1)
                if n:
                    chunk_out(n - 1)
            chunk_out(len(CHUNKS) - 1)
            for b in range(B):
                for m in range(KT):
                    for c in range(TB):
                        wait_drained(pe, ("oc", CHUNKS.index((c, b, m))))
                for pr in range(2):
                    token_products(("op", b, pr), b, pr, OT,
                                   [part(W, 1536, KT, H)[:, kt, :] for kt in range(KT)])

            transposes(3)
            router(1, r1w, E)
            ranks(1)
            pe.wait_ge(in_ffn1, 16 * 16)
            pe.wait_ge(in_gate1, 16)
            expert_tiles(1, NT1, I1, bufs1, [("eg", gate1), ("eu", up1)],
                         [down1[:, k, :, :] for k in range(I1 // P)])


def kernel(**inputs):
    import numpy as np
    import concourse.bacc as bacc
    from concourse.bass_utils import run_bass_kernel_spmd as launch

    a = {k: np.asarray(v) for k, v in inputs.items()}

    def rows(w):
        return np.ascontiguousarray(w.reshape(w.shape[0] // 128, 128, -1).swapaxes(0, 1))

    def col(v):
        return v.reshape(2, 128).T

    def by_expert(w):
        return np.ascontiguousarray(w.reshape(w.shape[0], -1, 128, w.shape[2]).transpose(2, 1, 0, 3))

    wd = a["L0_ffn_w_down"]
    tail = np.zeros((8, 128, 256), wd.dtype)
    tail[:, 80:] = wd[:, 128:]
    shared_down = np.zeros((768, 256), wd.dtype)
    shared_down[:704] = a["L0_ffn_sw_down"]
    arrays = {
        "x": a["L0_attn_x"],
        "w0": np.stack([rows(a["L0_attn_" + n].T).reshape(128, 512) for n in ("Wq", "Wk", "Wv", "Wo")]),
        "bias_col": np.stack([col(a["L0_attn_bq"]), col(a["L0_attn_bk"]), col(a["L1_attn_bqkv"][:256]),
                              col(a["L1_attn_bqkv"][256:512])], axis=1),
        "bv0": a["L0_attn_bv"],
        "bo0": a["L0_attn_bo"],
        "slopes": a["L1_attn_slopes"],
        "slopes_col": col(np.repeat(a["L1_attn_slopes"], 16)),
        "r0w": rows(np.concatenate([a["L0_ffn_gate_w"].T, a["L0_ffn_shared_gate_w"]], axis=1)),
        "r1w": rows(a["L1_ffn_router_w"]),
        "ffn0": np.concatenate([w.reshape(128, -1) for w in (
            by_expert(np.concatenate([a["L0_ffn_w_gate"], a["L0_ffn_w_up"]], axis=2)),
            wd[:, :128].swapaxes(0, 1), tail.swapaxes(0, 1), rows(a["L0_ffn_sw_gate"]), rows(a["L0_ffn_sw_up"]),
            rows(shared_down))], axis=1),
        "wqkv1": rows(a["L1_attn_Wqkv"]).reshape(128, 1536),
        "wout1": rows(a["L1_attn_Wout"]).reshape(128, 512),
        "bkv1": a["L1_attn_bqkv"][256:],
        "bout1": a["L1_attn_bout"],
        "gate1": by_expert(a["L1_ffn_gate_w"]),
        "ffn1": np.concatenate([by_expert(a["L1_ffn_up_w"]).reshape(128, -1),
                                by_expert(a["L1_ffn_down_w"]).reshape(128, -1)], axis=1),
    }
    arrays = {k: np.ascontiguousarray(v) for k, v in arrays.items()}
    nc = bacc.Bacc("TRN2", target_bir_lowering=False, num_devices=1)
    d = {k: nc.dram_tensor("in_" + k, v.shape, mybir.dt.from_np(v.dtype), kind="ExternalInput").ap()
         for k, v in arrays.items()}
    d["out"] = nc.dram_tensor("out", [2, 512, 256], mybir.dt.float32, kind="ExternalOutput").ap()
    two_layers(nc, d)
    r = launch(nc, [{"in_" + k: v for k, v in arrays.items()}], core_ids=[0])
    return r.results[0]["out"]
```

```python
from contextlib import ExitStack

import concourse.bass as bass
from concourse import mybir

F32 = mybir.dt.float32
BF16 = mybir.dt.bfloat16
I32 = mybir.dt.int32
ALU = mybir.AluOpType
ACT = mybir.ActivationFunctionType
AX = mybir.AxisListType

P = 128
B, S, H = 2, 512, 256
TB = S // P
T = B * TB
KT = H // P
NH, HD = 16, 16
HP = P // HD
E = 8
I0, IS0, I1 = 176, 704, 512
GU0 = 2 * I0
MS = 6
NT0 = 2 * B * S // P + E - 1
NT1 = B * S // P + E - 1
FFN0_PIECES = 20
NZ = (NT0 + 1) // 2 + (NT1 + 1) // 2
KR = 6 * HD
UN = 8
LAG = 7
NPT = 8


TWO_ONES = 1.0 + 0x3F80 / 2 ** 23


class Uses:

    def __init__(self):
        self.at, self.count, self.turn = {}, [0] * 8, 0

    def next7(self, keep):
        bank = self.turn
        self.turn = (bank + 1) % (7 if keep else 8)
        return bank

    def add(self, key, bank=None):
        if bank is None:
            bank = self.turn
            self.turn = (self.turn + 1) % 8
        self.at[key] = (bank, self.count[bank])
        self.count[bank] += 1


def quarter_of(q):
    out = {}
    if q < 4 * UN:
        out["max"] = divmod(q, 4)
    if q % 4 == 0 and 0 < q <= 4 * UN:
        out["negmax"] = q // 4 - 1
    if q < 8 - EARLY:
        out["project"] = EARLY + q
    if LATER <= q < 8 - EARLY + LATER:
        out["remainder"] = EARLY + q - LATER
    if 0 <= q - LAG < 4 * UN:
        out["score"] = divmod(q - LAG, 4)
    if 0 <= q - LAG - 1 < 4 * UN:
        out["pv"] = divmod(q - LAG - 1, 4)
    if 0 <= q - LAG - 2 < 4 * UN and (q - LAG - 2) % 4 == 3:
        out["norm"] = (q - LAG - 2) // 4
    if 0 <= q - LAG - 3 < 4 * UN and (q - LAG - 3) % 16 == 15:
        out["ctxT"] = (q - LAG - 3) // 16
    if 0 <= q - LAG - 4 < 4 * UN and (q - LAG - 4) % 16 == 15:
        out["wo"] = (q - LAG - 4) // 16
    return out


NQ = 4 * UN + LAG + 4
WARM = 36
EARLY = 6
LATER = 1
TAIL_BANKS = (3, 4, 5, 0, 1, 2)
SHARED_BANKS = (0, 1, 2, 3, 4, 5, 7)


def proj_key(i):
    return i % 2, i // 4, i // 2 % 2


def plan():
    u = Uses()
    for kt in range(KT):
        u.add(("xt", 0, 0, kt))
    for i in range(4):
        u.add(("qk", i))
    for kt in range(KT):
        u.add(("xt", 0, 1, kt))
    for b in range(B):
        for pr in range(2):
            u.add(("v", b, pr), 2 * b + pr)
    for i in range(4, 8):
        u.add(("qk", i), i)
    for q in range(NQ):
        w = quarter_of(q)
        if "max" in w:
            for h in range(4):
                u.add(("mx", *w["max"], h), (4 * q + h) % 3)
        if "negmax" in w:
            u.add(("nm", w["negmax"]), 7)
        if "score" in w:
            for h in range(4):
                u.add(("s", *w["score"], h), 3 + (4 * q + h) % 3 if q < 4 * UN + 1 else TAIL_BANKS[(4 * q + h) % 6])
        if "pv" in w and w["pv"][1] == 0:
            u.add(("pv", w["pv"][0]), 6)
        if "norm" in w:
            u.add(("ct", w["norm"]), 7)
        if "ctxT" in w:
            for kt in range(KT):
                u.add(("cx", w["ctxT"], kt), 7 if w["ctxT"] == 0 or kt == 0 else 0)
            if w["ctxT"] == 1:
                for kt in range(KT):
                    u.add(("xt", 1, 0, kt), 4 + kt)
        if "wo" in w:
            for pr in range(2):
                u.add(("o", w["wo"], pr), 7 if w["wo"] == 0 or pr == 0 else 0)
    u.add(("r", 0), 6)

    def shared(c, ms=range(MS)):
        for m in ms:
            for i, key in enumerate(("sg", "su")):
                u.add((key, c, m), SHARED_BANKS[(2 * m + i) % 7] if c == 0 else None)
        if ms[-1] == MS - 1:
            for pr in range(2):
                u.add(("sd", c, pr))

    shared(0, range(2))
    for kt in range(KT):
        u.add(("xt", 1, 1, kt), (5, 7)[kt])
    u.add(("rank", 0), 6)
    shared(0, range(2, MS))
    for i in range(NT0 + 3):
        if i < NT0:
            u.add(("ex", 0, i))
        if 0 <= i - 1 < NT0:
            u.add(("eg", 0, i - 1))
        if 0 <= i - 2 < NT0:
            u.add(("eh", 0, i - 2))
        if 0 <= i - 3 < NT0:
            u.add(("ed", 0, i - 3))
    shared(1)
    for kt in range(KT):
        u.add(("xt", 2, 0, kt))
    for b in range(B):
        for m in range(KT):
            u.add(("q1", b, m))
            u.add(("k1", b, m))
        for t in range(TB):
            u.add(("kv", TB * b + t))
        if b == 0:
            for kt in range(KT):
                u.add(("xt", 2, 1, kt))
        else:
            u.add(("r", 1), 7)
            u.turn = 0
            for kt in range(KT):
                u.add(("xt", 3, 0, kt))
        first = NC * b
        for n in range(first, first + NC + 1):
            if n < first + NC:
                for hf in range(2):
                    u.add(("sc", n, hf), u.next7(b))
            if n > first:
                u.add(("oc", n - 1), u.next7(b))
                if CHUNKS[n - 1][0] < TB - 1:
                    u.add(("st", n - 1), u.next7(b))
        for pr in range(2):
            u.add(("op", b, pr), u.next7(b))
    for kt in range(KT):
        u.add(("xt", 3, 1, kt), u.next7(1))
    u.turn = 0
    u.add(("rank", 1))
    for i in range(NT1 + 3):
        if 0 <= i - 1 < NT1:
            u.add(("eg", 1, i - 1))
            u.add(("eu", 1, i - 1))
        if i < NT1:
            u.add(("ex", 1, i))
        if 0 <= i - 2 < NT1:
            u.add(("eh", 1, i - 2))
        if 0 <= i - 3 < NT1:
            u.add(("ed", 1, i - 3))
    return u


CHUNKS = [(c, b, m) for b in range(B) for c in range(TB) for m in range(KT)]
NC = len(CHUNKS) // B


def two_layers(nc, d):
    uses = plan()
    ctx = ExitStack()
    with ctx:
        def sb(name, shape, dt=F32):
            return ctx.enter_context(nc.sbuf_tensor(name, shape, dt))

        def sem(name):
            return ctx.enter_context(nc.semaphore(name))

        def sems(name, n):
            return [sem(f"{name}{i}") for i in range(n)]

        R1 = sb("R1", [P, 16384])
        R2 = sb("R2", [P, 8192])
        R3 = sb("R3", [P, 4096])
        R4 = sb("R4", [P, 14080])
        W = sb("W", [P, 2048])
        ROW = 2 * H + 2
        rows_all = sb("rows_all", [P, T, ROW])
        XN = rows_all[:, :, 0:H]
        X = rows_all[:, :, H:2 * H]
        XT = sb("XT", [P, KT, B * S])

        def part(region, at, *shape, dt=F32):
            n = 1
            for s in shape:
                n *= s
            words = n // 2 if dt == BF16 else n
            v = region[:, at:at + words]
            if dt != F32:
                v = v.bitcast(dt)
            if len(shape) == 2:
                v = v.rearrange("p (a b) -> p a b", a=shape[0])
            elif len(shape) == 3:
                v = v.rearrange("p (a b c) -> p a b c", a=shape[0], b=shape[1])
            return v

        QP = [part(R1, 8192 * b, NH, S, dt=BF16) for b in range(B)]
        KP = [part(R1, 8192 * b + 4096, NH, S, dt=BF16) for b in range(B)]
        up1 = part(R1, 0, KT, E, I1)
        down1 = part(R1, 8192, I1 // P, E, H)
        gate1 = part(R2, 0, KT, E, I1)
        VS = NH * (HD + 1) + HD
        VA = part(R2, 0, T, VS)
        PT = part(R2, 2304, NPT, S)
        CT = part(R2, 6400, 2, S)
        bv_row = part(R2, 7424, H)
        bo_row = part(R2, 7680, H)
        PC = part(R3, 0, 4, 3 * S, dt=BF16)
        RES = part(R3, 3072, 2, S)
        HS = part(R3, 0, MS, S)
        SSG = part(R3, 3072, 2, S)
        PD = part(R3, 0, 2, HP * P)
        first_of = part(R3, 0, T, P)
        QB = part(R3, 2048, 2, HP * P)
        gu0 = part(R4, 0, KT, E, GU0)
        da0 = part(R4, 5632, E, H)
        db0 = part(R4, 7680, E, H)
        sg0 = part(R4, 9728, KT, IS0)
        su0 = part(R4, 11136, KT, IS0)
        sd0 = part(R4, 12544, MS, H)
        QT1 = part(R4, 0, KT, B * S)
        KT1 = part(R4, 2048, KT, B * S)
        VP = part(R4, 4096, T, 8 * 48)
        DT = part(R4, 7168, NH, P)
        bkv_row = part(R4, 9216, 2 * H)
        KD1 = part(R4, 9728, T, H)
        QDEC = part(R4, 11776, 2, P)
        ST = part(R4, 12032, 4, P)
        TMP = part(R4, 12544, 2, P)
        bout_row = part(R4, 12800, H)
        QD = part(R4, 13056, KT, P)

        def tile_buffers(region, n, hw):
            at, out = 0, []
            for shape in ((4, H) if n == 0 else (8, ROW), (2, H), (2, hw), (2, hw), (2, max(hw, H)), (4, H),
                          (16 if n == 0 else 0, H)):
                out.append(part(region, at, *shape) if shape[0] else None)
                at += shape[0] * shape[1]
            return out + [at]

        *bufs0, small0 = tile_buffers(R2, 0, I0)
        *bufs1, small1 = tile_buffers(R4, 1, I1)

        logits = [part(W, 0, T, E + 1), part(R4, small1, T, E + 1)]
        chosen_of = {}

        identity = sb("identity", [P, P])
        identity_bf = sb("identity_bf", [P, P], BF16)
        ones_bf = sb("ones_bf", [P, P], BF16)
        before_bf = sb("before_bf", [P, P], BF16)
        diff = sb("diff", [P, P])
        iota_i = sb("iota_i", [P, P])
        block_diag = sb("block_diag", [P, HP, HD])
        iota_e = sb("iota_e", [P, E])
        steps = sb("steps", [P, E])
        upto = sb("upto", [P, E, E])
        below = sb("below", [P, E, E])
        iota_j = sb("iota_j", [P, NT0])
        back = sb("back", [P, 1])
        blank = sb("blank", [P, ROW])
        slopes_row = sb("slopes_row", [P, NH])
        nslopes_row = sb("nslopes_row", [P, NH])
        slopes_col = sb("slopes_col", [P, KT])
        nslopes_col = sb("nslopes_col", [P, KT])
        KDEC = sb("KDEC", [P, NH])
        chunk_decay = sb("chunk_decay", [P, KT])
        bias_col = sb("bias_col", [P, 4, KT])
        r0w = sb("r0w", [P, KT, E + 1])
        r1w = sb("r1w", [P, KT, E])
        stats = sb("stats", [P, T, 6])
        mv = sb("mv", [P, T, 2])
        sd = sb("sd", [P, T])
        rstd = sb("rstd", [P, T])
        eps = sb("eps", [P, 1])
        MX = sb("MX", [P, UN, 4, TB])
        nres = sb("nres", [P, 16])
        NM = sb("NM", [P, 2, 48], BF16)
        NMT = sb("NMT", [48, 2, P], BF16)
        RD = sb("RD", [P, 16])
        gate = sb("gate", [P, T])
        weight = [sb(f"weight{k}", [P, T]) for k in range(2)]
        slot = sb("slot", [P, 2, T], I32)
        target = sb("target", [P, 8], I32)
        owner = [sb(f"owner{n}", [1, nt], I32) for n, nt in enumerate((NT0, NT1))]
        ps = ctx.enter_context(nc.psum_tensor("ps", [P, 8, 512], F32))

        qkp = [nc.dram_tensor(f"qkp{i}", [3, P, S], BF16, kind="Internal").ap() for i in range(8)]
        nmr = [nc.dram_tensor(f"nmr{i}", [48, P], BF16, kind="Internal").ap() for i in range(UN)]
        sorted_x = [nc.dram_tensor(f"sorted_x{n}", [(nt + 1) // 2 * 2 * P, (H, ROW)[n]], F32, kind="Internal").ap()
                    for n, nt in enumerate((NT0, NT1))]
        sorted_y = nc.dram_tensor("sorted_y", [NT0 * P, H], F32, kind="Internal").ap()

        filled, drained = sems("filled", 8), sems("drained", 8)
        in_x = sems("in_x", 2 * B)
        in_w = sems("in_proj", 4)
        in_small = sem("in_small")
        in_bias = sem("in_bias")
        in_rows0 = sem("in_rows0")
        in_ffn0 = sem("in_ffn0")
        in_w1 = sem("in_w1")
        in_rows1 = sem("in_rows1")
        in_ffn1 = sem("in_ffn1")
        in_gate1 = sem("in_gate1")
        zeroed = sem("zeroed")
        consts = sem("consts")
        iotas = sem("iotas")
        vector_step = sem("vector_step")
        scalar_step = sem("scalar_step")
        pool_step = sem("pool_step")
        moments = sem("moments")
        sqrt_done = sem("sqrt_done")
        xn_done = sem("xn_done")
        part1_done = sem("part1_done")
        part2_done = sem("part2_done")
        part3_done = sem("part3_done")
        parts_stored = sems("parts_stored", 8)
        packed = sems("packed", 4)
        bias_added = sem("bias_added")
        negmax_done = sem("negmax_done")
        negmax_stored = sems("negmax_stored", UN)
        negmax_loaded = sems("negmax_loaded", UN)
        pv_done = sem("pv_done")
        silu_done = sem("silu_done")
        route_exp_done = sem("route_exp_done")
        counted = sem("counted")
        slots_done = sem("slots_done")
        owners_done = sem("owners_done")
        scattered = sems("scattered", 2)
        sorted_loaded = [sems(f"sorted_loaded{n}_", (4, 8)[n]) for n in range(2)]
        y_stored = sems("y_stored", 4)
        gathered = sems("gathered", 16)
        added = sem("added")
        target_done = sem("target_done")
        decays = sem("decays")
        masks_made = sem("masks_made")
        spread = sem("spread")
        qdec_done = sem("qdec_done")
        kdec_done = sem("kdec_done")
        state_done = sem("state_done")
        out_sent = sems("out_sent", 4)
        in_bkv1 = sem("in_bkv1")
        first_found = sem("first_found")

        def wait_free(pe, key):
            bank, n = uses.at[key]
            if n:
                pe.wait_ge(drained[bank], n)
            return bank

        def wait_filled(eng, key):
            bank, n = uses.at[key]
            eng.wait_ge(filled[bank], n + 1)
            return bank

        def wait_drained(eng, key):
            bank, n = uses.at[key]
            eng.wait_ge(drained[bank], n + 1)

        def tok(t, n=1):
            return slice(P * t, P * (t + n))

        block = ctx.enter_context(nc.Block())

        @block.sync
        def _(sp):
            for b in range(B):
                for half in range(2):
                    t = TB * b + 2 * half
                    sp.dma_start(X[:, t:t + 2, :], d["x"][b, 2 * P * half:2 * P * half + 2 * P, :]
                                 .rearrange("(t p) h -> p t h", p=P)).then_inc(in_x[2 * b + half], 16)
                if b == 0:
                    for n in range(2):
                        sp.dma_start(part(W, 512 * n, 512), d["w0"][n]).then_inc(in_w[n], 16)
                    sp.dma_start(bias_col[:], d["bias_col"]).then_inc(in_bias, 16)
            sp.dma_start(part(W, 1024, 512), d["w0"][2]).then_inc(in_w[2], 16)
            sp.dma_start(bv_row, d["bv0"].partition_broadcast(P)).then_inc(in_rows0, 16)
            sp.dma_start(bo_row, d["bo0"].partition_broadcast(P)).then_inc(in_rows0, 16)
            sp.dma_start(part(W, 1536, 512), d["w0"][3]).then_inc(in_w[3], 16)
            sp.dma_start(slopes_row[:], d["slopes"].partition_broadcast(P)).then_inc(in_small, 16)
            sp.dma_start(slopes_col[:], d["slopes_col"]).then_inc(in_small, 16)
            sp.dma_start(r0w[:], d["r0w"]).then_inc(in_small, 16)
            sp.dma_start(r1w[:], d["r1w"]).then_inc(in_small, 16)

            def store_parts(i):
                qk, b, m = proj_key(i)
                sp.wait_ge(part3_done, i + 1)
                sp.dma_start(qkp[i].rearrange("a p t -> p a t"),
                             PC[:, i % 4, :].rearrange("p (a t) -> p a t", a=3)).then_inc(parts_stored[i], 16)

            def load_packed(i):
                qk, b, m = proj_key(i)
                sp.wait_ge(parts_stored[i], 16)
                row = 0
                for k, n in enumerate((3, 2, 1)):
                    src = qkp[i][0:n] if qk else qkp[i][k:k + 1].to_broadcast([n, P, S])
                    sp.dma_start((QP, KP)[qk][b][HD * row:HD * (row + n), HP * m:HP * m + HP, :],
                                 src.rearrange("a (e j) t -> a e j t", j=HP)).then_inc(packed[2 * b + m], 16)
                    row += n

            store_parts(0)
            store_parts(1)
            load_packed(0)
            load_packed(1)
            store_parts(2)
            store_parts(3)
            load_packed(2)
            load_packed(3)
            store_parts(4)
            store_parts(5)
            load_packed(4)
            store_parts(6)
            load_packed(5)
            sp.wait_ge(consts, 3)

            def ffn0_weights(c):
                cols = slice(704 * c, 704 * c + 704)
                sp.dma_start(R4[:, cols], d["ffn0"][:, cols]).then_inc(in_ffn0, 16)

            def zero_rows(n, j):
                sp.dma_start(sorted_x[n][P * j:P * j + 2 * P, :].rearrange("(j p) h -> p j h", p=P),
                             blank[:, 0:(H, ROW)[n]].unsqueeze(1).to_broadcast([P, 2, (H, ROW)[n]]))\
                    .then_inc(zeroed, 16)

            pieces = [(ffn0_weights, (c,)) for c in range(FFN0_PIECES)]
            pieces += [(zero_rows, (n, j)) for n, nt in enumerate((NT0, NT1)) for j in range(0, nt, 2)]
            per_quarter = -(-len(pieces) // (4 * UN - 6))
            for q in range(NQ):
                w = quarter_of(q)
                if "max" in w and q >= 6:
                    wait_filled(sp, ("mx", *w["max"], 3))
                    for piece, args in pieces[per_quarter * (q - 6):per_quarter * (q - 5)]:
                        piece(*args)
                if "negmax" in w:
                    u = w["negmax"]
                    wait_drained(sp, ("nm", u))
                    sp.dma_start(nmr[u], NMT[:, u % 2, :]).then_inc(negmax_stored[u], 16)
                    sp.wait_ge(negmax_stored[u], 16)
                    b, g = divmod(u, 4)
                    sp.dma_start(QP[b][KR:KR + 3, 4 * g:4 * g + 4, :],
                                 nmr[u].rearrange("(a h q) t -> a h (q t)", a=3, h=4))\
                        .then_inc(negmax_loaded[u], 16)
                    if u == 0:
                        store_parts(7)
                        load_packed(6)
                        load_packed(7)
            for b in range(B):
                for pr in range(2):
                    wait_filled(sp, ("o", b, pr))

            def ffn1_weights(c):
                cols = slice(1024 * c, 1024 * c + 1024)
                sp.dma_start(R1[:, cols], d["ffn1"][:, cols]).then_inc(in_ffn1, 16)

            def expert_tiles(n, nt, k, bufs):
                rows, out = bufs[0], bufs[5]
                ring = (4, 8)[n]

                def load(j):
                    if j >= ring:
                        (wait_filled if n == 0 else wait_drained)(sp, (("ex", "ed")[n], n, j - ring))
                    sp.dma_start(rows[:, j % ring, :], sorted_x[n][P * j:P * j + P, :])\
                        .then_inc(sorted_loaded[n][j % ring], 16)

                sp.wait_ge(scattered[n], 16 * T * k)
                for j in range(4):
                    load(j)
                for i in range(nt + 3):
                    if i + 4 < nt:
                        load(i + 4)
                    if n == 0 and i < 16:
                        ffn1_weights(i)
                    j = i - 3
                    if n == 0 and j >= 0:
                        wait_drained(sp, ("ed", n, j))
                        sp.dma_start(sorted_y[P * j:P * j + P, :], out[:, j % 4, :])\
                            .then_inc(y_stored[j % 4], 16)

            sp.wait_ge(owners_done, 1)
            sp.dma_start(part(W, 0, 1536), d["wqkv1"]).then_inc(in_w1, 16)
            sp.dma_start(part(W, 1536, 512), d["wout1"]).then_inc(in_w1, 16)
            expert_tiles(0, NT0, 2, bufs0)
            sp.dma_start(bkv_row, d["bkv1"].partition_broadcast(P)).then_inc(in_bkv1, 16)
            sp.wait_ge(added, 2 * T)
            sp.dma_start(bout_row, d["bout1"].partition_broadcast(P)).then_inc(in_rows1, 16)
            sp.dma_start(gate1, d["gate1"]).then_inc(in_gate1, 16)
            expert_tiles(1, NT1, 1, bufs1)
            for i in range(4):
                sp.wait_ge(out_sent[i], 16 * len(range(i, NT1, 4)))

        @block.gpsimd
        def _(pool):
            g = nc.gpsimd
            own = [0]

            def link(ins):
                own[0] += 1
                ins.then_inc(pool_step, 1)
                pool.wait_ge(pool_step, own[0])

            link(g.memset(identity[:], 0.0))
            g.affine_select(out=identity[:], in_=identity[:], compare_op=ALU.not_equal, fill=1.0, base=0,
                            pattern=[[-1, P]], channel_multiplier=1).then_inc(consts, 1)
            pool.wait_ge(consts, 1)
            g.tensor_copy(identity_bf[:], identity[:]).then_inc(consts, 1)
            link(g.memset(blank[:], 0.0))
            g.memset(blank[:, ROW - 1:ROW], 4.0 * B * S).then_inc(consts, 1)
            g.memset(eps[:], 1e-5).then_inc(consts, 1)
            g.memset(part(R2, 0, T * VS), 1.0).then_inc(consts, 1)

            def third_part(i):
                pool.wait_ge(part2_done, i + 1)
                if i >= 4:
                    pool.wait_ge(parts_stored[i - 4], 16)
                g.tensor_tensor(PC[:, i % 4, 2 * S:3 * S], RES[:, i % 2, :], PC[:, i % 4, S:2 * S],
                                ALU.subtract).then_inc(part3_done, 1)

            for i in range(8):
                third_part(i)
            pool.wait_ge(part3_done, 8)
            for b in range(B):
                g.memset(KP[b][KR:KR + 3, :, :].rearrange("p h t -> p (h t)").bitcast(F32), TWO_ONES)\
                    .then_inc(consts, 1)
                pool.wait_ge(consts, 6 + b)
            link(g.memset(ones_bf[:], 1.0))
            g.affine_select(out=before_bf[:], in_=ones_bf[:], compare_op=ALU.is_gt, fill=0.0, base=0,
                            pattern=[[1, P]], channel_multiplier=-1).then_inc(iotas, 1)
            g.iota(iota_e[:], pattern=[[1, E]], base=0, channel_multiplier=0,
                   allow_small_or_imprecise_dtypes=True).then_inc(iotas, 1)
            g.iota(steps[:], pattern=[[P, E]], base=0, channel_multiplier=0,
                   allow_small_or_imprecise_dtypes=True).then_inc(iotas, 1)
            g.iota(iota_j[:], pattern=[[1, NT0]], base=0, channel_multiplier=0,
                   allow_small_or_imprecise_dtypes=True).then_inc(iotas, 1)
            link(g.memset(upto[:], 1.0))
            g.affine_select(out=upto[:], in_=upto[:], compare_op=ALU.is_ge, fill=0.0, base=0,
                            pattern=[[1, E], [-1, E]], channel_multiplier=0).then_inc(iotas, 1)
            link(g.memset(below[:], float(P)))
            g.affine_select(out=below[:], in_=below[:], compare_op=ALU.is_gt, fill=0.0, base=0,
                            pattern=[[1, E], [-1, E]], channel_multiplier=0).then_inc(iotas, 1)
            g.iota(rows_all[:, :, ROW - 1:ROW], pattern=[[P, T], [0, 1]], base=0, channel_multiplier=1,
                   allow_small_or_imprecise_dtypes=True).then_inc(iotas, 1)
            g.iota(iota_i[:], pattern=[[1, P]], base=0, channel_multiplier=0,
                   allow_small_or_imprecise_dtypes=True).then_inc(iotas, 1)
            g.iota(back[:], pattern=[[0, 1]], base=-P, channel_multiplier=1,
                   allow_small_or_imprecise_dtypes=True).then_inc(iotas, 1)
            link(g.iota(diff[:], pattern=[[1, P]], base=0, channel_multiplier=-1,
                        allow_small_or_imprecise_dtypes=True))
            g.tensor_scalar(diff[:], diff[:], 0.0, None, ALU.max).then_inc(iotas, 1)
            link(g.memset(block_diag[:], 1.0))
            link(g.affine_select(out=block_diag[:], in_=block_diag[:], compare_op=ALU.is_ge, fill=0.0, base=0,
                                 pattern=[[-HD, HP], [0, HD]], channel_multiplier=1))
            g.affine_select(out=block_diag[:], in_=block_diag[:], compare_op=ALU.is_ge, fill=0.0, base=HD - 1,
                            pattern=[[HD, HP], [0, HD]], channel_multiplier=-1).then_inc(iotas, 1)
            pool.wait_ge(in_small, 16 * 4)
            g.tensor_scalar(nslopes_row[:], slopes_row[:], -1.0, None, ALU.mult).then_inc(iotas, 1)
            g.tensor_scalar(nslopes_col[:], slopes_col[:], -1.0, None, ALU.mult).then_inc(iotas, 1)
            pool.wait_ge(in_rows0, 32)
            for b in range(B):
                pool.wait_ge(xn_done, TB * (b + 1))
                xs = X[:, TB * b:TB * b + TB, :]
                g.tensor_tensor(xs, xs, bo_row.unsqueeze(1).to_broadcast([P, TB, H]), ALU.add)\
                    .then_inc(bias_added, 1)
            def sort_rows(n, topk):
                pool.wait_ge(slots_done, n + 1)
                pool.wait_ge(zeroed, 16 * NZ)
                for t in range(T):
                    for k in range(topk):
                        g.indirect_dma_start(sorted_x[n], bass.IndirectOffsetOnAxis(ap=slot[:, k, t:t + 1], axis=0),
                                             rows_all[:, t, 0:(H, ROW)[n]], None).then_inc(scattered[n], 16)

            sort_rows(0, 2)
            for s in range(4):
                pool.wait_ge(y_stored[s], 16 * ((NT0 + 3 - s) // 4))
            for i in range(2 * T):
                t, k = divmod(i, 2)
                g.indirect_dma_start(bufs0[6][:, i, :], None, sorted_y,
                                     bass.IndirectOffsetOnAxis(ap=slot[:, k, t:t + 1], axis=0))\
                    .then_inc(gathered[i], 16)
            wait_filled(pool, ("ed", 0, NT0 - 1))
            g.memset(part(R4, 4096, T * 8 * 48), 0.0).then_inc(masks_made, 1)
            pool.wait_ge(decays, 1)
            g.affine_select(out=DT, in_=DT, compare_op=ALU.is_ge, fill=0.0, base=0,
                            pattern=[[0, NH], [1, P]], channel_multiplier=-1).then_inc(masks_made, 1)
            for pr in range(2):
                wait_filled(pool, ("sd", 1, pr))
            g.memset(part(R4, 12032, 4 * P), 0.0).then_inc(masks_made, 1)

            def add_bias(b):
                xs = X[:, TB * b:TB * b + TB, :]
                g.tensor_tensor(xs, xs, bout_row.unsqueeze(1).to_broadcast([P, TB, H]), ALU.add)\
                    .then_inc(bias_added, 1)

            for n, (c, b, m) in enumerate(CHUNKS):
                if c == 0:
                    wait_drained(pool, ("q1", b, m))
                if n >= 2:
                    wait_filled(pool, ("sc", n - 2, 1))
                q = QT1[:, m, tok(TB * b + c)]
                g.tensor_tensor(QB[:, n % 2, :].rearrange("p (j i) -> p j i", j=HP),
                                q.unsqueeze(1).to_broadcast([P, HP, P]),
                                block_diag[:, :, 0:1].to_broadcast([P, HP, P]), ALU.mult).then_inc(spread, 1)
                if n % NC == NC // 2:
                    if b == 0:
                        pool.wait_ge(in_rows1, 16)
                    pool.wait_ge(xn_done, 2 * T + TB * (b + 1))
                    add_bias(b)
            sort_rows(1, 1)
            for j in range(NT1):
                wait_drained(pool, ("ed", 1, j))
                pool.wait_ge(target_done, j + 1)
                g.indirect_dma_start(d["out"].rearrange("b s h -> (b s) h"),
                                     bass.IndirectOffsetOnAxis(ap=target[:, j % 8:j % 8 + 1], axis=0),
                                     bufs1[5][:, j % 4, :], None, bounds_check=B * S - 1, oob_is_err=False)\
                    .then_inc(out_sent[j % 4], 16)

        @block.scalar
        def _(act):
            s = nc.scalar
            own = [0]

            def link(ins):
                own[0] += 1
                ins.then_inc(scalar_step, 1)
                act.wait_ge(scalar_step, own[0])

            def norm_sqrt(n, b):
                act.wait_ge(moments, B * n + b + 1)
                if n == 0 and b == 0:
                    act.wait_ge(consts, 4)
                s.activation(sd[:, TB * b:TB * b + TB], mv[:, TB * b:TB * b + TB, 1], ACT.Sqrt, bias=eps[:])\
                    .then_inc(sqrt_done, 1)

            def take_xt(n, b):
                for kt in range(KT):
                    bank = wait_filled(act, ("xt", n, b, kt))
                    s.activation(XT[:, kt, S * b:S * b + S], ps[:, bank, :], ACT.Copy).then_inc(drained[bank], 1)

            def first_part(i):
                qk, b, m = proj_key(i)
                if i == 0:
                    act.wait_ge(in_bias, 16)
                bank = wait_filled(act, ("qk", i))
                if i >= 4:
                    act.wait_ge(parts_stored[i - 4], 16)
                s.activation(PC[:, i % 4, 0:S], ps[:, bank, :], ACT.Identity, bias=bias_col[:, qk, m:m + 1])\
                    .then_inc(part1_done, 1)

            def second_part(i):
                wait_drained(act, ("qk", i))
                s.activation(PC[:, i % 4, S:2 * S], RES[:, i % 2, :], ACT.Copy).then_inc(part2_done, 1)

            norm_sqrt(0, 0)
            take_xt(0, 0)
            norm_sqrt(0, 1)
            for i in range(8):
                if i == 4:
                    second_part(3)
                    take_xt(0, 1)
                first_part(i)
                if i % 4:
                    second_part(i - 1)
            second_part(7)
            for q in range(NQ):
                w = quarter_of(q)
                if "negmax" in w:
                    u = w["negmax"]
                    bank = wait_filled(act, ("nm", u))
                    if u >= 2:
                        act.wait_ge(negmax_stored[u - 2], 16)
                    s.activation(NMT[:, u % 2, :], ps[0:48, bank, 0:P // 2].bitcast(BF16), ACT.Copy)\
                        .then_inc(drained[bank], 1)
                if "score" in w:
                    u, kt = w["score"]
                    for h in range(4):
                        i = 16 * u + 4 * kt + h
                        bank = wait_filled(act, ("s", u, kt, h))
                        if i >= NPT:
                            pu, pk = divmod((i - NPT) // 4, 4)
                            if pk == 3:
                                wait_filled(act, ("pv", pu))
                            else:
                                act.wait_ge(pv_done, 3 * pu + pk + 1)
                        s.activation(PT[:, i % NPT, :], ps[:, bank, :], ACT.Exp, scale=1.0 / HD ** 0.5)\
                            .then_inc(drained[bank], 1)
                if "pv" in w and w["pv"][1] == 3:
                    u = w["pv"][0]
                    wait_filled(act, ("pv", u))
                    if u >= 2:
                        wait_filled(act, ("ct", u - 2))
                    s.activation(CT[:, u % 2, :], ps[:, 6, :], ACT.Copy).then_inc(drained[6], 1)
                    if u == UN - 1:
                        norm_sqrt(1, 0)
                if "ctxT" in w:
                    b = w["ctxT"]
                    for kt in range(KT):
                        bank = wait_filled(act, ("cx", b, kt))
                        s.activation(XT[:, kt, S * b:S * b + S], ps[:, bank, :], ACT.Copy).then_inc(drained[bank], 1)

            take_xt(1, 0)
            norm_sqrt(1, 1)
            take_xt(1, 1)

            def route_exp(n):
                lg = logits[n]
                if n == 0:
                    wait_drained(act, ("r", n))
                    s.activation(lg[:, :, 0:E], lg[:, :, 0:E], ACT.Exp)
                    s.activation(lg[:, :, E:E + 1], lg[:, :, E:E + 1], ACT.Exp, scale=-1.0).then_inc(route_exp_done, 1)
                else:
                    bank = wait_filled(act, ("r", n))
                    s.activation(lg[:, :, 0:E], ps[:, bank, 0:16 * T].rearrange("p (t e) -> p t e", t=T)[:, :, 0:E],
                                 ACT.Exp, scale=-1.0).then_inc(drained[bank], 1)

            route_exp(0)
            def shared_silus(c):
                for m in range(MS):
                    if (c, m) == (1, 3):
                        norm_sqrt(2, 0)
                    rows = min(P, IS0 - P * m)
                    i = MS * c + m
                    bank = wait_filled(act, ("sg", c, m))
                    if i >= 2:
                        wait_drained(act, ("su", (i - 2) // MS, (i - 2) % MS))
                    s.activation(SSG[0:rows, i % 2, :], ps[0:rows, bank, :], ACT.Silu).then_inc(drained[bank], 1)

            def expert_tiles(n, nt, hw, bufs):
                xst, sg, ht, out = bufs[1], bufs[2], bufs[4], bufs[5]
                def take_rows(i):
                    bank = wait_filled(act, ("ex", n, i))
                    s.activation(xst[:, i % 2, :], ps[:, bank, 0:H], ACT.Copy).then_inc(drained[bank], 1)

                for i in range(nt + 3):
                    if n == 0 and i < nt:
                        take_rows(i)
                    j = i - 1
                    if 0 <= j < nt:
                        bank = wait_filled(act, ("eg", n, j))
                        if j >= 2:
                            wait_drained(act, ("eg" if n == 0 else "eu", n, j - 2))
                        ins = s.activation(sg[:, j % 2, :], ps[:, bank, 0:hw], ACT.Silu)
                        ins.then_inc(silu_done if n == 0 else drained[bank], 1)
                    if n == 1 and i < nt:
                        take_rows(i)
                    j = i - 3
                    if n == 0 and 0 <= j < nt:
                        bank = wait_filled(act, ("ed", n, j))
                        if j >= 4:
                            act.wait_ge(y_stored[j % 4], 16 * (j // 4))
                        s.activation(out[:, j % 4, :], ps[:, bank, 0:H], ACT.Copy).then_inc(drained[bank], 1)

            shared_silus(0)
            expert_tiles(0, NT0, I0, bufs0)
            act.wait_ge(iotas, 13)
            s.activation(KDEC[:], slopes_row[:], ACT.Exp, scale=back[:])
            s.activation(chunk_decay[:], nslopes_col[:], ACT.Exp, scale=float(P))
            for h in range(NH):
                ins = s.activation(DT[:, h, :], diff[:], ACT.Exp, scale=nslopes_row[:, h:h + 1])
            ins.then_inc(decays, 1)
            shared_silus(1)
            def take_qk(b, m):
                for key, dst, n in (("q1", QT1, 2), ("k1", KT1, 3)):
                    bank = wait_filled(act, (key, b, m))
                    s.activation(dst[:, m, S * b:S * b + S], ps[:, bank, :], ACT.Identity,
                                 bias=bias_col[:, n, m:m + 1]).then_inc(drained[bank], 1)

            def take_chunks(b):
                for n in range(NC * b, NC * b + NC):
                    c, _, m = CHUNKS[n]
                    bank = wait_filled(act, ("oc", n))
                    s.activation(XN[:, TB * b + c, P * m:P * m + P], ps[:, bank, 0:P], ACT.Copy)\
                        .then_inc(drained[bank], 1)

            take_xt(2, 0)
            take_qk(0, 0)
            norm_sqrt(2, 1)
            take_qk(0, 1)
            for m in range(KT):
                s.activation(QD[:, m, :], iota_i[:], ACT.Exp, scale=nslopes_col[:, m:m + 1]).then_inc(decays, 1)
            take_xt(2, 1)
            take_chunks(0)
            norm_sqrt(3, 0)
            take_qk(1, 0)
            take_qk(1, 1)
            take_xt(3, 0)
            take_chunks(1)
            norm_sqrt(3, 1)
            take_xt(3, 1)
            route_exp(1)
            expert_tiles(1, NT1, I1, bufs1)

        @block.vector
        def _(dve):
            v = nc.vector
            own = [0]

            def step(ins):
                own[0] += 1
                ins.then_inc(vector_step, 1)
                return own[0]

            def link(ins):
                dve.wait_ge(vector_step, step(ins))

            def add_output(b, key):
                bank = wait_filled(dve, key)
                t = TB * b + 2 * key[2]
                xs = X[:, t:t + 2, :]
                v.tensor_tensor(xs, ps[:, bank, :].rearrange("p (t h) -> p t h", t=2), xs, ALU.add)\
                    .then_inc(drained[bank], 1)

            def normalise(n, b, keys=()):
                take_moments(n, b, keys)
                scale_rows(n, b)

            def take_moments(n, b, keys=(), add=False):
                for t in range(TB * b, TB * b + TB):
                    if n == 0:
                        dve.wait_ge(in_x[t // 2], 16)
                    elif t % 2 == 0 and keys:
                        if add:
                            add_output(b, keys[t % TB // 2])
                        wait_drained(dve, keys[t % TB // 2])
                    k = step(v.bn_stats(stats[:, t, :], X[:, t, :]))
                dve.wait_ge(vector_step, k)
                for t in range(TB * b, TB * b + TB):
                    k = v.bn_aggr(mv[:, t, :], stats[:, t, :])
                    if t < TB * b + TB - 1:
                        step(k)
                k.then_inc(moments, 1)

            def scale_rows(n, b):
                dve.wait_ge(sqrt_done, B * n + b + 1)
                link(v.reciprocal(rstd[:, TB * b:TB * b + TB], sd[:, TB * b:TB * b + TB]))
                for t in range(TB * b, TB * b + TB):
                    v.tensor_scalar(XN[:, t, :], X[:, t, :], mv[:, t, 0:1], rstd[:, t:t + 1],
                                    ALU.subtract, ALU.mult).then_inc(xn_done, 1)

            def remainder(i):
                qk, b, m = proj_key(i)
                dve.wait_ge(part1_done, i + 1)
                if i >= 2:
                    dve.wait_ge(part3_done, i - 1)
                bank, _ = uses.at["qk", i]
                v.scalar_tensor_tensor(RES[:, i % 2, :], ps[:, bank, :], bias_col[:, qk, m:m + 1],
                                       PC[:, i % 4, 0:S], ALU.add, ALU.subtract).then_inc(drained[bank], 1)

            def take_v(b, pr):
                bank = wait_filled(dve, ("v", b, pr))
                if (b, pr) == (0, 0):
                    dve.wait_ge(in_rows0, 32)
                    dve.wait_ge(consts, 5)
                t = TB * b + 2 * pr
                v.tensor_tensor(VA[:, t:t + 2, 0:NH * (HD + 1)].rearrange("p t (h e) -> p t h e", h=NH)[:, :, :, 0:HD],
                                ps[:, bank, :].rearrange("p (t h e) -> p t h e", t=2, h=NH),
                                bv_row.rearrange("p (h e) -> p h e", h=NH).unsqueeze(1).to_broadcast([P, 2, NH, HD]),
                                ALU.add).then_inc(drained[bank], 1)

            for b in range(B):
                normalise(0, b)
            dve.wait_ge(in_bias, 16)
            for i in range(4):
                remainder(i)
            for b in range(B):
                for pr in range(2):
                    take_v(b, pr)
            for i in range(4, EARLY):
                remainder(i)
            for q in range(NQ):
                w = quarter_of(q)
                if "max" in w:
                    u, qt = w["max"]
                    for h in range(4):
                        bank = wait_filled(dve, ("mx", u, qt, h))
                        v.reduce_max(MX[:, u, h, qt:qt + 1], ps[:, bank, :], AX.X).then_inc(drained[bank], 1)
                if "remainder" in w:
                    remainder(w["remainder"])
                if "max" in w and qt == 3:
                    mx = MX[:, u, :, :].rearrange("p h q -> p (h q)")
                    nm = NM[:, u % 2, :]
                    wait_drained(dve, ("mx", u, 3, 3))
                    if u >= 2:
                        wait_filled(dve, ("nm", u - 2))
                    link(v.tensor_scalar(nm[:, 0:16], mx, -1.0, None, ALU.mult))
                    link(v.scalar_tensor_tensor(nres[:], mx, -1.0, nm[:, 0:16], ALU.mult, ALU.subtract))
                    link(v.tensor_copy(nm[:, 16:32], nres[:]))
                    v.tensor_tensor(nm[:, 32:48], nres[:], nm[:, 16:32], ALU.subtract).then_inc(negmax_done, 1)
                if "norm" in w:
                    u = w["norm"]
                    b, g = divmod(u, 4)
                    bank = wait_filled(dve, ("ct", u))
                    if u:
                        wait_drained(dve, ("ct", u - 1))
                    sums = ps[:, bank, :].rearrange("p (t h e) -> p t h e", t=TB, h=4)
                    rd = RD[:].rearrange("p (t h) -> p t h", t=TB).unsqueeze(3)
                    link(v.reciprocal(rd, sums[:, :, :, HD:HD + 1]))
                    v.tensor_tensor(XN[:, TB * b:TB * b + TB, 64 * g:64 * g + 64].rearrange("p t (h e) -> p t h e", h=4),
                                    sums[:, :, :, 0:HD], rd.to_broadcast([P, TB, 4, HD]), ALU.mult)\
                        .then_inc(drained[bank], 1)
                    if u == UN - 1:
                        scale_rows(1, 0)
                if q == 4 * UN + 2:
                    take_moments(1, 0, [("o", 0, pr) for pr in range(2)])
                if "wo" in w and w["wo"] == 0:
                    dve.wait_ge(bias_added, 2)
                    for pr in range(2):
                        add_output(0, ("o", 0, pr))

            def route(n, topk):
                nt = (NT0, NT1)[n]
                region, at = ((W, 0), (R4, small1))[n]
                at += T * (E + 1)

                def small(*shape, dt=F32):
                    nonlocal at
                    w = 1
                    for x in shape:
                        w *= x
                    out = part(region, at, *shape, dt=dt)
                    at += w
                    return out

                lg = logits[n]
                bc = lambda a: a.unsqueeze(2).to_broadcast([P, T, E])
                row = lambda a: a[:].unsqueeze(1).to_broadcast([P, T, E])
                prob, eq, rest = small(T, E), small(T, E), small(T, E)
                one = [small(T, E) for _ in range(topk)]
                top = [small(T) for _ in range(2)]
                low, tmp = small(T), small(T)
                chosen = small(T + 1, E, dt=BF16)
                pos, cnt, tiles, ends, base = small(T, E), small(E, E), small(E), small(E), small(E)
                own_of = small(nt, E)
                own_f = small(nt)
                slot_f = small(T)

                link(v.memset(chosen[:, T:T + 1, :], 0.0))
                bank = wait_filled(dve, ("r", n))
                raw = ps[:, bank, 0:16 * T].rearrange("p (t e) -> p t e", t=T)
                if n == 0:
                    v.tensor_copy(lg[:, :, E:E + 1], raw[:, :, E:E + 1])
                    link(v.reduce_max(tmp, raw[:, :, 0:E], AX.X))
                    v.tensor_tensor(lg[:, :, 0:E], raw[:, :, 0:E], bc(tmp), ALU.subtract).then_inc(drained[bank], 1)
                    dve.wait_ge(route_exp_done, 1)
                else:
                    wait_drained(dve, ("r", n))
                if n == 0:
                    link(v.reduce_sum(tmp, lg[:, :, 0:E], AX.X))
                    link(v.reciprocal(low, tmp))
                    link(v.tensor_tensor(prob, lg[:, :, 0:E], bc(low), ALU.mult))
                    link(v.tensor_scalar(gate[:].unsqueeze(2), lg[:, :, E:E + 1], 1.0, None, ALU.add))
                    link(v.reciprocal(gate[:], gate[:]))
                else:
                    link(v.tensor_scalar(prob, lg[:, :, 0:E], 1.0, None, ALU.add))
                    link(v.reciprocal(prob, prob))
                dve.wait_ge(iotas, 13)
                at_hand = prob
                for k in range(topk):
                    link(v.reduce_max(top[k], at_hand, AX.X))
                    link(v.tensor_tensor(eq, at_hand, bc(top[k]), ALU.is_equal))
                    link(v.scalar_tensor_tensor(eq, eq, -64.0, row(iota_e), ALU.mult, ALU.add))
                    link(v.tensor_reduce(low, eq, AX.X, ALU.min))
                    if topk == 1:
                        v.tensor_tensor(chosen[:, 0:T, :], eq, bc(low), ALU.is_equal).then_inc(counted, 1)
                    link(v.tensor_tensor(one[k], eq, bc(low), ALU.is_equal))
                    if k + 1 < topk:
                        link(v.scalar_tensor_tensor(rest, one[k], -2.0, prob, ALU.mult, ALU.add))
                        at_hand = rest
                if topk == 2:
                    v.tensor_tensor(chosen[:, 0:T, :], one[0], one[1], ALU.add).then_inc(counted, 1)
                    link(v.tensor_tensor(tmp, top[0], top[1], ALU.add))
                    link(v.reciprocal(low, tmp))
                    for k in range(2):
                        link(v.tensor_tensor(weight[k][:], top[k], low, ALU.mult))
                else:
                    link(v.tensor_copy(rows_all[:, :, 2 * H:2 * H + 1], top[0].unsqueeze(2)))
                chosen_of[n] = chosen
                bank = wait_filled(dve, ("rank", n))
                rank = ps[:, bank, 0:T * E].rearrange("p (t e) -> p t e", t=T)
                total = ps[:, bank, T * E:T * E + E]
                link(v.tensor_tensor(cnt, total.unsqueeze(2).to_broadcast([P, E, E]),
                                     steps[:].unsqueeze(1).to_broadcast([P, E, E]), ALU.is_gt))
                link(v.reduce_sum(tiles, cnt, AX.X))
                link(v.tensor_tensor(cnt, below[:], tiles.unsqueeze(1).to_broadcast([P, E, E]), ALU.mult))
                link(v.reduce_sum(base, cnt, AX.X))
                v.tensor_tensor(pos, rank, base.unsqueeze(1).to_broadcast([P, T, E]), ALU.add)\
                    .then_inc(drained[bank], 1)
                wait_drained(dve, ("rank", n))
                for k in range(topk):
                    link(v.tensor_tensor(eq, one[k], pos, ALU.mult))
                    link(v.reduce_sum(slot_f, eq, AX.X))
                    ins = v.tensor_copy(slot[:, k, :], slot_f)
                    if k + 1 < topk:
                        link(ins)
                ins.then_inc(slots_done, 1)
                if n == 1:
                    v.tensor_tensor(first_of, slot_f.unsqueeze(2).to_broadcast([P, T, P]),
                                    iota_i[:].unsqueeze(1).to_broadcast([P, T, P]), ALU.is_equal)\
                        .then_inc(first_found, 1)
                link(v.tensor_tensor(cnt, upto[:], tiles.unsqueeze(1).to_broadcast([P, E, E]), ALU.mult))
                link(v.reduce_sum(ends, cnt, AX.X))
                link(v.tensor_tensor(own_of[0:1], iota_j[0:1, 0:nt].unsqueeze(2).to_broadcast([1, nt, E]),
                                     ends[0:1].unsqueeze(1).to_broadcast([1, nt, E]), ALU.is_ge))
                link(v.reduce_sum(own_f[0:1], own_of[0:1], AX.X))
                link(v.tensor_scalar(own_f[0:1], own_f[0:1], float(E - 1), None, ALU.min))
                v.tensor_copy(owner[n][:], own_f[0:1]).then_inc(owners_done, 1)

            def expert_tiles(n, nt, hw, bufs):
                rows, sg, hh, ht, out = bufs[0], bufs[2], bufs[3], bufs[4], bufs[5]
                for i in range(nt + 3):
                    j = i - 1
                    if 0 <= j < nt:
                        if n == 0:
                            bank = wait_filled(dve, ("eg", n, j))
                            dve.wait_ge(silu_done, j + 1)
                            up = ps[:, bank, hw:2 * hw]
                        else:
                            bank = wait_filled(dve, ("eu", n, j))
                            wait_drained(dve, ("eg", n, j))
                            up = ps[:, bank, 0:hw]
                        v.tensor_tensor(hh[:, j % 2, 0:hw], up, sg[:, j % 2, 0:hw], ALU.mult).then_inc(drained[bank], 1)
                    j = i - 2
                    if 0 <= j < nt:
                        bank = wait_filled(dve, ("eh", n, j))
                        w = max(hw, H)
                        v.tensor_copy(ht[:, j % 2, 0:w], ps[:, bank, 0:w]).then_inc(drained[bank], 1)
                    j = i - 3
                    if n == 1 and 0 <= j < nt:
                        dve.wait_ge(sorted_loaded[1][j % 8], 16 * (j // 8 + 1))
                        if j >= 4:
                            dve.wait_ge(out_sent[j % 4], 16 * (j // 4))
                        row = rows[:, j % 8, :]
                        v.tensor_copy(target[:, j % 8:j % 8 + 1], row[:, ROW - 1:ROW]).then_inc(target_done, 1)
                        bank = wait_filled(dve, ("ed", n, j))
                        v.scalar_tensor_tensor(out[:, j % 4, :], ps[:, bank, 0:H], row[:, 2 * H:2 * H + 1],
                                               row[:, H:2 * H], ALU.mult, ALU.add).then_inc(drained[bank], 1)

            def combine(b):
                for i in range(2 * TB * b, 2 * TB * (b + 1)):
                    t, k = divmod(i, 2)
                    dve.wait_ge(gathered[i], 16)
                    if k:
                        dve.wait_ge(added, i)
                    v.scalar_tensor_tensor(X[:, t, :], bufs0[6][:, i, :], weight[k][:, t:t + 1], X[:, t, :],
                                           ALU.mult, ALU.add).then_inc(added, 1)
                dve.wait_ge(added, 2 * TB * (b + 1))

            take_moments(1, 1, [("o", 1, pr) for pr in range(2)], add=True)
            scale_rows(1, 1)
            route(0, 2)
            def shared_expert(c):
                for m in range(MS):
                    if (c, m) == (1, 3):
                        combine(0)
                        normalise(2, 0)
                    rows = min(P, IS0 - P * m)
                    bank = wait_filled(dve, ("su", c, m))
                    wait_drained(dve, ("sg", c, m))
                    v.tensor_tensor(HS[0:rows, m, :], ps[0:rows, bank, :], SSG[0:rows, (MS * c + m) % 2, :],
                                    ALU.mult).then_inc(drained[bank], 1)
                for pr in range(2):
                    bank = wait_filled(dve, ("sd", c, pr))
                    for e in range(2):
                        t = TB * c + 2 * pr + e
                        ins = v.scalar_tensor_tensor(X[:, t, :], ps[:, bank, H * e:H * e + H], gate[:, t:t + 1],
                                                     X[:, t, :], ALU.mult, ALU.add)
                    ins.then_inc(drained[bank], 1)
            shared_expert(0)
            expert_tiles(0, NT0, I0, bufs0)
            shared_expert(1)
            wait_drained(dve, ("sd", 1, 1))
            combine(1)
            normalise(2, 1)

            dve.wait_ge(in_bkv1, 16)
            dve.wait_ge(masks_made, 1)
            dve.wait_ge(decays, 1)
            for b in range(B):
                for t in range(TB * b, TB * b + TB):
                    bank = wait_filled(dve, ("kv", t))
                    kd = KD1[:, t, :]
                    link(v.tensor_tensor(kd, ps[:, bank, 0:H], bkv_row[:, 0:H], ALU.add))
                    k3 = kd.rearrange("p (h e) -> p h e", h=NH)
                    v.tensor_tensor(k3, k3, KDEC[:].unsqueeze(2).to_broadcast([P, NH, HD]), ALU.mult)\
                        .then_inc(kdec_done, 1)
                    vp = VP[:, t, :].rearrange("p (a e) -> p a e", a=8)
                    for e in range(2):
                        ins = v.tensor_tensor(vp[:, :, 32 * e:32 * e + HD],
                                              ps[:, bank, H:2 * H].rearrange("p (a e f) -> p a e f", a=8, e=2)[:, :, e, :],
                                              bkv_row[:, H:2 * H].rearrange("p (a e f) -> p a e f", a=8, e=2)[:, :, e, :],
                                              ALU.add)
                    ins.then_inc(drained[bank], 1)
                for n in range(NC * b, NC * b + NC + 1):
                    if n < NC * b + NC:
                        c, _, m = CHUNKS[n]
                        if n == 0:
                            dve.wait_ge(masks_made, 3)
                            dve.wait_ge(decays, 3)
                        wait_drained(dve, ("q1", b, m))
                        if n >= 2:
                            wait_filled(dve, ("oc", n - 2))
                        v.tensor_tensor(QDEC[:, n % 2, :], QT1[:, m, tok(TB * b + c)], QD[:, m, :], ALU.mult)\
                            .then_inc(qdec_done, 1)
                        for hf in range(2):
                            bank = wait_filled(dve, ("sc", n, hf))
                            v.tensor_tensor(PD[:, n % 2, 512 * hf:512 * hf + 512].rearrange("p (h i) -> p h i", h=4),
                                            ps[:, bank, :].rearrange("p (h i) -> p h i", h=4),
                                            DT[:, 8 * m + 4 * hf:8 * m + 4 * hf + 4, :], ALU.mult)\
                                .then_inc(drained[bank], 1)
                    if n > NC * b and CHUNKS[n - 1][0] < TB - 1:
                        c, _, m = CHUNKS[n - 1]
                        bank = wait_filled(dve, ("st", n - 1))
                        state = ST[:, 2 * b + m, :]
                        v.tensor_tensor(TMP[:, n % 2, :], ps[:, bank, 0:P],
                                        block_diag[:].rearrange("p j e -> p (j e)"), ALU.mult)\
                            .then_inc(drained[bank], 1)
                        wait_drained(dve, ("st", n - 1))
                        v.scalar_tensor_tensor(state, state, chunk_decay[:, m:m + 1], TMP[:, n % 2, :],
                                               ALU.mult, ALU.add).then_inc(state_done, 1)
                dve.wait_ge(bias_added, 3 + b)
                take_moments(3, b, [("op", b, pr) for pr in range(2)], add=True)
                scale_rows(3, b)

            route(1, 1)
            expert_tiles(1, NT1, I1, bufs1)

        @block.tensor
        def _(pe):
            t_ = nc.tensor

            def transposes(n, b):
                for kt in range(KT):
                    bank = wait_free(pe, ("xt", n, b, kt))
                    for t in range(TB):
                        if kt == 0:
                            pe.wait_ge(xn_done, T * n + TB * b + t + 1)
                        ins = t_.transpose(ps[:, bank, tok(t)], XN[:, TB * b + t, P * kt:P * kt + P], identity[:])
                    ins.then_inc(filled[bank], 1)

            def product(out, pairs, **kw):
                for n, (lhsT, rhs) in enumerate(pairs):
                    ins = t_.matmul(out, lhsT, rhs, start=n == 0, stop=n == len(pairs) - 1, **kw)
                return ins

            def w0(n, cols):
                w = part(W, 512 * n, KT, H)
                return [w[:, kt, cols] for kt in range(KT)]

            def project(i):
                qk, b, m = proj_key(i)
                pe.wait_ge(in_w[qk], 16)
                bank = wait_free(pe, ("qk", i))
                product(ps[:, bank, :], [(w, XT[:, kt, S * b:S * b + S]) for kt, w in
                                         enumerate(w0(qk, slice(P * m, P * m + P)))]).then_inc(filled[bank], 1)

            def token_products(key, b, pr, src, w):
                bank = wait_free(pe, key)
                for e in range(2):
                    t = TB * b + 2 * pr + e
                    ins = product(ps[:, bank, H * e:H * e + H], [(src[:, kt, tok(t)], w[kt]) for kt in range(KT)])
                ins.then_inc(filled[bank], 1)

            pe.wait_ge(consts, 2)
            for i in range(WARM):
                t_.matmul(ps[:, 7, 0:P], identity_bf[:], identity_bf[:], start=True, stop=True)
            transposes(0, 0)
            for kt in range(KT):
                wait_drained(pe, ("xt", 0, 0, kt))
            for i in range(4):
                project(i)
            transposes(0, 1)
            pe.wait_ge(in_w[2], 16)
            for b in range(B):
                if b:
                    for kt in range(KT):
                        wait_drained(pe, ("xt", 0, 1, kt))
                for pr in range(2):
                    token_products(("v", b, pr), b, pr, XT, w0(2, slice(0, H)))
            for i in range(4, EARLY):
                project(i)
            def maxima(u, qt, heads):
                b, g = divmod(u, 4)
                for h in heads:
                    bank = wait_free(pe, ("mx", u, qt, h))
                    t_.matmul(ps[:, bank, :], QP[b][0:KR, 4 * g + h, tok(qt)], KP[b][0:KR, 4 * g + h, :],
                              start=True, stop=True).then_inc(filled[bank], 1)

            for q in range(NQ):
                w = quarter_of(q)
                if "max" in w:
                    u, qt = w["max"]
                    b, g = divmod(u, 4)
                    if qt == 0 and g % 2 == 0:
                        pe.wait_ge(packed[2 * b + g // 2], 96)
                    maxima(u, qt, range(4) if "score" not in w else (0,))
                if "project" in w:
                    project(w["project"])
                if "negmax" in w:
                    u = w["negmax"]
                    bank = wait_free(pe, ("nm", u))
                    pe.wait_ge(negmax_done, u + 1)
                    t_.transpose(ps[0:48, bank, 0:P // 2].bitcast(BF16), NM[:, u % 2, :], identity_bf[:])\
                        .then_inc(filled[bank], 1)
                if "score" in w:
                    u, kt = w["score"]
                    b, g = divmod(u, 4)
                    if u == 0 and kt == 0:
                        pe.wait_ge(consts, 7)
                    if kt == 0:
                        pe.wait_ge(negmax_loaded[u], 16)
                    for h in range(4):
                        if h and "max" in w:
                            maxima(*w["max"], (h,))
                        bank = wait_free(pe, ("s", u, kt, h))
                        t_.matmul(ps[:, bank, :], KP[b][0:KR + 3, 4 * g + h, tok(kt)], QP[b][0:KR + 3, 4 * g + h, :],
                                  start=True, stop=True).then_inc(filled[bank], 1)
                if "pv" in w:
                    u, kt = w["pv"]
                    b, g = divmod(u, 4)
                    if kt == 0:
                        wait_free(pe, ("pv", u))
                        for pr in range(2):
                            wait_drained(pe, ("v", b, pr))
                    for h in (2, 3):
                        wait_drained(pe, ("s", u, kt, h))
                    for h in range(4):
                        col = (HD + 1) * (4 * g + h)
                        ins = t_.matmul(ps[32 * h:32 * h + 32, 6, :], VA[:, TB * b + kt, col:col + 32],
                                        PT[:, (16 * u + 4 * kt + h) % NPT, :], start=kt == 0, stop=kt == 3)
                    ins.then_inc(filled[6] if kt == 3 else pv_done, 1)
                if "norm" in w:
                    u = w["norm"]
                    bank = wait_free(pe, ("ct", u))
                    wait_drained(pe, ("pv", u))
                    for t in range(TB):
                        ins = t_.transpose(ps[:, bank, tok(t)], CT[:, u % 2, tok(t)], identity[:])
                    ins.then_inc(filled[bank], 1)
                if "ctxT" in w:
                    b = w["ctxT"]
                    wait_drained(pe, ("ct", 4 * b + 3))
                    for kt in range(KT):
                        bank = wait_free(pe, ("cx", b, kt))
                        for t in range(TB):
                            ins = t_.transpose(ps[:, bank, tok(t)], XN[:, TB * b + t, P * kt:P * kt + P], identity[:])
                        ins.then_inc(filled[bank], 1)
                    if b == 1:
                        transposes(1, 0)
                if "wo" in w:
                    b = w["wo"]
                    pe.wait_ge(in_w[3], 16)
                    for kt in range(KT):
                        wait_drained(pe, ("cx", b, kt))
                    for pr in range(2):
                        token_products(("o", b, pr), b, pr, XT, w0(3, slice(0, H)))

            def router(n, b, rw, nl):
                bank, _ = uses.at["r", n]
                if b == 0:
                    wait_free(pe, ("r", n))
                for kt in range(KT):
                    wait_drained(pe, ("xt", 2 * n + 1, b, kt))
                for t in range(TB * b, TB * b + TB):
                    ins = product(ps[:, bank, 16 * t:16 * t + nl],
                                  [(XT[:, kt, tok(t)], rw[:, kt, :]) for kt in range(KT)])
                if b == B - 1:
                    ins.then_inc(filled[bank], 1)

            def ranks(n):
                pe.wait_ge(counted, n + 1)
                bank = wait_free(pe, ("rank", n))
                chosen = chosen_of[n]
                out = ps[:, bank, 0:(T + 1) * E]
                t_.matmul(out, before_bf[:], chosen, start=True, stop=True)
                for t in range(T):
                    ins = t_.matmul(ps[:, bank, E * (t + 1):(T + 1) * E].rearrange("p (t e) -> p t e", e=E), ones_bf[:],
                                    chosen[:, t:t + 1, :].to_broadcast([P, T - t, E]),
                                    start=False, stop=True, skip_group_check=True)
                ins.then_inc(filled[bank], 1)

            def expert_tiles(n, nt, hw, bufs, ups, downs):
                rows, xst, hh, ht = bufs[0], bufs[1], bufs[3], bufs[4]
                expert = {}
                def turn_rows(i):
                    if True:
                        ring = (4, 8)[n]
                        if (n, i) != (1, 0):
                            pe.wait_ge(sorted_loaded[n][i % ring], 16 * (i // ring + 1))
                        bank = wait_free(pe, ("ex", n, i))
                        for kt in range(KT):
                            if (n, i) == (1, 0):
                                pe.wait_ge(first_found, 1)
                                ins = product(ps[:, bank, tok(kt)], [(XN[:, t, tok(kt)], first_of[:, t, :])
                                                                     for t in range(T)])
                            else:
                                ins = t_.transpose(ps[:, bank, tok(kt)], rows[:, i % ring, tok(kt)], identity[:])
                        ins.then_inc(filled[bank], 1)
                for i in range(nt + 3):
                    if n == 0 and i < nt:
                        turn_rows(i)
                    j = i - 1
                    if 0 <= j < nt:
                        if j == 0:
                            pe.wait_ge(owners_done, n + 1)
                        expert[j] = t_.value_load(owner[n][0:1, j:j + 1], min_val=0, max_val=E - 1)
                        wait_drained(pe, ("ex", n, j))
                        for key, w in ups:
                            bank = wait_free(pe, (key, n, j))
                            product(ps[:, bank, 0:w.shape[3]],
                                    [(xst[:, j % 2, tok(kt)], w[:, kt, bass.ds(expert[j], 1), :]) for kt in range(KT)])\
                                .then_inc(filled[bank], 1)
                    if n == 1 and i < nt:
                        turn_rows(i)
                    j = i - 2
                    if 0 <= j < nt:
                        wait_drained(pe, (ups[-1][0], n, j))
                        bank = wait_free(pe, ("eh", n, j))
                        if n == 0:
                            starts = (0, hw - P)
                        else:
                            starts = range(0, hw, P)
                        for k, c in enumerate(starts):
                            ins = t_.transpose(ps[:, bank, tok(k)], hh[:, j % 2, c:c + P], identity[:])
                        ins.then_inc(filled[bank], 1)
                    j = i - 3
                    if 0 <= j < nt:
                        wait_drained(pe, ("eh", n, j))
                        bank = wait_free(pe, ("ed", n, j))
                        product(ps[:, bank, 0:H], [(ht[:, j % 2, tok(k)], w[:, bass.ds(expert[j], 1), :])
                                                   for k, w in enumerate(downs)]).then_inc(filled[bank], 1)

            def shared_expert(c, ms=range(MS)):
                for m in ms:
                    rows = min(P, IS0 - P * m)
                    for key, w in (("sg", sg0), ("su", su0)):
                        bank = wait_free(pe, (key, c, m))
                        product(ps[0:rows, bank, :], [(w[:, kt, P * m:P * m + rows], XT[:, kt, S * c:S * c + S])
                                                      for kt in range(KT)]).then_inc(filled[bank], 1)
                    if c == 0 and m == 2:
                        ranks(0)
                if ms[-1] < MS - 1:
                    return
                for m in range(MS):
                    wait_drained(pe, ("su", c, m))
                for pr in range(2):
                    bank = wait_free(pe, ("sd", c, pr))
                    for e in range(2):
                        t = 2 * pr + e
                        ins = product(ps[:, bank, H * e:H * e + H],
                                      [(HS[0:min(P, IS0 - P * m), m, tok(t)], sd0[0:min(P, IS0 - P * m), m, :])
                                       for m in range(MS)])
                    ins.then_inc(filled[bank], 1)
            pe.wait_ge(in_small, 16 * 4)
            router(0, 0, r0w, E + 1)
            pe.wait_ge(in_ffn0, 16 * FFN0_PIECES)
            shared_expert(0, range(2))
            transposes(1, 1)
            router(0, 1, r0w, E + 1)
            shared_expert(0, range(2, MS))
            expert_tiles(0, NT0, I0, bufs0, [("eg", gu0)], [da0, db0])
            shared_expert(1)

            wqkv = part(W, 0, KT, 3 * H)
            states = {}

            def chunk_out(n):
                c, b, m = CHUNKS[n]
                t = TB * b + c
                pe.wait_ge(qdec_done, n + 1)
                if c:
                    pe.wait_ge(state_done, states[c - 1, b, m])
                for hf in range(2):
                    wait_drained(pe, ("sc", n, hf))
                bank = wait_free(pe, ("oc", n))
                t_.matmul(ps[:, bank, 0:P], ST[:, 2 * b + m, :], QDEC[:, n % 2, :], start=True, stop=True)
                for k in range(HP):
                    pair, e = divmod(k, 2)
                    col = 48 * (4 * m + pair) + 16 * e
                    ins = t_.matmul(ps[32 * pair:32 * pair + 32, bank, 0:P], VP[:, t, col:col + 32],
                                    PD[:, n % 2, P * k:P * k + P], start=False, stop=True, skip_group_check=True)
                ins.then_inc(filled[bank], 1)
                if c < TB - 1:
                    bank = wait_free(pe, ("st", n))
                    states[c, b, m] = len(states) + 1
                    pe.wait_ge(kdec_done, t + 1)
                    vv = VP[:, t, 192 * m:192 * m + 192].rearrange("p (a s) -> p a s", a=4)
                    vv = vv[:, :, 0:48].rearrange("p a (e f) -> p a e f", e=3)[:, :, 0:3:2, :]
                    t_.matmul(ps[:, bank, 0:P], KD1[:, t, P * m:P * m + P], vv, start=True, stop=True)\
                        .then_inc(filled[bank], 1)

            transposes(2, 0)
            pe.wait_ge(in_w1, 32)
            for b in range(B):
                for kt in range(KT):
                    wait_drained(pe, ("xt", 2, b, kt))
                for m in range(KT):
                    for n, key in enumerate(("q1", "k1")):
                        bank = wait_free(pe, (key, b, m))
                        product(ps[:, bank, :], [(wqkv[:, kt, H * n + P * m:H * n + P * m + P], XT[:, kt, S * b:S * b + S])
                                                 for kt in range(KT)]).then_inc(filled[bank], 1)
                for t in range(TB * b, TB * b + TB):
                    bank = wait_free(pe, ("kv", t))
                    product(ps[:, bank, :], [(XT[:, kt, tok(t)], wqkv[:, kt, H:3 * H]) for kt in range(KT)])\
                        .then_inc(filled[bank], 1)
                if b == 0:
                    transposes(2, 1)
                else:
                    transposes(3, 0)
                    router(1, 0, r1w, E)
                pe.wait_ge(masks_made, 3)
                for m in range(KT):
                    wait_drained(pe, ("k1", b, m))
                for t in range(TB * b, TB * b + TB):
                    wait_drained(pe, ("kv", t))
                for n in range(NC * b, NC * b + NC + 1):
                    if n < NC * b + NC:
                        c, _, m = CHUNKS[n]
                        pe.wait_ge(spread, n + 1)
                        for hf in range(2):
                            bank = wait_free(pe, ("sc", n, hf))
                            t_.matmul(ps[:, bank, :], KT1[:, m, tok(TB * b + c)], QB[:, n % 2, 512 * hf:512 * hf + 512],
                                      start=True, stop=True).then_inc(filled[bank], 1)
                    if n > NC * b:
                        chunk_out(n - 1)
                for n in range(NC * b, NC * b + NC):
                    wait_drained(pe, ("oc", n))
                wout = part(W, 1536, KT, H)
                for pr in range(2):
                    bank = wait_free(pe, ("op", b, pr))
                    for e in range(2):
                        t = TB * b + 2 * pr + e
                        ins = product(ps[:, bank, H * e:H * e + H],
                                      [(XN[:, t, P * kt:P * kt + P], wout[:, kt, :]) for kt in range(KT)])
                    ins.then_inc(filled[bank], 1)

            transposes(3, 1)
            router(1, 1, r1w, E)
            ranks(1)
            pe.wait_ge(in_ffn1, 16 * 16)
            pe.wait_ge(in_gate1, 16)
            expert_tiles(1, NT1, I1, bufs1, [("eg", gate1), ("eu", up1)],
                         [down1[:, k, :, :] for k in range(I1 // P)])


def kernel(**inputs):
    import numpy as np
    import concourse.bacc as bacc
    from concourse.bass_utils import run_bass_kernel_spmd as launch

    a = {k: np.asarray(v) for k, v in inputs.items()}

    def rows(w):
        return np.ascontiguousarray(w.reshape(w.shape[0] // 128, 128, -1).swapaxes(0, 1))

    def col(v):
        return v.reshape(2, 128).T

    def by_expert(w):
        return np.ascontiguousarray(w.reshape(w.shape[0], -1, 128, w.shape[2]).transpose(2, 1, 0, 3))

    by_dim = np.arange(256).reshape(2, 8, 16).transpose(0, 2, 1).reshape(256)
    wq, wk, wv, wo = (a["L0_attn_" + n].T for n in ("Wq", "Wk", "Wv", "Wo"))
    wd = a["L0_ffn_w_down"]
    tail = np.zeros((8, 128, 256), wd.dtype)
    tail[:, 80:] = wd[:, 128:]
    shared_down = np.zeros((768, 256), wd.dtype)
    shared_down[:704] = a["L0_ffn_sw_down"]
    arrays = {
        "x": a["L0_attn_x"],
        "w0": np.stack([rows(w).reshape(128, 512) for w in (wq[:, by_dim], wk[:, by_dim], wv, wo)]),
        "bias_col": np.stack([col(a["L0_attn_bq"][by_dim]), col(a["L0_attn_bk"][by_dim]), col(a["L1_attn_bqkv"][:256]),
                              col(a["L1_attn_bqkv"][256:512])], axis=1),
        "bv0": a["L0_attn_bv"],
        "bo0": a["L0_attn_bo"],
        "slopes": a["L1_attn_slopes"],
        "slopes_col": col(np.repeat(a["L1_attn_slopes"], 16)),
        "r0w": rows(np.concatenate([a["L0_ffn_gate_w"].T, a["L0_ffn_shared_gate_w"]], axis=1)),
        "r1w": rows(a["L1_ffn_router_w"]),
        "ffn0": np.concatenate([w.reshape(128, -1) for w in (
            by_expert(np.concatenate([a["L0_ffn_w_gate"], a["L0_ffn_w_up"]], axis=2)),
            wd[:, :128].swapaxes(0, 1), tail.swapaxes(0, 1), rows(a["L0_ffn_sw_gate"]), rows(a["L0_ffn_sw_up"]),
            rows(shared_down))], axis=1),
        "wqkv1": rows(a["L1_attn_Wqkv"]).reshape(128, 1536),
        "wout1": rows(a["L1_attn_Wout"]).reshape(128, 512),
        "bkv1": a["L1_attn_bqkv"][256:],
        "bout1": a["L1_attn_bout"],
        "gate1": by_expert(a["L1_ffn_gate_w"]),
        "ffn1": np.concatenate([by_expert(a["L1_ffn_up_w"]).reshape(128, -1),
                                by_expert(a["L1_ffn_down_w"]).reshape(128, -1)], axis=1),
    }
    arrays = {k: np.ascontiguousarray(v) for k, v in arrays.items()}
    nc = bacc.Bacc("TRN2", target_bir_lowering=False, num_devices=1)
    d = {k: nc.dram_tensor("in_" + k, v.shape, mybir.dt.from_np(v.dtype), kind="ExternalInput").ap()
         for k, v in arrays.items()}
    d["out"] = nc.dram_tensor("out", [2, 512, 256], mybir.dt.float32, kind="ExternalOutput").ap()
    two_layers(nc, d)
    r = launch(nc, [{"in_" + k: v for k, v in arrays.items()}], core_ids=[0])
    return r.results[0]["out"]
```

```python
from contextlib import ExitStack

import concourse.bass as bass
from concourse import mybir

F32 = mybir.dt.float32
BF16 = mybir.dt.bfloat16
I32 = mybir.dt.int32
ALU = mybir.AluOpType
ACT = mybir.ActivationFunctionType
AX = mybir.AxisListType

P = 128
B, S, H = 2, 512, 256
TB = S // P
T = B * TB
KT = H // P
NH, HD = 16, 16
HP = P // HD
E = 8
I0, IS0, I1 = 176, 704, 512
GU0 = 2 * I0
MS = 6
FULL = IS0 // P
NT0 = 2 * B * S // P + E - 1
NT1 = B * S // P + E - 1
FFN0_PIECES = 20
NZ = (NT0 + 1) // 2 + (NT1 + 1) // 2
KR = 6 * HD
UN = 8
LAG = 7
NPT = 8


TWO_ONES = 1.0 + 0x3F80 / 2 ** 23


NORMS = [(n, b, pr) for n in range(4) for b in range(B) for pr in ((0, 1) if (n % 2, b) == (1, 1) else (None,))]


def norm_at(n, b, pr=None):
    first = TB * b + 2 * (pr or 0)
    return NORMS.index((n, b, pr)), range(first, first + (TB if pr is None else 2))


def up_key(c, m):
    return "su" if m < FULL else "sg", c, m


class Uses:

    def __init__(self):
        self.at, self.count, self.turn = {}, [0] * 8, 0

    def next7(self, keep):
        bank = self.turn
        self.turn = (bank + 1) % (7 if keep else 8)
        return bank

    def add(self, key, bank=None):
        if bank is None:
            bank = self.turn
            self.turn = (self.turn + 1) % 8
        self.at[key] = (bank, self.count[bank])
        self.count[bank] += 1


def quarter_of(q):
    out = {}
    if q < 4 * UN:
        out["max"] = divmod(q, 4)
    if q % 4 == 0 and 0 < q <= 4 * UN:
        out["negmax"] = q // 4 - 1
    if 0 <= q < 2:
        out["v"] = 1, q
    if 2 <= q < 6:
        out["project"] = q + 2
    if 3 <= q < 7:
        out["split"] = q + 1
    if 0 <= q - LAG < 4 * UN:
        out["score"] = divmod(q - LAG, 4)
    if 0 <= q - LAG - 1 < 4 * UN:
        out["pv"] = divmod(q - LAG - 1, 4)
    if 0 <= q - LAG - 2 < 4 * UN and (q - LAG - 2) % 4 == 3:
        out["norm"] = (q - LAG - 2) // 4
    if 0 <= q - LAG - 3 < 4 * UN and (q - LAG - 3) % 16 == 15:
        out["ctxT"] = (q - LAG - 3) // 16
    if 0 <= q - LAG - 4 < 4 * UN and (q - LAG - 4) % 16 == 15:
        out["wo"] = (q - LAG - 4) // 16
    return out


NQ = 4 * UN + LAG + 4
WARM = 36
BULK = 10
TAIL_BANKS = (3, 4, 5, 0, 1, 2)
SHARED_BANKS = (0, 1, 2, 3, 4, 5, 7)


def proj_key(i):
    return i % 2, i // 4, i // 2 % 2


def plan():
    u = Uses()
    for kt in range(KT):
        u.add(("xt", 0, 0, kt))
    for i in range(4):
        u.add(("qk", i))
    for kt in range(KT):
        u.add(("xt", 0, 1, kt))
    for pr in range(2):
        u.add(("v", 0, pr), 4 + pr)
    for q in range(NQ):
        w = quarter_of(q)
        if "max" in w:
            for h in range(4):
                u.add(("mx", *w["max"], h), (4 * q + h) % 3)
        if "v" in w:
            u.add(("v", *w["v"]), 6 + q)
        if "project" in w:
            u.add(("qk", w["project"]), w["project"])
        if "negmax" in w:
            u.add(("nm", w["negmax"]), 7)
        if "score" in w:
            for h in range(4):
                u.add(("s", *w["score"], h), 3 + (4 * q + h) % 3 if q < 4 * UN + 1 else TAIL_BANKS[(4 * q + h) % 6])
        if "pv" in w and w["pv"][1] == 0:
            u.add(("pv", w["pv"][0]), 6)
        if "norm" in w:
            u.add(("ct", w["norm"]), 7)
        if "ctxT" in w:
            for kt in range(KT):
                u.add(("cx", w["ctxT"], kt), 7 if w["ctxT"] == 0 or kt == 0 else 0)
            if w["ctxT"] == 1:
                for kt in range(KT):
                    u.add(("xt", 1, 0, kt), 4 + kt)
        if "wo" in w:
            for pr in range(2):
                u.add(("o", w["wo"], pr), 7 if w["wo"] == 0 or pr == 0 else 0)
    u.add(("r", 0), 6)

    def shared(c, ms=range(MS)):
        for m in ms:
            for i, key in enumerate(("sg", "su") if m < FULL else ("sg",)):
                u.add((key, c, m), SHARED_BANKS[(2 * m + i) % 7] if c == 0 else None)
        if ms[-1] == MS - 1:
            for pr in range(2):
                u.add(("sd", c, pr))

    shared(0, range(1))
    for pr in range(2):
        u.add(("xp", 1, 1, pr), (5, 7)[pr])
    u.add(("rank", 0), 6)
    shared(0, range(1, MS))
    for i in range(NT0 + 3):
        if i < NT0:
            u.add(("ex", 0, i))
        if 0 <= i - 1 < NT0:
            u.add(("eg", 0, i - 1))
        if 0 <= i - 2 < NT0:
            u.add(("eh", 0, i - 2))
        if 0 <= i - 3 < NT0:
            u.add(("ed", 0, i - 3))
    shared(1)
    for kt in range(KT):
        u.add(("xt", 2, 0, kt))
    for b in range(B):
        for m in range(KT):
            u.add(("q1", b, m))
            u.add(("k1", b, m))
        for t in range(TB):
            u.add(("kv", TB * b + t))
        if b == 0:
            for kt in range(KT):
                u.add(("xt", 2, 1, kt))
        else:
            u.add(("r", 1), 7)
            u.turn = 0
            for kt in range(KT):
                u.add(("xt", 3, 0, kt))
        first = NC * b
        for n in range(first, first + NC + 1):
            if n < first + NC:
                for hf in range(2):
                    u.add(("sc", n, hf), u.next7(b))
            if n > first:
                u.add(("oc", n - 1), u.next7(b))
                if CHUNKS[n - 1][0] < TB - 1:
                    u.add(("st", n - 1), u.next7(b))
        for pr in range(2):
            u.add(("op", b, pr), u.next7(b))
    for pr in range(2):
        u.add(("xp", 3, 1, pr), u.next7(1))
    u.turn = 0
    u.add(("rank", 1))
    for i in range(NT1 + 3):
        if 0 <= i - 1 < NT1:
            u.add(("eg", 1, i - 1))
            u.add(("eu", 1, i - 1))
        if i < NT1:
            u.add(("ex", 1, i))
        if 0 <= i - 2 < NT1:
            u.add(("eh", 1, i - 2))
        if 0 <= i - 3 < NT1:
            u.add(("ed", 1, i - 3))
    return u


CHUNKS = [(c, b, m) for b in range(B) for c in range(TB) for m in range(KT)]
NC = len(CHUNKS) // B


def two_layers(nc, d):
    uses = plan()
    ctx = ExitStack()
    with ctx:
        def sb(name, shape, dt=F32):
            return ctx.enter_context(nc.sbuf_tensor(name, shape, dt))

        def sem(name):
            return ctx.enter_context(nc.semaphore(name))

        def sems(name, n):
            return [sem(f"{name}{i}") for i in range(n)]

        R1 = sb("R1", [P, 16384])
        R2 = sb("R2", [P, 8192])
        R3 = sb("R3", [P, 4096])
        R4 = sb("R4", [P, 14080])
        W = sb("W", [P, 2048])
        ROW = 2 * H + 2
        rows_all = sb("rows_all", [P, T, ROW])
        XN = rows_all[:, :, 0:H]
        X = rows_all[:, :, H:2 * H]
        XT = sb("XT", [P, KT, B * S])

        def part(region, at, *shape, dt=F32):
            n = 1
            for s in shape:
                n *= s
            words = n // 2 if dt == BF16 else n
            v = region[:, at:at + words]
            if dt != F32:
                v = v.bitcast(dt)
            if len(shape) == 2:
                v = v.rearrange("p (a b) -> p a b", a=shape[0])
            elif len(shape) == 3:
                v = v.rearrange("p (a b c) -> p a b c", a=shape[0], b=shape[1])
            return v

        QP = [part(R1, 8192 * b, NH, S, dt=BF16) for b in range(B)]
        KP = [part(R1, 8192 * b + 4096, NH, S, dt=BF16) for b in range(B)]
        up1 = part(R1, 0, KT, E, I1)
        down1 = part(R1, 8192, I1 // P, E, H)
        gate1 = part(R2, 0, KT, E, I1)
        VS = NH * (HD + 1) + HD
        VA = part(R2, 0, T, VS)
        PT = part(R2, 2304, NPT, S)
        CT = part(R2, 6400, 2, S)
        bv_row = part(R2, 7424, H)
        bo_row = part(R2, 7680, H)
        PC = part(R3, 0, 4, 3 * S, dt=BF16)
        RES = part(R3, 3072, 2, S)
        HS = part(R3, 0, MS, S)
        SSG = part(R3, 3072, 2, S)
        PD = part(R3, 0, 2, HP * P)
        first_of = part(R3, 0, T, P)
        QB = part(R3, 2048, 2, HP * P)
        gu0 = part(R4, 0, KT, E, GU0)
        da0 = part(R4, 5632, E, H)
        db0 = part(R4, 7680, E, H)
        sg0 = part(R4, 9728, KT, P * FULL)
        su0 = part(R4, 11008, KT, P * FULL)
        st0 = part(R4, 12288, KT, P)
        sd0 = part(R4, 12544, MS, H)
        QT1 = part(R4, 0, KT, B * S)
        KT1 = part(R4, 2048, KT, B * S)
        VP = part(R4, 4096, T, 8 * 48)
        DT = part(R4, 7168, NH, P)
        bkv_row = part(R4, 9216, 2 * H)
        KD1 = part(R4, 9728, T, H)
        QDEC = part(R4, 11776, 2, P)
        ST = part(R4, 12032, 4, P)
        TMP = part(R4, 12544, 2, P)
        bout_row = part(R4, 12800, H)
        QD = part(R4, 13056, KT, P)

        def tile_buffers(region, n, hw):
            at, out = 0, []
            for shape in ((4, H) if n == 0 else (8, ROW), (2, H), (2, hw), (2, hw), (2, max(hw, H)), (4, H),
                          (16 if n == 0 else 0, H)):
                out.append(part(region, at, *shape) if shape[0] else None)
                at += shape[0] * shape[1]
            return out + [at]

        *bufs0, small0 = tile_buffers(R2, 0, I0)
        *bufs1, small1 = tile_buffers(R4, 1, I1)

        logits = [part(W, 0, T, E + 1), part(R4, small1, T, E + 1)]
        chosen_of = {}

        identity = sb("identity", [P, P])
        identity_bf = sb("identity_bf", [P, P], BF16)
        ones_bf = sb("ones_bf", [P, P], BF16)
        before_bf = sb("before_bf", [P, P], BF16)
        diff = sb("diff", [P, P])
        iota_i = sb("iota_i", [P, P])
        block_diag = sb("block_diag", [P, HP, HD])
        iota_e = sb("iota_e", [P, E])
        steps = sb("steps", [P, E])
        upto = sb("upto", [P, E, E])
        below = sb("below", [P, E, E])
        iota_j = sb("iota_j", [P, NT0])
        back = sb("back", [P, 1])
        unread = sb("unread", [P, 1])
        blank = sb("blank", [P, ROW])
        slopes_row = sb("slopes_row", [P, NH])
        nslopes_row = sb("nslopes_row", [P, NH])
        slopes_col = sb("slopes_col", [P, KT])
        nslopes_col = sb("nslopes_col", [P, KT])
        KDEC = sb("KDEC", [P, NH])
        chunk_decay = sb("chunk_decay", [P, KT])
        bias_col = sb("bias_col", [P, 4, KT])
        r0w = sb("r0w", [P, KT, E + 1])
        r1w = sb("r1w", [P, KT, E])
        stats = sb("stats", [P, T, 6])
        mv = sb("mv", [P, T, 2])
        sd = sb("sd", [P, T])
        rstd = sb("rstd", [P, T])
        eps = sb("eps", [P, 1])
        MX = sb("MX", [P, UN, 4, TB])
        nres = sb("nres", [P, 16])
        NM = sb("NM", [P, 2, 48], BF16)
        NMT = sb("NMT", [48, 2, P], BF16)
        RD = sb("RD", [P, 16])
        gate = sb("gate", [P, T])
        weight = [sb(f"weight{k}", [P, T]) for k in range(2)]
        slot = sb("slot", [P, 2, T], I32)
        target = sb("target", [P, 8], I32)
        owner = [sb(f"owner{n}", [1, nt], I32) for n, nt in enumerate((NT0, NT1))]
        ps = ctx.enter_context(nc.psum_tensor("ps", [P, 8, 512], F32))

        sorted_x = [nc.dram_tensor(f"sorted_x{n}", [(nt + 1) // 2 * 2 * P, (H, ROW)[n]], F32, kind="Internal").ap()
                    for n, nt in enumerate((NT0, NT1))]
        sorted_y = nc.dram_tensor("sorted_y", [NT0 * P, H], F32, kind="Internal").ap()

        filled, drained = sems("filled", 8), sems("drained", 8)
        in_x = sems("in_x", 2 * B)
        in_w = sems("in_proj", 4)
        in_small = sem("in_small")
        in_bias = sem("in_bias")
        in_rows0 = sem("in_rows0")
        in_ffn0 = sem("in_ffn0")
        in_w1 = sem("in_w1")
        in_rows1 = sem("in_rows1")
        in_ffn1 = sem("in_ffn1")
        in_gate1 = sem("in_gate1")
        zeroed = sem("zeroed")
        consts = sem("consts")
        iotas = sem("iotas")
        vector_step = sem("vector_step")
        scalar_step = sem("scalar_step")
        pool_step = sem("pool_step")
        moments = sem("moments")
        sqrt_done = sem("sqrt_done")
        xn_done = sem("xn_done")
        part1_done = sem("part1_done")
        part2_done = sem("part2_done")
        part3_done = sem("part3_done")
        parts_moved = sems("parts_moved", 8)
        bias_added = sem("bias_added")
        negmax_done = sem("negmax_done")
        negmax_loaded = sems("negmax_loaded", UN)
        pv_done = sem("pv_done")
        silu_done = sem("silu_done")
        route_exp_done = sem("route_exp_done")
        counted = sem("counted")
        slots_done = sem("slots_done")
        owners_done = sem("owners_done")
        scattered = sems("scattered", 2)
        sorted_loaded = [sems(f"sorted_loaded{n}_", (4, 8)[n]) for n in range(2)]
        y_stored = sems("y_stored", 4)
        gathered = sems("gathered", 16)
        added = sem("added")
        target_done = sem("target_done")
        decays = sem("decays")
        masks_made = sem("masks_made")
        spread = sem("spread")
        qdec_done = sem("qdec_done")
        kdec_done = sem("kdec_done")
        state_done = sem("state_done")
        out_sent = sems("out_sent", 4)
        in_bkv1 = sem("in_bkv1")
        first_found = sem("first_found")
        hidden_zero = sem("hidden_zero")
        tail_silu = sem("tail_silu")

        def wait_free(pe, key):
            bank, n = uses.at[key]
            if n:
                pe.wait_ge(drained[bank], n)
            return bank

        def wait_filled(eng, key):
            bank, n = uses.at[key]
            eng.wait_ge(filled[bank], n + 1)
            return bank

        def wait_drained(eng, key):
            bank, n = uses.at[key]
            eng.wait_ge(drained[bank], n + 1)

        def tok(t, n=1):
            return slice(P * t, P * (t + n))

        block = ctx.enter_context(nc.Block())

        @block.sync
        def _(sp):
            for b in range(B):
                for half in range(2):
                    t = TB * b + 2 * half
                    sp.dma_start(X[:, t:t + 2, :], d["x"][b, 2 * P * half:2 * P * half + 2 * P, :]
                                 .rearrange("(t p) h -> p t h", p=P)).then_inc(in_x[2 * b + half], 16)
                if b == 0:
                    for n in range(2):
                        sp.dma_start(part(W, 512 * n, 512), d["w0"][n]).then_inc(in_w[n], 16)
                    sp.dma_start(bias_col[:], d["bias_col"]).then_inc(in_bias, 16)
            sp.dma_start(part(W, 1024, 512), d["w0"][2]).then_inc(in_w[2], 16)
            sp.dma_start(bv_row, d["bv0"].partition_broadcast(P)).then_inc(in_rows0, 16)
            sp.dma_start(bo_row, d["bo0"].partition_broadcast(P)).then_inc(in_rows0, 16)
            sp.dma_start(part(W, 1536, 512), d["w0"][3]).then_inc(in_w[3], 16)
            sp.dma_start(slopes_row[:], d["slopes"].partition_broadcast(P)).then_inc(in_small, 16)
            sp.dma_start(slopes_col[:], d["slopes_col"]).then_inc(in_small, 16)
            sp.dma_start(r0w[:], d["r0w"]).then_inc(in_small, 16)
            sp.dma_start(r1w[:], d["r1w"]).then_inc(in_small, 16)

            groups = (((0, 1, 2), (3, 4), (5,)), ((0, 3, 5), (1, 4), (2,)))

            def move_part(i, k):
                qk, b, m = proj_key(i)
                sp.wait_ge((part1_done, part2_done, part3_done)[k], i + 1)
                for g in groups[qk][k]:
                    sp.dma_start((QP, KP)[qk][b][HD * g:HD * g + HD, HP * m:HP * m + HP, :],
                                 PC[:, i % 4, S * k:S * k + S]).then_inc(parts_moved[i], 16)

            def move_pair(i):
                for j, k in ((i, 0), (i + 1, 0), (i, 1), (i, 2), (i + 1, 1), (i + 1, 2)):
                    move_part(j, k)

            move_pair(0)
            move_pair(2)
            sp.wait_ge(consts, 3)

            def ffn0_weights(c):
                cols = slice(704 * c, 704 * c + 704)
                sp.dma_start(R4[:, cols], d["ffn0"][:, cols]).then_inc(in_ffn0, 16)

            def zero_rows(n, j):
                sp.dma_start(sorted_x[n][P * j:P * j + 2 * P, :].rearrange("(j p) h -> p j h", p=P),
                             blank[:, 0:(H, ROW)[n]].unsqueeze(1).to_broadcast([P, 2, (H, ROW)[n]]))\
                    .then_inc(zeroed, 16)

            pieces = [(ffn0_weights, (c,)) for c in range(FFN0_PIECES)]
            pieces += [(zero_rows, (n, j)) for n, nt in enumerate((NT0, NT1)) for j in range(0, nt, 2)]
            per_quarter = -(-len(pieces) // (4 * UN - BULK))
            for q in range(NQ):
                w = quarter_of(q)
                if "max" in w and q >= BULK:
                    wait_filled(sp, ("mx", *w["max"], 3))
                    for piece, args in pieces[per_quarter * (q - BULK):per_quarter * (q - BULK + 1)]:
                        piece(*args)
                if "negmax" in w:
                    u = w["negmax"]
                    wait_drained(sp, ("nm", u))
                    b, g = divmod(u, 4)
                    for a in range(3):
                        sp.dma_start(QP[b][KR + a:KR + a + 1, 4 * g:4 * g + 4, :]
                                     .rearrange("a h (q t) -> a (h q) t", t=P),
                                     NMT[16 * a:16 * a + 16, u % 2, :]).then_inc(negmax_loaded[u], 16)
                    if u < 2:
                        move_pair(4 + 2 * u)
            for b in range(B):
                for pr in range(2):
                    wait_filled(sp, ("o", b, pr))

            def ffn1_weights(c):
                cols = slice(1024 * c, 1024 * c + 1024)
                sp.dma_start(R1[:, cols], d["ffn1"][:, cols]).then_inc(in_ffn1, 16)

            def expert_tiles(n, nt, k, bufs):
                rows, out = bufs[0], bufs[5]
                ring = (4, 8)[n]

                def load(j):
                    if j >= ring:
                        (wait_filled if n == 0 else wait_drained)(sp, (("ex", "ed")[n], n, j - ring))
                    sp.dma_start(rows[:, j % ring, :], sorted_x[n][P * j:P * j + P, :])\
                        .then_inc(sorted_loaded[n][j % ring], 16)

                sp.wait_ge(scattered[n], 16 * T * k)
                for j in (0, 1, 2, 3) if n == 0 else (1, 2, 3, 0):
                    load(j)
                for i in range(nt + 3):
                    if i + 4 < nt:
                        load(i + 4)
                    if n == 0 and i < 16:
                        ffn1_weights(i)
                    j = i - 3
                    if n == 0 and j >= 0:
                        wait_drained(sp, ("ed", n, j))
                        sp.dma_start(sorted_y[P * j:P * j + P, :], out[:, j % 4, :])\
                            .then_inc(y_stored[j % 4], 16)

            sp.wait_ge(owners_done, 1)
            sp.dma_start(part(W, 0, 1536), d["wqkv1"]).then_inc(in_w1, 16)
            sp.dma_start(part(W, 1536, 512), d["wout1"]).then_inc(in_w1, 16)
            expert_tiles(0, NT0, 2, bufs0)
            sp.dma_start(bkv_row, d["bkv1"].partition_broadcast(P)).then_inc(in_bkv1, 16)
            sp.wait_ge(added, 2 * T)
            sp.dma_start(bout_row, d["bout1"].partition_broadcast(P)).then_inc(in_rows1, 16)
            sp.dma_start(gate1, d["gate1"]).then_inc(in_gate1, 16)
            expert_tiles(1, NT1, 1, bufs1)
            for i in range(4):
                sp.wait_ge(out_sent[i], 16 * len(range(i, NT1, 4)))

        @block.gpsimd
        def _(pool):
            g = nc.gpsimd
            own = [0]

            def link(ins):
                own[0] += 1
                ins.then_inc(pool_step, 1)
                pool.wait_ge(pool_step, own[0])

            link(g.memset(identity[:], 0.0))
            g.affine_select(out=identity[:], in_=identity[:], compare_op=ALU.not_equal, fill=1.0, base=0,
                            pattern=[[-1, P]], channel_multiplier=1).then_inc(consts, 1)
            pool.wait_ge(consts, 1)
            g.tensor_copy(identity_bf[:], identity[:]).then_inc(consts, 1)
            link(g.memset(blank[:], 0.0))
            g.memset(blank[:, ROW - 1:ROW], 4.0 * B * S).then_inc(consts, 1)
            g.memset(eps[:], 1e-5).then_inc(consts, 1)
            g.memset(part(R2, 0, T * VS), 1.0).then_inc(consts, 1)

            def third_part(i):
                pool.wait_ge(part2_done, i + 1)
                if i >= 4:
                    pool.wait_ge(parts_moved[i - 4], 96)
                g.tensor_tensor(PC[:, i % 4, 2 * S:3 * S], RES[:, i % 2, :], PC[:, i % 4, S:2 * S],
                                ALU.subtract).then_inc(part3_done, 1)

            for i in range(4):
                third_part(i)
            pool.wait_ge(part3_done, 4)
            for b in range(B):
                g.memset(KP[b][KR:KR + 3, :, :].rearrange("p h t -> p (h t)").bitcast(F32), TWO_ONES)\
                    .then_inc(consts, 1)
                pool.wait_ge(consts, 6 + b)
            link(g.memset(ones_bf[:], 1.0))
            g.affine_select(out=before_bf[:], in_=ones_bf[:], compare_op=ALU.is_gt, fill=0.0, base=0,
                            pattern=[[1, P]], channel_multiplier=-1).then_inc(iotas, 1)
            g.iota(iota_e[:], pattern=[[1, E]], base=0, channel_multiplier=0,
                   allow_small_or_imprecise_dtypes=True).then_inc(iotas, 1)
            g.iota(steps[:], pattern=[[P, E]], base=0, channel_multiplier=0,
                   allow_small_or_imprecise_dtypes=True).then_inc(iotas, 1)
            g.iota(iota_j[:], pattern=[[1, NT0]], base=0, channel_multiplier=0,
                   allow_small_or_imprecise_dtypes=True).then_inc(iotas, 1)
            link(g.memset(upto[:], 1.0))
            g.affine_select(out=upto[:], in_=upto[:], compare_op=ALU.is_ge, fill=0.0, base=0,
                            pattern=[[1, E], [-1, E]], channel_multiplier=0).then_inc(iotas, 1)
            link(g.memset(below[:], float(P)))
            g.affine_select(out=below[:], in_=below[:], compare_op=ALU.is_gt, fill=0.0, base=0,
                            pattern=[[1, E], [-1, E]], channel_multiplier=0).then_inc(iotas, 1)
            g.iota(rows_all[:, :, ROW - 1:ROW], pattern=[[P, T], [0, 1]], base=0, channel_multiplier=1,
                   allow_small_or_imprecise_dtypes=True).then_inc(iotas, 1)
            g.iota(iota_i[:], pattern=[[1, P]], base=0, channel_multiplier=0,
                   allow_small_or_imprecise_dtypes=True).then_inc(iotas, 1)
            g.iota(back[:], pattern=[[0, 1]], base=-P, channel_multiplier=1,
                   allow_small_or_imprecise_dtypes=True).then_inc(iotas, 1)
            link(g.iota(diff[:], pattern=[[1, P]], base=0, channel_multiplier=-1,
                        allow_small_or_imprecise_dtypes=True))
            g.tensor_scalar(diff[:], diff[:], 0.0, None, ALU.max).then_inc(iotas, 1)
            link(g.memset(block_diag[:], 1.0))
            link(g.affine_select(out=block_diag[:], in_=block_diag[:], compare_op=ALU.is_ge, fill=0.0, base=0,
                                 pattern=[[-HD, HP], [0, HD]], channel_multiplier=1))
            g.affine_select(out=block_diag[:], in_=block_diag[:], compare_op=ALU.is_ge, fill=0.0, base=HD - 1,
                            pattern=[[HD, HP], [0, HD]], channel_multiplier=-1).then_inc(iotas, 1)
            pool.wait_ge(in_small, 16 * 4)
            g.tensor_scalar(nslopes_row[:], slopes_row[:], -1.0, None, ALU.mult).then_inc(iotas, 1)
            g.tensor_scalar(nslopes_col[:], slopes_col[:], -1.0, None, ALU.mult).then_inc(iotas, 1)
            for i in range(4, 8):
                third_part(i)
            pool.wait_ge(in_rows0, 32)
            for b in range(B):
                pool.wait_ge(xn_done, TB * (b + 1))
                xs = X[:, TB * b:TB * b + TB, :]
                g.tensor_tensor(xs, xs, bo_row.unsqueeze(1).to_broadcast([P, TB, H]), ALU.add)\
                    .then_inc(bias_added, 1)
            pool.wait_ge(parts_moved[7], 96)
            g.memset(HS[0:P // 2, MS - 1, :], 0.0).then_inc(hidden_zero, 1)

            def sort_rows(n, topk):
                pool.wait_ge(slots_done, n + 1)
                pool.wait_ge(zeroed, 16 * NZ)
                for t in range(T):
                    for k in range(topk):
                        g.indirect_dma_start(sorted_x[n], bass.IndirectOffsetOnAxis(ap=slot[:, k, t:t + 1], axis=0),
                                             rows_all[:, t, 0:(H, ROW)[n]], None).then_inc(scattered[n], 16)

            sort_rows(0, 2)
            for s in range(4):
                pool.wait_ge(y_stored[s], 16 * ((NT0 + 3 - s) // 4))
            for i in range(2 * T):
                t, k = divmod(i, 2)
                g.indirect_dma_start(bufs0[6][:, i, :], None, sorted_y,
                                     bass.IndirectOffsetOnAxis(ap=slot[:, k, t:t + 1], axis=0))\
                    .then_inc(gathered[i], 16)
            wait_filled(pool, ("ed", 0, NT0 - 1))
            g.memset(part(R4, 4096, T * 8 * 48), 0.0).then_inc(masks_made, 1)
            pool.wait_ge(decays, 1)
            g.affine_select(out=DT, in_=DT, compare_op=ALU.is_ge, fill=0.0, base=0,
                            pattern=[[0, NH], [1, P]], channel_multiplier=-1).then_inc(masks_made, 1)
            for pr in range(2):
                wait_filled(pool, ("sd", 1, pr))
            g.memset(part(R4, 12032, 4 * P), 0.0).then_inc(masks_made, 1)

            def add_bias(b):
                xs = X[:, TB * b:TB * b + TB, :]
                g.tensor_tensor(xs, xs, bout_row.unsqueeze(1).to_broadcast([P, TB, H]), ALU.add)\
                    .then_inc(bias_added, 1)

            for n, (c, b, m) in enumerate(CHUNKS):
                if c == 0:
                    wait_drained(pool, ("q1", b, m))
                if n >= 2:
                    wait_filled(pool, ("sc", n - 2, 1))
                q = QT1[:, m, tok(TB * b + c)]
                g.tensor_tensor(QB[:, n % 2, :].rearrange("p (j i) -> p j i", j=HP),
                                q.unsqueeze(1).to_broadcast([P, HP, P]),
                                block_diag[:, :, 0:1].to_broadcast([P, HP, P]), ALU.mult).then_inc(spread, 1)
                if n % NC == NC // 2:
                    if b == 0:
                        pool.wait_ge(in_rows1, 16)
                    pool.wait_ge(xn_done, 2 * T + TB * (b + 1))
                    add_bias(b)
            sort_rows(1, 1)
            for j in range(NT1):
                wait_drained(pool, ("ed", 1, j))
                pool.wait_ge(target_done, j + 1)
                g.indirect_dma_start(d["out"].rearrange("b s h -> (b s) h"),
                                     bass.IndirectOffsetOnAxis(ap=target[:, j % 8:j % 8 + 1], axis=0),
                                     bufs1[5][:, j % 4, :], None, bounds_check=B * S - 1, oob_is_err=False)\
                    .then_inc(out_sent[j % 4], 16)

        @block.scalar
        def _(act):
            s = nc.scalar
            own = [0]

            def link(ins):
                own[0] += 1
                ins.then_inc(scalar_step, 1)
                act.wait_ge(scalar_step, own[0])

            def norm_sqrt(n, b, pr=None):
                at, tiles = norm_at(n, b, pr)
                act.wait_ge(moments, at + 1)
                if at == 0:
                    act.wait_ge(consts, 4)
                ts = slice(tiles[0], tiles[-1] + 1)
                s.activation(sd[:, ts], mv[:, ts, 1], ACT.Sqrt, bias=eps[:]).then_inc(sqrt_done, 1)

            def take_pair(n, b, pr):
                bank = wait_filled(act, ("xp", n, b, pr))
                cols = slice(S * b + 2 * P * pr, S * b + 2 * P * pr + 2 * P)
                s.activation(XT[:, :, cols], ps[:, bank, :].rearrange("p (k t) -> p k t", k=KT), ACT.Copy)\
                    .then_inc(drained[bank], 1)

            def take_xt(n, b):
                for kt in range(KT):
                    bank = wait_filled(act, ("xt", n, b, kt))
                    s.activation(XT[:, kt, S * b:S * b + S], ps[:, bank, :], ACT.Copy).then_inc(drained[bank], 1)

            def first_part(i):
                qk, b, m = proj_key(i)
                if i == 0:
                    act.wait_ge(in_bias, 16)
                bank = wait_filled(act, ("qk", i))
                if i >= 4:
                    act.wait_ge(parts_moved[i - 4], 96)
                s.activation(PC[:, i % 4, 0:S], ps[:, bank, :], ACT.Identity, bias=bias_col[:, qk, m:m + 1])\
                    .then_inc(part1_done, 1)

            def second_part(i):
                wait_drained(act, ("qk", i))
                s.activation(PC[:, i % 4, S:2 * S], RES[:, i % 2, :], ACT.Copy).then_inc(part2_done, 1)

            norm_sqrt(0, 0)
            take_xt(0, 0)
            norm_sqrt(0, 1)
            for i in range(4):
                first_part(i)
                if i:
                    second_part(i - 1)
            second_part(3)
            take_xt(0, 1)
            s.activation(unread[:], eps[:], ACT.Exp)
            for q in range(NQ):
                w = quarter_of(q)
                if "split" in w:
                    second_part(w["split"])
                if "project" in w:
                    first_part(w["project"])
                if "score" in w:
                    u, kt = w["score"]
                    for h in range(4):
                        i = 16 * u + 4 * kt + h
                        bank = wait_filled(act, ("s", u, kt, h))
                        if i >= NPT:
                            pu, pk = divmod((i - NPT) // 4, 4)
                            if pk == 3:
                                wait_filled(act, ("pv", pu))
                            else:
                                act.wait_ge(pv_done, 3 * pu + pk + 1)
                        s.activation(PT[:, i % NPT, :], ps[:, bank, :], ACT.Exp, scale=1.0 / HD ** 0.5)\
                            .then_inc(drained[bank], 1)
                if "negmax" in w:
                    u = w["negmax"]
                    bank = wait_filled(act, ("nm", u))
                    if u >= 2:
                        act.wait_ge(negmax_loaded[u - 2], 48)
                    s.activation(NMT[:, u % 2, :], ps[0:48, bank, 0:P // 2].bitcast(BF16), ACT.Copy)\
                        .then_inc(drained[bank], 1)
                if "pv" in w and w["pv"][1] == 3:
                    u = w["pv"][0]
                    wait_filled(act, ("pv", u))
                    if u >= 2:
                        wait_filled(act, ("ct", u - 2))
                    s.activation(CT[:, u % 2, :], ps[:, 6, :], ACT.Copy).then_inc(drained[6], 1)
                    if u == UN - 1:
                        norm_sqrt(1, 0)
                if "ctxT" in w:
                    b = w["ctxT"]
                    for kt in range(KT):
                        bank = wait_filled(act, ("cx", b, kt))
                        s.activation(XT[:, kt, S * b:S * b + S], ps[:, bank, :], ACT.Copy).then_inc(drained[bank], 1)

            take_xt(1, 0)
            for pr in range(2):
                norm_sqrt(1, 1, pr)
            for pr in range(2):
                take_pair(1, 1, pr)

            def route_exp(n):
                lg = logits[n]
                if n == 0:
                    wait_drained(act, ("r", n))
                    s.activation(lg[:, :, 0:E], lg[:, :, 0:E], ACT.Exp)
                    s.activation(lg[:, :, E:E + 1], lg[:, :, E:E + 1], ACT.Exp, scale=-1.0).then_inc(route_exp_done, 1)
                else:
                    bank = wait_filled(act, ("r", n))
                    s.activation(lg[:, :, 0:E], ps[:, bank, 0:16 * T].rearrange("p (t e) -> p t e", t=T)[:, :, 0:E],
                                 ACT.Exp, scale=-1.0).then_inc(drained[bank], 1)

            route_exp(0)
            def shared_silus(c):
                for m in range(MS):
                    if (c, m) == (1, 1):
                        norm_sqrt(2, 0)
                    i = MS * c + m
                    bank = wait_filled(act, ("sg", c, m))
                    if i >= 2:
                        wait_drained(act, up_key((i - 2) // MS, (i - 2) % MS))
                    if m < FULL:
                        s.activation(SSG[:, i % 2, :], ps[:, bank, :], ACT.Silu).then_inc(drained[bank], 1)
                    else:
                        s.activation(SSG[P // 2:P, i % 2, :], ps[0:P // 2, bank, :], ACT.Silu).then_inc(tail_silu, 1)

            def expert_tiles(n, nt, hw, bufs):
                xst, sg, ht, out = bufs[1], bufs[2], bufs[4], bufs[5]
                def take_rows(i):
                    bank = wait_filled(act, ("ex", n, i))
                    s.activation(xst[:, i % 2, :], ps[:, bank, 0:H], ACT.Copy).then_inc(drained[bank], 1)

                for i in range(nt + 3):
                    if n == 0 and i < nt:
                        take_rows(i)
                    j = i - 1
                    if 0 <= j < nt:
                        bank = wait_filled(act, ("eg", n, j))
                        if j >= 2:
                            wait_drained(act, ("eg" if n == 0 else "eu", n, j - 2))
                        ins = s.activation(sg[:, j % 2, :], ps[:, bank, 0:hw], ACT.Silu)
                        ins.then_inc(silu_done if n == 0 else drained[bank], 1)
                    if n == 1 and i < nt:
                        take_rows(i)
                    j = i - 3
                    if n == 0 and 0 <= j < nt:
                        bank = wait_filled(act, ("ed", n, j))
                        if j >= 4:
                            act.wait_ge(y_stored[j % 4], 16 * (j // 4))
                        s.activation(out[:, j % 4, :], ps[:, bank, 0:H], ACT.Copy).then_inc(drained[bank], 1)

            shared_silus(0)
            expert_tiles(0, NT0, I0, bufs0)
            act.wait_ge(iotas, 13)
            s.activation(KDEC[:], slopes_row[:], ACT.Exp, scale=back[:])
            s.activation(chunk_decay[:], nslopes_col[:], ACT.Exp, scale=float(P))
            for h in range(NH):
                ins = s.activation(DT[:, h, :], diff[:], ACT.Exp, scale=nslopes_row[:, h:h + 1])
            ins.then_inc(decays, 1)
            shared_silus(1)
            def take_qk(b, m):
                for key, dst, n in (("q1", QT1, 2), ("k1", KT1, 3)):
                    bank = wait_filled(act, (key, b, m))
                    s.activation(dst[:, m, S * b:S * b + S], ps[:, bank, :], ACT.Identity,
                                 bias=bias_col[:, n, m:m + 1]).then_inc(drained[bank], 1)

            def take_chunks(b):
                for n in range(NC * b, NC * b + NC):
                    c, _, m = CHUNKS[n]
                    bank = wait_filled(act, ("oc", n))
                    s.activation(XN[:, TB * b + c, P * m:P * m + P], ps[:, bank, 0:P], ACT.Copy)\
                        .then_inc(drained[bank], 1)

            take_xt(2, 0)
            take_qk(0, 0)
            norm_sqrt(2, 1)
            take_qk(0, 1)
            for m in range(KT):
                s.activation(QD[:, m, :], iota_i[:], ACT.Exp, scale=nslopes_col[:, m:m + 1]).then_inc(decays, 1)
            take_xt(2, 1)
            take_chunks(0)
            norm_sqrt(3, 0)
            take_qk(1, 0)
            take_qk(1, 1)
            take_xt(3, 0)
            take_chunks(1)
            for pr in range(2):
                norm_sqrt(3, 1, pr)
            for pr in range(2):
                take_pair(3, 1, pr)
            route_exp(1)
            expert_tiles(1, NT1, I1, bufs1)

        @block.vector
        def _(dve):
            v = nc.vector
            own = [0]

            def step(ins):
                own[0] += 1
                ins.then_inc(vector_step, 1)
                return own[0]

            def link(ins):
                dve.wait_ge(vector_step, step(ins))

            def add_output(b, key):
                bank = wait_filled(dve, key)
                t = TB * b + 2 * key[2]
                xs = X[:, t:t + 2, :]
                v.tensor_tensor(xs, ps[:, bank, :].rearrange("p (t h) -> p t h", t=2), xs, ALU.add)\
                    .then_inc(drained[bank], 1)

            def normalise(n, b, keys=()):
                take_moments(n, b, keys)
                scale_rows(n, b)

            def take_moments(n, b, keys=(), pr=None, add=False):
                for t in norm_at(n, b, pr)[1]:
                    if n == 0:
                        dve.wait_ge(in_x[t // 2], 16)
                    elif t % 2 == 0 and keys:
                        if add:
                            add_output(b, keys[t % TB // 2])
                        wait_drained(dve, keys[t % TB // 2])
                    k = step(v.bn_stats(stats[:, t, :], X[:, t, :]))
                dve.wait_ge(vector_step, k)
                for t in norm_at(n, b, pr)[1]:
                    if t > norm_at(n, b, pr)[1][0]:
                        step(k)
                    k = v.bn_aggr(mv[:, t, :], stats[:, t, :])
                k.then_inc(moments, 1)

            def scale_rows(n, b, pr=None):
                at, tiles = norm_at(n, b, pr)
                dve.wait_ge(sqrt_done, at + 1)
                ts = slice(tiles[0], tiles[-1] + 1)
                link(v.reciprocal(rstd[:, ts], sd[:, ts]))
                for t in tiles:
                    v.tensor_scalar(XN[:, t, :], X[:, t, :], mv[:, t, 0:1], rstd[:, t:t + 1],
                                    ALU.subtract, ALU.mult).then_inc(xn_done, 1)

            def normalise_pairs(n, key):
                for pr in range(2):
                    take_moments(n, 1, [(key, 1, pr) for pr in range(2)], pr, add=True)
                for pr in range(2):
                    scale_rows(n, 1, pr)

            def remainder(i):
                qk, b, m = proj_key(i)
                dve.wait_ge(part1_done, i + 1)
                if i >= 2:
                    dve.wait_ge(part3_done, i - 1)
                bank, _ = uses.at["qk", i]
                v.scalar_tensor_tensor(RES[:, i % 2, :], ps[:, bank, :], bias_col[:, qk, m:m + 1],
                                       PC[:, i % 4, 0:S], ALU.add, ALU.subtract).then_inc(drained[bank], 1)

            def take_v(b, pr):
                bank = wait_filled(dve, ("v", b, pr))
                if (b, pr) == (0, 0):
                    dve.wait_ge(in_rows0, 32)
                    dve.wait_ge(consts, 5)
                t = TB * b + 2 * pr
                v.tensor_tensor(VA[:, t:t + 2, 0:NH * (HD + 1)].rearrange("p t (h e) -> p t h e", h=NH)[:, :, :, 0:HD],
                                ps[:, bank, :].rearrange("p (t h e) -> p t h e", t=2, h=NH),
                                bv_row.rearrange("p (h e) -> p h e", h=NH).unsqueeze(1).to_broadcast([P, 2, NH, HD]),
                                ALU.add).then_inc(drained[bank], 1)

            for b in range(B):
                normalise(0, b)
            dve.wait_ge(in_bias, 16)
            for i in range(4):
                remainder(i)
            for pr in range(2):
                take_v(0, pr)
            for q in range(NQ):
                w = quarter_of(q)
                if "max" in w:
                    u, qt = w["max"]
                    for h in range(4):
                        bank = wait_filled(dve, ("mx", u, qt, h))
                        v.reduce_max(MX[:, u, h, qt:qt + 1], ps[:, bank, :], AX.X).then_inc(drained[bank], 1)
                if "v" in w:
                    take_v(*w["v"])
                if "split" in w:
                    remainder(w["split"])
                if "max" in w and qt == 3:
                    mx = MX[:, u, :, :].rearrange("p h q -> p (h q)")
                    nm = NM[:, u % 2, :]
                    wait_drained(dve, ("mx", u, 3, 3))
                    if u >= 2:
                        wait_filled(dve, ("nm", u - 2))
                    link(v.tensor_scalar(nm[:, 0:16], mx, -1.0, None, ALU.mult))
                    link(v.scalar_tensor_tensor(nres[:], mx, -1.0, nm[:, 0:16], ALU.mult, ALU.subtract))
                    link(v.tensor_copy(nm[:, 16:32], nres[:]))
                    v.tensor_tensor(nm[:, 32:48], nres[:], nm[:, 16:32], ALU.subtract).then_inc(negmax_done, 1)
                if "norm" in w:
                    u = w["norm"]
                    b, g = divmod(u, 4)
                    bank = wait_filled(dve, ("ct", u))
                    if u:
                        wait_drained(dve, ("ct", u - 1))
                    sums = ps[:, bank, :].rearrange("p (t h e) -> p t h e", t=TB, h=4)
                    rd = RD[:].rearrange("p (t h) -> p t h", t=TB).unsqueeze(3)
                    link(v.reciprocal(rd, sums[:, :, :, HD:HD + 1]))
                    v.tensor_tensor(XN[:, TB * b:TB * b + TB, 64 * g:64 * g + 64].rearrange("p t (h e) -> p t h e", h=4),
                                    sums[:, :, :, 0:HD], rd.to_broadcast([P, TB, 4, HD]), ALU.mult)\
                        .then_inc(drained[bank], 1)
                    if u == UN - 1:
                        scale_rows(1, 0)
                if q == 4 * UN + 2:
                    take_moments(1, 0, [("o", 0, pr) for pr in range(2)])
                if "wo" in w and w["wo"] == 0:
                    dve.wait_ge(bias_added, 2)
                    for pr in range(2):
                        add_output(0, ("o", 0, pr))

            def route(n, topk):
                nt = (NT0, NT1)[n]
                region, at = ((W, 0), (R4, small1))[n]
                at += T * (E + 1)

                def small(*shape, dt=F32):
                    nonlocal at
                    w = 1
                    for x in shape:
                        w *= x
                    out = part(region, at, *shape, dt=dt)
                    at += w
                    return out

                lg = logits[n]
                bc = lambda a: a.unsqueeze(2).to_broadcast([P, T, E])
                row = lambda a: a[:].unsqueeze(1).to_broadcast([P, T, E])
                prob, eq, rest = small(T, E), small(T, E), small(T, E)
                one = [small(T, E) for _ in range(topk)]
                top = [small(T) for _ in range(2)]
                low, tmp = small(T), small(T)
                chosen = small(T + 1, E, dt=BF16)
                pos, cnt, tiles, ends, base = small(T, E), small(E, E), small(E), small(E), small(E)
                own_of = small(nt, E)
                own_f = small(nt)
                slot_f = small(T)

                link(v.memset(chosen[:, T:T + 1, :], 0.0))
                bank = wait_filled(dve, ("r", n))
                raw = ps[:, bank, 0:16 * T].rearrange("p (t e) -> p t e", t=T)
                if n == 0:
                    v.tensor_copy(lg[:, :, E:E + 1], raw[:, :, E:E + 1])
                    link(v.reduce_max(tmp, raw[:, :, 0:E], AX.X))
                    v.tensor_tensor(lg[:, :, 0:E], raw[:, :, 0:E], bc(tmp), ALU.subtract).then_inc(drained[bank], 1)
                    dve.wait_ge(route_exp_done, 1)
                else:
                    wait_drained(dve, ("r", n))
                if n == 0:
                    link(v.reduce_sum(tmp, lg[:, :, 0:E], AX.X))
                    link(v.reciprocal(low, tmp))
                    link(v.tensor_tensor(prob, lg[:, :, 0:E], bc(low), ALU.mult))
                else:
                    link(v.tensor_scalar(prob, lg[:, :, 0:E], 1.0, None, ALU.add))
                    link(v.reciprocal(prob, prob))
                dve.wait_ge(iotas, 13)
                at_hand = prob
                for k in range(topk):
                    link(v.reduce_max(top[k], at_hand, AX.X))
                    link(v.tensor_tensor(eq, at_hand, bc(top[k]), ALU.is_equal))
                    link(v.scalar_tensor_tensor(eq, eq, -64.0, row(iota_e), ALU.mult, ALU.add))
                    link(v.tensor_reduce(low, eq, AX.X, ALU.min))
                    if topk == 1:
                        v.tensor_tensor(chosen[:, 0:T, :], eq, bc(low), ALU.is_equal).then_inc(counted, 1)
                    link(v.tensor_tensor(one[k], eq, bc(low), ALU.is_equal))
                    if k + 1 < topk:
                        link(v.scalar_tensor_tensor(rest, one[k], -2.0, prob, ALU.mult, ALU.add))
                        at_hand = rest
                if topk == 2:
                    v.tensor_tensor(chosen[:, 0:T, :], one[0], one[1], ALU.add).then_inc(counted, 1)
                    link(v.tensor_tensor(tmp, top[0], top[1], ALU.add))
                    link(v.reciprocal(low, tmp))
                    for k in range(2):
                        link(v.tensor_tensor(weight[k][:], top[k], low, ALU.mult))
                else:
                    link(v.tensor_copy(rows_all[:, :, 2 * H:2 * H + 1], top[0].unsqueeze(2)))
                chosen_of[n] = chosen
                bank = wait_filled(dve, ("rank", n))
                rank = ps[:, bank, 0:T * E].rearrange("p (t e) -> p t e", t=T)
                total = ps[:, bank, T * E:T * E + E]
                link(v.tensor_tensor(cnt, total.unsqueeze(2).to_broadcast([P, E, E]),
                                     steps[:].unsqueeze(1).to_broadcast([P, E, E]), ALU.is_gt))
                link(v.reduce_sum(tiles, cnt, AX.X))
                link(v.tensor_tensor(cnt, below[:], tiles.unsqueeze(1).to_broadcast([P, E, E]), ALU.mult))
                link(v.reduce_sum(base, cnt, AX.X))
                v.tensor_tensor(pos, rank, base.unsqueeze(1).to_broadcast([P, T, E]), ALU.add)\
                    .then_inc(drained[bank], 1)
                wait_drained(dve, ("rank", n))
                for k in range(topk):
                    link(v.tensor_tensor(eq, one[k], pos, ALU.mult))
                    link(v.reduce_sum(slot_f, eq, AX.X))
                    ins = v.tensor_copy(slot[:, k, :], slot_f)
                    if k + 1 < topk:
                        link(ins)
                ins.then_inc(slots_done, 1)
                if n == 1:
                    v.tensor_tensor(first_of, slot_f.unsqueeze(2).to_broadcast([P, T, P]),
                                    iota_i[:].unsqueeze(1).to_broadcast([P, T, P]), ALU.is_equal)\
                        .then_inc(first_found, 1)
                if n == 0:
                    link(v.tensor_scalar(gate[:].unsqueeze(2), lg[:, :, E:E + 1], 1.0, None, ALU.add))
                    link(v.reciprocal(gate[:], gate[:]))
                link(v.tensor_tensor(cnt, upto[:], tiles.unsqueeze(1).to_broadcast([P, E, E]), ALU.mult))
                link(v.reduce_sum(ends, cnt, AX.X))
                link(v.tensor_tensor(own_of[0:1], iota_j[0:1, 0:nt].unsqueeze(2).to_broadcast([1, nt, E]),
                                     ends[0:1].unsqueeze(1).to_broadcast([1, nt, E]), ALU.is_ge))
                link(v.reduce_sum(own_f[0:1], own_of[0:1], AX.X))
                link(v.tensor_scalar(own_f[0:1], own_f[0:1], float(E - 1), None, ALU.min))
                v.tensor_copy(owner[n][:], own_f[0:1]).then_inc(owners_done, 1)

            def expert_tiles(n, nt, hw, bufs):
                rows, sg, hh, ht, out = bufs[0], bufs[2], bufs[3], bufs[4], bufs[5]
                for i in range(nt + 3):
                    j = i - 1
                    if 0 <= j < nt:
                        if n == 0:
                            bank = wait_filled(dve, ("eg", n, j))
                            dve.wait_ge(silu_done, j + 1)
                            up = ps[:, bank, hw:2 * hw]
                        else:
                            bank = wait_filled(dve, ("eu", n, j))
                            wait_drained(dve, ("eg", n, j))
                            up = ps[:, bank, 0:hw]
                        v.tensor_tensor(hh[:, j % 2, 0:hw], up, sg[:, j % 2, 0:hw], ALU.mult).then_inc(drained[bank], 1)
                    j = i - 2
                    if 0 <= j < nt:
                        bank = wait_filled(dve, ("eh", n, j))
                        w = max(hw, H)
                        v.tensor_copy(ht[:, j % 2, 0:w], ps[:, bank, 0:w]).then_inc(drained[bank], 1)
                    j = i - 3
                    if n == 1 and 0 <= j < nt:
                        dve.wait_ge(sorted_loaded[1][j % 8], 16 * (j // 8 + 1))
                        if j >= 4:
                            dve.wait_ge(out_sent[j % 4], 16 * (j // 4))
                        row = rows[:, j % 8, :]
                        v.tensor_copy(target[:, j % 8:j % 8 + 1], row[:, ROW - 1:ROW]).then_inc(target_done, 1)
                        bank = wait_filled(dve, ("ed", n, j))
                        v.scalar_tensor_tensor(out[:, j % 4, :], ps[:, bank, 0:H], row[:, 2 * H:2 * H + 1],
                                               row[:, H:2 * H], ALU.mult, ALU.add).then_inc(drained[bank], 1)

            def combine(b):
                for i in range(2 * TB * b, 2 * TB * (b + 1)):
                    t, k = divmod(i, 2)
                    dve.wait_ge(gathered[i], 16)
                    if k:
                        dve.wait_ge(added, i)
                    v.scalar_tensor_tensor(X[:, t, :], bufs0[6][:, i, :], weight[k][:, t:t + 1], X[:, t, :],
                                           ALU.mult, ALU.add).then_inc(added, 1)
                dve.wait_ge(added, 2 * TB * (b + 1))

            normalise_pairs(1, "o")
            route(0, 2)
            def shared_expert(c):
                for m in range(MS):
                    if (c, m) == (1, 1):
                        combine(0)
                        take_moments(2, 0)
                    if (c, m) == (1, 1):
                        scale_rows(2, 0)
                    bank = wait_filled(dve, up_key(c, m))
                    if m < FULL:
                        wait_drained(dve, ("sg", c, m))
                    else:
                        dve.wait_ge(tail_silu, c + 1)
                    rows = slice(0, P) if m < FULL else slice(P // 2, P)
                    v.tensor_tensor(HS[rows, m, :], ps[rows, bank, :], SSG[rows, (MS * c + m) % 2, :], ALU.mult)\
                        .then_inc(drained[bank], 1)
                for pr in range(2):
                    bank = wait_filled(dve, ("sd", c, pr))
                    for e in range(2):
                        t = TB * c + 2 * pr + e
                        ins = v.scalar_tensor_tensor(X[:, t, :], ps[:, bank, H * e:H * e + H], gate[:, t:t + 1],
                                                     X[:, t, :], ALU.mult, ALU.add)
                    ins.then_inc(drained[bank], 1)
            shared_expert(0)
            expert_tiles(0, NT0, I0, bufs0)
            shared_expert(1)
            wait_drained(dve, ("sd", 1, 1))
            combine(1)
            normalise(2, 1)

            dve.wait_ge(in_bkv1, 16)
            dve.wait_ge(masks_made, 1)
            dve.wait_ge(decays, 1)
            for b in range(B):
                for t in range(TB * b, TB * b + TB):
                    bank = wait_filled(dve, ("kv", t))
                    kd = KD1[:, t, :]
                    link(v.tensor_tensor(kd, ps[:, bank, 0:H], bkv_row[:, 0:H], ALU.add))
                    k3 = kd.rearrange("p (h e) -> p h e", h=NH)
                    v.tensor_tensor(k3, k3, KDEC[:].unsqueeze(2).to_broadcast([P, NH, HD]), ALU.mult)\
                        .then_inc(kdec_done, 1)
                    vp = VP[:, t, :].rearrange("p (a e) -> p a e", a=8)
                    for e in range(2):
                        ins = v.tensor_tensor(vp[:, :, 32 * e:32 * e + HD],
                                              ps[:, bank, H:2 * H].rearrange("p (a e f) -> p a e f", a=8, e=2)[:, :, e, :],
                                              bkv_row[:, H:2 * H].rearrange("p (a e f) -> p a e f", a=8, e=2)[:, :, e, :],
                                              ALU.add)
                    ins.then_inc(drained[bank], 1)
                for n in range(NC * b, NC * b + NC + 1):
                    if n < NC * b + NC:
                        c, _, m = CHUNKS[n]
                        if n == 0:
                            dve.wait_ge(masks_made, 3)
                            dve.wait_ge(decays, 3)
                        wait_drained(dve, ("q1", b, m))
                        if n >= 2:
                            wait_filled(dve, ("oc", n - 2))
                        v.tensor_tensor(QDEC[:, n % 2, :], QT1[:, m, tok(TB * b + c)], QD[:, m, :], ALU.mult)\
                            .then_inc(qdec_done, 1)
                        for hf in range(2):
                            bank = wait_filled(dve, ("sc", n, hf))
                            v.tensor_tensor(PD[:, n % 2, 512 * hf:512 * hf + 512].rearrange("p (h i) -> p h i", h=4),
                                            ps[:, bank, :].rearrange("p (h i) -> p h i", h=4),
                                            DT[:, 8 * m + 4 * hf:8 * m + 4 * hf + 4, :], ALU.mult)\
                                .then_inc(drained[bank], 1)
                    if n > NC * b and CHUNKS[n - 1][0] < TB - 1:
                        c, _, m = CHUNKS[n - 1]
                        bank = wait_filled(dve, ("st", n - 1))
                        state = ST[:, 2 * b + m, :]
                        v.tensor_tensor(TMP[:, n % 2, :], ps[:, bank, 0:P],
                                        block_diag[:].rearrange("p j e -> p (j e)"), ALU.mult)\
                            .then_inc(drained[bank], 1)
                        wait_drained(dve, ("st", n - 1))
                        v.scalar_tensor_tensor(state, state, chunk_decay[:, m:m + 1], TMP[:, n % 2, :],
                                               ALU.mult, ALU.add).then_inc(state_done, 1)
                dve.wait_ge(bias_added, 3 + b)
                if b == 0:
                    take_moments(3, b, [("op", b, pr) for pr in range(2)], add=True)
                    scale_rows(3, b)
                else:
                    normalise_pairs(3, "op")

            route(1, 1)
            expert_tiles(1, NT1, I1, bufs1)

        @block.tensor
        def _(pe):
            t_ = nc.tensor

            def transposes(n, b):
                for kt in range(KT):
                    bank = wait_free(pe, ("xt", n, b, kt))
                    for t in range(TB):
                        if kt == 0:
                            pe.wait_ge(xn_done, T * n + TB * b + t + 1)
                        ins = t_.transpose(ps[:, bank, tok(t)], XN[:, TB * b + t, P * kt:P * kt + P], identity[:])
                    ins.then_inc(filled[bank], 1)

            def turn_pair(n, b, pr):
                bank = wait_free(pe, ("xp", n, b, pr))
                for e in range(2):
                    t = TB * b + 2 * pr + e
                    pe.wait_ge(xn_done, T * n + t + 1)
                    for kt in range(KT):
                        ins = t_.transpose(ps[:, bank, tok(2 * kt + e)], XN[:, t, P * kt:P * kt + P], identity[:])
                ins.then_inc(filled[bank], 1)

            def product(out, pairs, **kw):
                for n, (lhsT, rhs) in enumerate(pairs):
                    ins = t_.matmul(out, lhsT, rhs, start=n == 0, stop=n == len(pairs) - 1, **kw)
                return ins

            def w0(n, cols):
                w = part(W, 512 * n, KT, H)
                return [w[:, kt, cols] for kt in range(KT)]

            def project(i, kts=range(KT)):
                qk, b, m = proj_key(i)
                if kts[0] == 0:
                    pe.wait_ge(in_w[qk], 16)
                    wait_free(pe, ("qk", i))
                bank, _ = uses.at["qk", i]
                w = w0(qk, slice(P * m, P * m + P))
                for kt in kts:
                    ins = t_.matmul(ps[:, bank, :], w[kt], XT[:, kt, S * b:S * b + S], start=kt == 0, stop=kt == KT - 1)
                if kts[-1] == KT - 1:
                    ins.then_inc(filled[bank], 1)

            def token_products(key, b, pr, src, w, es=range(2)):
                if es[0] == 0:
                    wait_free(pe, key)
                bank, _ = uses.at[key]
                for e in es:
                    t = TB * b + 2 * pr + e
                    ins = product(ps[:, bank, H * e:H * e + H], [(src[:, kt, tok(t)], w[kt]) for kt in range(KT)])
                if es[-1] == 1:
                    ins.then_inc(filled[bank], 1)

            def keep_warm(key, n):
                bank = wait_free(pe, key)
                for i in range(n):
                    t_.matmul(ps[:, bank, 0:P], identity_bf[:], identity_bf[:], start=True, stop=True)

            pe.wait_ge(consts, 2)
            keep_warm(("xt", 0, 0, 0), WARM)
            transposes(0, 0)
            for kt in range(KT):
                wait_drained(pe, ("xt", 0, 0, kt))
            for i in range(4):
                project(i)
            transposes(0, 1)
            def project_v(b, pr, es=range(2)):
                if pr == 0 and es[0] == 0:
                    pe.wait_ge(in_w[2], 16)
                    for kt in range(KT):
                        wait_drained(pe, ("xt", 0, b, kt))
                token_products(("v", b, pr), b, pr, XT, w0(2, slice(0, H)), es)

            for pr in range(2):
                project_v(0, pr)

            def maxima(u, qt, heads):
                b, g = divmod(u, 4)
                for h in heads:
                    bank = wait_free(pe, ("mx", u, qt, h))
                    t_.matmul(ps[:, bank, :], QP[b][0:KR, 4 * g + h, tok(qt)], KP[b][0:KR, 4 * g + h, :],
                              start=True, stop=True).then_inc(filled[bank], 1)

            for q in range(NQ):
                w = quarter_of(q)
                if "max" in w:
                    u, qt = w["max"]
                    b, g = divmod(u, 4)
                    if qt == 0 and g % 2 == 0:
                        for i in (4 * b + g, 4 * b + g + 1):
                            pe.wait_ge(parts_moved[i], 96)
                    if "score" in w:
                        maxima(u, qt, (0,))
                    else:
                        for half in range(2):
                            maxima(u, qt, (2 * half, 2 * half + 1))
                            if "v" in w:
                                project_v(*w["v"], (half,))
                            elif "project" in w:
                                project(w["project"], (half,))
                            elif q == LAG - 1:
                                keep_warm(("s", 0, 0, 0), 14)
                if "score" in w:
                    u, kt = w["score"]
                    b, g = divmod(u, 4)
                    if u == 0 and kt == 0:
                        pe.wait_ge(consts, 7)
                    if kt == 0:
                        pe.wait_ge(negmax_loaded[u], 48)
                    for h in range(4):
                        if h and "max" in w:
                            maxima(*w["max"], (h,))
                        bank = wait_free(pe, ("s", u, kt, h))
                        t_.matmul(ps[:, bank, :], KP[b][0:KR + 3, 4 * g + h, tok(kt)], QP[b][0:KR + 3, 4 * g + h, :],
                                  start=True, stop=True).then_inc(filled[bank], 1)
                if "negmax" in w:
                    u = w["negmax"]
                    bank = wait_free(pe, ("nm", u))
                    pe.wait_ge(negmax_done, u + 1)
                    t_.transpose(ps[0:48, bank, 0:P // 2].bitcast(BF16), NM[:, u % 2, :], identity_bf[:])\
                        .then_inc(filled[bank], 1)
                if "pv" in w:
                    u, kt = w["pv"]
                    b, g = divmod(u, 4)
                    if kt == 0:
                        wait_free(pe, ("pv", u))
                        for pr in range(2):
                            wait_drained(pe, ("v", b, pr))
                    for h in (2, 3):
                        wait_drained(pe, ("s", u, kt, h))
                    for h in range(4):
                        col = (HD + 1) * (4 * g + h)
                        ins = t_.matmul(ps[32 * h:32 * h + 32, 6, :], VA[:, TB * b + kt, col:col + 32],
                                        PT[:, (16 * u + 4 * kt + h) % NPT, :], start=kt == 0, stop=kt == 3)
                    ins.then_inc(filled[6] if kt == 3 else pv_done, 1)
                if "norm" in w:
                    u = w["norm"]
                    bank = wait_free(pe, ("ct", u))
                    wait_drained(pe, ("pv", u))
                    for t in range(TB):
                        ins = t_.transpose(ps[:, bank, tok(t)], CT[:, u % 2, tok(t)], identity[:])
                    ins.then_inc(filled[bank], 1)
                if "ctxT" in w:
                    b = w["ctxT"]
                    wait_drained(pe, ("ct", 4 * b + 3))
                    for kt in range(KT):
                        bank = wait_free(pe, ("cx", b, kt))
                        for t in range(TB):
                            ins = t_.transpose(ps[:, bank, tok(t)], XN[:, TB * b + t, P * kt:P * kt + P], identity[:])
                        ins.then_inc(filled[bank], 1)
                    if b == 1:
                        transposes(1, 0)
                if "wo" in w:
                    b = w["wo"]
                    pe.wait_ge(in_w[3], 16)
                    for kt in range(KT):
                        wait_drained(pe, ("cx", b, kt))
                    for pr in range(2):
                        token_products(("o", b, pr), b, pr, XT, w0(3, slice(0, H)))

            def router(n, b, rw, nl):
                bank, _ = uses.at["r", n]
                if b == 0:
                    wait_free(pe, ("r", n))
                    for kt in range(KT):
                        wait_drained(pe, ("xt", 2 * n + 1, b, kt))
                for t in range(TB * b, TB * b + TB):
                    if b and t % 2 == 0:
                        wait_drained(pe, ("xp", 2 * n + 1, b, t % TB // 2))
                    ins = product(ps[:, bank, 16 * t:16 * t + nl],
                                  [(XT[:, kt, tok(t)], rw[:, kt, :]) for kt in range(KT)])
                if b == B - 1:
                    ins.then_inc(filled[bank], 1)

            def ranks(n):
                pe.wait_ge(counted, n + 1)
                bank = wait_free(pe, ("rank", n))
                chosen = chosen_of[n]
                out = ps[:, bank, 0:(T + 1) * E]
                t_.matmul(out, before_bf[:], chosen, start=True, stop=True)
                for t in range(T):
                    ins = t_.matmul(ps[:, bank, E * (t + 1):(T + 1) * E].rearrange("p (t e) -> p t e", e=E), ones_bf[:],
                                    chosen[:, t:t + 1, :].to_broadcast([P, T - t, E]),
                                    start=False, stop=True, skip_group_check=True)
                ins.then_inc(filled[bank], 1)

            def expert_tiles(n, nt, hw, bufs, ups, downs):
                rows, xst, hh, ht = bufs[0], bufs[1], bufs[3], bufs[4]
                expert = {}
                def turn_rows(i):
                    ring = (4, 8)[n]
                    if (n, i) != (1, 0):
                        pe.wait_ge(sorted_loaded[n][i % ring], 16 * (i // ring + 1))
                    bank = wait_free(pe, ("ex", n, i))
                    for kt in range(KT):
                        if (n, i) == (1, 0):
                            pe.wait_ge(first_found, 1)
                            ins = product(ps[:, bank, tok(kt)], [(XN[:, t, tok(kt)], first_of[:, t, :])
                                                                 for t in range(T)])
                        else:
                            ins = t_.transpose(ps[:, bank, tok(kt)], rows[:, i % ring, tok(kt)], identity[:])
                    ins.then_inc(filled[bank], 1)

                for i in range(nt + 3):
                    if n == 0 and i < nt:
                        turn_rows(i)
                    j = i - 1
                    if 0 <= j < nt:
                        if j == 0:
                            pe.wait_ge(owners_done, n + 1)
                        expert[j] = t_.value_load(owner[n][0:1, j:j + 1], min_val=0, max_val=E - 1)
                        wait_drained(pe, ("ex", n, j))
                        for key, w in ups:
                            bank = wait_free(pe, (key, n, j))
                            product(ps[:, bank, 0:w.shape[3]],
                                    [(xst[:, j % 2, tok(kt)], w[:, kt, bass.ds(expert[j], 1), :]) for kt in range(KT)])\
                                .then_inc(filled[bank], 1)
                    if n == 1 and i < nt:
                        turn_rows(i)
                    j = i - 2
                    if 0 <= j < nt:
                        wait_drained(pe, (ups[-1][0], n, j))
                        bank = wait_free(pe, ("eh", n, j))
                        if n == 0:
                            starts = (0, hw - P)
                        else:
                            starts = range(0, hw, P)
                        for k, c in enumerate(starts):
                            ins = t_.transpose(ps[:, bank, tok(k)], hh[:, j % 2, c:c + P], identity[:])
                        ins.then_inc(filled[bank], 1)
                    j = i - 3
                    if 0 <= j < nt:
                        wait_drained(pe, ("eh", n, j))
                        bank = wait_free(pe, ("ed", n, j))
                        product(ps[:, bank, 0:H], [(ht[:, j % 2, tok(k)], w[:, bass.ds(expert[j], 1), :])
                                                   for k, w in enumerate(downs)]).then_inc(filled[bank], 1)

            def shared_expert(c, ms=range(MS)):
                for m in ms:
                    for key, w in (("sg", sg0), ("su", su0)) if m < FULL else (("sg", st0),):
                        bank = wait_free(pe, (key, c, m))
                        cols = slice(P * m, P * m + P) if m < FULL else slice(0, P)
                        product(ps[:, bank, :], [(w[:, kt, cols], XT[:, kt, S * c:S * c + S]) for kt in range(KT)])\
                            .then_inc(filled[bank], 1)
                    if c == 0 and m == 2:
                        ranks(0)
                if ms[-1] < MS - 1:
                    return
                for m in range(MS):
                    wait_drained(pe, up_key(c, m))
                pe.wait_ge(hidden_zero, 1)
                for pr in range(2):
                    bank = wait_free(pe, ("sd", c, pr))
                    for e in range(2):
                        t = 2 * pr + e
                        ins = product(ps[:, bank, H * e:H * e + H],
                                      [(HS[:, m, tok(t)], sd0[:, m, :])
                                       for m in range(MS)])
                    ins.then_inc(filled[bank], 1)
            pe.wait_ge(in_small, 16 * 4)
            router(0, 0, r0w, E + 1)
            pe.wait_ge(in_ffn0, 16 * FFN0_PIECES)
            shared_expert(0, range(1))
            for pr in range(2):
                turn_pair(1, 1, pr)
            router(0, 1, r0w, E + 1)
            shared_expert(0, range(1, MS))
            expert_tiles(0, NT0, I0, bufs0, [("eg", gu0)], [da0, db0])
            shared_expert(1)

            wqkv = part(W, 0, KT, 3 * H)
            states = {}

            def chunk_out(n):
                c, b, m = CHUNKS[n]
                t = TB * b + c
                pe.wait_ge(qdec_done, n + 1)
                if c:
                    pe.wait_ge(state_done, states[c - 1, b, m])
                for hf in range(2):
                    wait_drained(pe, ("sc", n, hf))
                bank = wait_free(pe, ("oc", n))
                t_.matmul(ps[:, bank, 0:P], ST[:, 2 * b + m, :], QDEC[:, n % 2, :], start=True, stop=True)
                for k in range(HP):
                    pair, e = divmod(k, 2)
                    col = 48 * (4 * m + pair) + 16 * e
                    ins = t_.matmul(ps[32 * pair:32 * pair + 32, bank, 0:P], VP[:, t, col:col + 32],
                                    PD[:, n % 2, P * k:P * k + P], start=False, stop=True, skip_group_check=True)
                ins.then_inc(filled[bank], 1)
                if c < TB - 1:
                    bank = wait_free(pe, ("st", n))
                    states[c, b, m] = len(states) + 1
                    pe.wait_ge(kdec_done, t + 1)
                    vv = VP[:, t, 192 * m:192 * m + 192].rearrange("p (a s) -> p a s", a=4)
                    vv = vv[:, :, 0:48].rearrange("p a (e f) -> p a e f", e=3)[:, :, 0:3:2, :]
                    t_.matmul(ps[:, bank, 0:P], KD1[:, t, P * m:P * m + P], vv, start=True, stop=True)\
                        .then_inc(filled[bank], 1)

            transposes(2, 0)
            pe.wait_ge(in_w1, 32)
            for b in range(B):
                for kt in range(KT):
                    wait_drained(pe, ("xt", 2, b, kt))
                for m in range(KT):
                    for n, key in enumerate(("q1", "k1")):
                        bank = wait_free(pe, (key, b, m))
                        product(ps[:, bank, :], [(wqkv[:, kt, H * n + P * m:H * n + P * m + P], XT[:, kt, S * b:S * b + S])
                                                 for kt in range(KT)]).then_inc(filled[bank], 1)
                for t in range(TB * b, TB * b + TB):
                    bank = wait_free(pe, ("kv", t))
                    product(ps[:, bank, :], [(XT[:, kt, tok(t)], wqkv[:, kt, H:3 * H]) for kt in range(KT)])\
                        .then_inc(filled[bank], 1)
                if b == 0:
                    transposes(2, 1)
                else:
                    transposes(3, 0)
                    router(1, 0, r1w, E)
                pe.wait_ge(masks_made, 3)
                for m in range(KT):
                    wait_drained(pe, ("k1", b, m))
                for t in range(TB * b, TB * b + TB):
                    wait_drained(pe, ("kv", t))
                for n in range(NC * b, NC * b + NC + 1):
                    if n < NC * b + NC:
                        c, _, m = CHUNKS[n]
                        pe.wait_ge(spread, n + 1)
                        for hf in range(2):
                            bank = wait_free(pe, ("sc", n, hf))
                            t_.matmul(ps[:, bank, :], KT1[:, m, tok(TB * b + c)], QB[:, n % 2, 512 * hf:512 * hf + 512],
                                      start=True, stop=True).then_inc(filled[bank], 1)
                    if n > NC * b:
                        chunk_out(n - 1)
                for n in range(NC * b, NC * b + NC):
                    wait_drained(pe, ("oc", n))
                wout = part(W, 1536, KT, H)
                for pr in range(2):
                    bank = wait_free(pe, ("op", b, pr))
                    for e in range(2):
                        t = TB * b + 2 * pr + e
                        ins = product(ps[:, bank, H * e:H * e + H],
                                      [(XN[:, t, P * kt:P * kt + P], wout[:, kt, :]) for kt in range(KT)])
                    ins.then_inc(filled[bank], 1)

            for pr in range(2):
                turn_pair(3, 1, pr)
            router(1, 1, r1w, E)
            ranks(1)
            pe.wait_ge(in_ffn1, 16 * 16)
            pe.wait_ge(in_gate1, 16)
            expert_tiles(1, NT1, I1, bufs1, [("eg", gate1), ("eu", up1)],
                         [down1[:, k, :, :] for k in range(I1 // P)])


def kernel(**inputs):
    import numpy as np
    import concourse.bacc as bacc
    from concourse.bass_utils import run_bass_kernel_spmd as launch

    a = {k: np.asarray(v) for k, v in inputs.items()}

    def rows(w):
        return np.ascontiguousarray(w.reshape(w.shape[0] // 128, 128, -1).swapaxes(0, 1))

    def col(v):
        return v.reshape(2, 128).T

    def by_expert(w):
        return np.ascontiguousarray(w.reshape(w.shape[0], -1, 128, w.shape[2]).transpose(2, 1, 0, 3))

    by_dim = np.arange(256).reshape(2, 8, 16).transpose(0, 2, 1).reshape(256)
    wq, wk, wv, wo = (a["L0_attn_" + n].T for n in ("Wq", "Wk", "Wv", "Wo"))
    wd = a["L0_ffn_w_down"]
    tail = np.zeros((8, 128, 256), wd.dtype)
    tail[:, 80:] = wd[:, 128:]
    shared_down = np.zeros((768, 256), wd.dtype)
    shared_down[:640] = a["L0_ffn_sw_down"][:640]
    shared_down[704:] = a["L0_ffn_sw_down"][640:]
    sg, su = a["L0_ffn_sw_gate"], a["L0_ffn_sw_up"]
    arrays = {
        "x": a["L0_attn_x"],
        "w0": np.stack([rows(w).reshape(128, 512) for w in (wq[:, by_dim], wk[:, by_dim], wv, wo)]),
        "bias_col": np.stack([col(a["L0_attn_bq"][by_dim]), col(a["L0_attn_bk"][by_dim]), col(a["L1_attn_bqkv"][:256]),
                              col(a["L1_attn_bqkv"][256:512])], axis=1),
        "bv0": a["L0_attn_bv"],
        "bo0": a["L0_attn_bo"],
        "slopes": a["L1_attn_slopes"],
        "slopes_col": col(np.repeat(a["L1_attn_slopes"], 16)),
        "r0w": rows(np.concatenate([a["L0_ffn_gate_w"].T, a["L0_ffn_shared_gate_w"]], axis=1)),
        "r1w": rows(a["L1_ffn_router_w"]),
        "ffn0": np.concatenate([w.reshape(128, -1) for w in (
            by_expert(np.concatenate([a["L0_ffn_w_gate"], a["L0_ffn_w_up"]], axis=2)),
            wd[:, :128].swapaxes(0, 1), tail.swapaxes(0, 1), rows(sg[:, :640]), rows(su[:, :640]),
            rows(np.concatenate([sg[:, 640:], su[:, 640:]], axis=1)), rows(shared_down))], axis=1),
        "wqkv1": rows(a["L1_attn_Wqkv"]).reshape(128, 1536),
        "wout1": rows(a["L1_attn_Wout"]).reshape(128, 512),
        "bkv1": a["L1_attn_bqkv"][256:],
        "bout1": a["L1_attn_bout"],
        "gate1": by_expert(a["L1_ffn_gate_w"]),
        "ffn1": np.concatenate([by_expert(a["L1_ffn_up_w"]).reshape(128, -1),
                                by_expert(a["L1_ffn_down_w"]).reshape(128, -1)], axis=1),
    }
    arrays = {k: np.ascontiguousarray(v) for k, v in arrays.items()}
    nc = bacc.Bacc("TRN2", target_bir_lowering=False, num_devices=1)
    d = {k: nc.dram_tensor("in_" + k, v.shape, mybir.dt.from_np(v.dtype), kind="ExternalInput").ap()
         for k, v in arrays.items()}
    d["out"] = nc.dram_tensor("out", [2, 512, 256], mybir.dt.float32, kind="ExternalOutput").ap()
    two_layers(nc, d)
    r = launch(nc, [{"in_" + k: v for k, v in arrays.items()}], core_ids=[0])
    return r.results[0]["out"]
```
